# Optimizing a Trainium2 kernel written in Bass

```python
import numpy as np
import jax
import jax.numpy as jnp

def _softmax(x, axis=-1):
    return jax.nn.softmax(x, axis=axis)

def _gelu(x):
    return jax.nn.gelu(x, approximate=True)

def _silu(x):
    return jax.nn.silu(x)

def _sigmoid(x):
    return jax.nn.sigmoid(x)

def _layernorm(x, axis=-1, eps=1e-05):
    m = jnp.mean(x, axis=axis, keepdims=True)
    v = jnp.var(x, axis=axis, keepdims=True)
    return (x - m) / jnp.sqrt(v + eps)

def _scatter_add(tgt, idx, src, axis=0):
    return tgt.at[idx].add(src)

def _segment_sum(src, seg, n):
    return jax.ops.segment_sum(src, seg, n)
kernel_name = 'mk_adj_preln_d4_adj_r2_e66bac'

def setup_inputs(seed: int=0):
    np.random.seed(seed)
    _w = jnp.asarray

    def _rec_inputs():
        import jax
        import jax.numpy as jnp
        _gk = jax.random.key(seed)
        x = -0.0002928 + 1 * jax.random.normal(jax.random.fold_in(_gk, 1), (2048, 512), jnp.float32)
        _a = jax.random.bernoulli(jax.random.fold_in(_gk, 2), 0.00195312, (2048, 2048))
        _a = jnp.logical_or(_a, jnp.eye(2048, dtype=bool))
        _af = _a.astype(jnp.float32)
        _af = _af * jax.random.uniform(jax.random.fold_in(_gk, 3), (2048, 2048), jnp.float32, 0.05, 1)
        adj = _af
        return (x, adj)
    x, adj = _rec_inputs()

    def _L0_gnn_setup():
        import jax, jax.numpy as jnp
        import numpy as np
        D_IN, D_ATTN, STEPS = (512, 64, 2)
        P_TOP, TAU, LN_EPS = (0.9, 1.0, 1e-05)
        N = 2048

        def _xavier(key, shape):
            fan_in, fan_out = (shape[0], shape[1])
            lim = jnp.sqrt(6.0 / (fan_in + fan_out))
            return jax.random.uniform(key, shape, jnp.float32, -lim, lim)

        def _adj_from_feats(Xa, W1, W2, W3):
            Q = Xa @ W1
            K = Xa @ W3
            logits = Q @ W2 @ K.T / TAU
            n = logits.shape[1]
            order = jnp.argsort(-logits, axis=1)
            vals = jnp.take_along_axis(logits, order, axis=1)
            probs = jax.nn.softmax(vals, axis=1)
            csum = jnp.cumsum(probs, axis=1)
            k_i = jnp.sum(csum < P_TOP, axis=1) + 1
            keep = jnp.arange(n)[None, :] < k_i[:, None]
            masked_sorted = jnp.where(keep, vals, -jnp.inf)
            rows = jnp.arange(n)[:, None]
            masked = jnp.full_like(logits, -jnp.inf).at[rows, order].set(masked_sorted)
            return jax.nn.softmax(masked, axis=1)
        key = jax.random.key(seed)
        ks = jax.random.split(key, 12)
        X = jax.random.normal(ks[0], (N, D_IN), jnp.float32)
        S = jax.random.uniform(ks[1], (N, N), jnp.float32)
        W1 = _xavier(ks[2], (D_IN, D_ATTN))
        W3 = _xavier(ks[3], (D_IN, D_ATTN))
        W2 = _xavier(ks[4], (D_ATTN, D_ATTN))
        U1_0 = _xavier(ks[5], (D_IN, D_IN))
        U1_1 = _xavier(ks[6], (D_IN, D_IN))
        U2_0 = _xavier(ks[7], (D_IN, D_IN))
        U2_1 = _xavier(ks[8], (D_IN, D_IN))
        gamma = jnp.ones((D_IN,), jnp.float32)
        beta = jnp.zeros((D_IN,), jnp.float32)
        return {'X': X, 'S': S, 'W1': W1, 'W2': W2, 'W3': W3, 'U1_0': U1_0, 'U1_1': U1_1, 'U2_0': U2_0, 'U2_1': U2_1, 'gamma': gamma, 'beta': beta}
    _L0_gnn_all = _L0_gnn_setup()
    _L0_gnn_in = {k: v for k, v in _L0_gnn_all.items() if k in ('W1', 'W2', 'W3', 'U1_0', 'U1_1', 'U2_0', 'U2_1', 'gamma', 'beta')}
    del _L0_gnn_all

    def _L1_gnn_setup():
        import jax, jax.numpy as jnp
        import numpy as np
        import math
        SENT_DIM = 512
        N_SENT = 2048
        key = jax.random.key(seed)
        ks = jax.random.split(key, 8)
        D = SENT_DIM
        s = 1.0 / math.sqrt(D)
        return {'sent_embed': jax.random.normal(ks[0], (N_SENT, D), dtype=jnp.float32), 'adj_tensor': jax.random.randint(ks[1], (N_SENT, N_SENT), 0, 2).astype(jnp.float32), 'W_q': jax.random.uniform(ks[2], (D, D), jnp.float32, -s, s), 'b_q': jax.random.uniform(ks[3], (D,), jnp.float32, -s, s), 'W_k': jax.random.uniform(ks[4], (D, D), jnp.float32, -s, s), 'b_k': jax.random.uniform(ks[5], (D,), jnp.float32, -s, s), 'W_v': jax.random.uniform(ks[6], (D, D), jnp.float32, -s, s), 'b_v': jax.random.uniform(ks[7], (D,), jnp.float32, -s, s)}
    _L1_gnn_all = _L1_gnn_setup()
    _L1_gnn_in = {k: v for k, v in _L1_gnn_all.items() if k in ('W_q', 'b_q', 'W_k', 'b_k', 'W_v', 'b_v')}
    del _L1_gnn_all

    def _L2_gnn_setup():
        import jax, jax.numpy as jnp
        import numpy as np
        N, H, E, HEADS = (1500, 512, 10000, 8)
        DK = H // HEADS
        key = jax.random.key(seed)
        k1, k2, k3, k4 = jax.random.split(key, 4)
        inst_feature = jax.random.normal(k1, (N, H), dtype=jnp.float32)
        rel_pair_index = jax.random.randint(k2, (E, 2), 0, N, dtype=jnp.int64)
        agg = jnp.zeros((N, N), dtype=jnp.float32)
        agg = agg.at[rel_pair_index[:, 0], rel_pair_index[:, 1]].set(1.0)
        agg = agg.at[jnp.arange(N), jnp.arange(N)].set(1.0)
        std = float(np.sqrt(2.0 / (H + DK)))
        Wq = jax.random.normal(k3, (H, H), dtype=jnp.float32) * std
        Wk = jax.random.normal(k4, (H, H), dtype=jnp.float32) * std
        bq = jnp.zeros((H,), dtype=jnp.float32)
        bk = jnp.zeros((H,), dtype=jnp.float32)
        return {'inst_feature': inst_feature, 'aggregator_matrix': agg, 'rel_pair_index': rel_pair_index, 'Wq': Wq, 'bq': bq, 'Wk': Wk, 'bk': bk}
    _L2_gnn_all = _L2_gnn_setup()
    _L2_gnn_in = {k: v for k, v in _L2_gnn_all.items() if k in ('rel_pair_index', 'Wq', 'bq', 'Wk', 'bk')}
    del _L2_gnn_all

    def _L3_gnn_setup():
        import jax, jax.numpy as jnp
        import numpy as np
        ALPHA = 0.2
        NEG = -9000000000000000.0
        N, NFEAT, NHID, NHEADS = (2048, 512, 64, 8)
        EMB = NHID * NHEADS
        key = jax.random.key(seed)
        ks = jax.random.split(key, 16)
        x = jax.random.normal(ks[0], (N, NFEAT), dtype=jnp.float32)
        adj = (jax.random.uniform(ks[1], (N, N)) < 0.01).astype(jnp.float32)
        adj = jnp.maximum(adj, jnp.eye(N, dtype=jnp.float32))
        s = 0.05
        W = jax.random.normal(ks[2], (NHEADS, NFEAT, NHID), dtype=jnp.float32) * s
        a1 = jax.random.normal(ks[3], (NHEADS, NHID), dtype=jnp.float32) * s
        a2 = jax.random.normal(ks[4], (NHEADS, NHID), dtype=jnp.float32) * s
        W1 = jax.random.normal(ks[5], (EMB // 2, EMB), dtype=jnp.float32) * s
        b1 = jnp.zeros((EMB // 2,), dtype=jnp.float32)
        W2 = jax.random.normal(ks[6], (NFEAT // 4, EMB // 2), dtype=jnp.float32) * s
        b2 = jnp.zeros((NFEAT // 4,), dtype=jnp.float32)
        W3 = jax.random.normal(ks[7], (NFEAT // 2, NFEAT // 4), dtype=jnp.float32) * s
        b3 = jnp.zeros((NFEAT // 2,), dtype=jnp.float32)
        W4 = jax.random.normal(ks[8], (NFEAT, NFEAT // 2), dtype=jnp.float32) * s
        b4 = jnp.zeros((NFEAT,), dtype=jnp.float32)
        return {'x': x, 'adj': adj, 'W': W, 'a1': a1, 'a2': a2, 'W1': W1, 'b1': b1, 'W2': W2, 'b2': b2, 'W3': W3, 'b3': b3, 'W4': W4, 'b4': b4}
    _L3_gnn_all = _L3_gnn_setup()
    _L3_gnn_in = {k: v for k, v in _L3_gnn_all.items() if k in ('W', 'a1', 'a2', 'W1', 'b1', 'W2', 'b2', 'W3', 'b3', 'W4', 'b4')}
    del _L3_gnn_all
    return {'x': x, 'adj': adj, 'L0_gnn_W1': _L0_gnn_in['W1'], 'L0_gnn_W2': _L0_gnn_in['W2'], 'L0_gnn_W3': _L0_gnn_in['W3'], 'L0_gnn_U1_0': _L0_gnn_in['U1_0'], 'L0_gnn_U1_1': _L0_gnn_in['U1_1'], 'L0_gnn_U2_0': _L0_gnn_in['U2_0'], 'L0_gnn_U2_1': _L0_gnn_in['U2_1'], 'L0_gnn_gamma': _L0_gnn_in['gamma'], 'L0_gnn_beta': _L0_gnn_in['beta'], 'L1_gnn_W_q': _L1_gnn_in['W_q'], 'L1_gnn_b_q': _L1_gnn_in['b_q'], 'L1_gnn_W_k': _L1_gnn_in['W_k'], 'L1_gnn_b_k': _L1_gnn_in['b_k'], 'L1_gnn_W_v': _L1_gnn_in['W_v'], 'L1_gnn_b_v': _L1_gnn_in['b_v'], 'L2_gnn_rel_pair_index': _L2_gnn_in['rel_pair_index'], 'L2_gnn_Wq': _L2_gnn_in['Wq'], 'L2_gnn_bq': _L2_gnn_in['bq'], 'L2_gnn_Wk': _L2_gnn_in['Wk'], 'L2_gnn_bk': _L2_gnn_in['bk'], 'L3_gnn_W': _L3_gnn_in['W'], 'L3_gnn_a1': _L3_gnn_in['a1'], 'L3_gnn_a2': _L3_gnn_in['a2'], 'L3_gnn_W1': _L3_gnn_in['W1'], 'L3_gnn_b1': _L3_gnn_in['b1'], 'L3_gnn_W2': _L3_gnn_in['W2'], 'L3_gnn_b2': _L3_gnn_in['b2'], 'L3_gnn_W3': _L3_gnn_in['W3'], 'L3_gnn_b3': _L3_gnn_in['b3'], 'L3_gnn_W4': _L3_gnn_in['W4'], 'L3_gnn_b4': _L3_gnn_in['b4']}

def reference(x, adj, L0_gnn_W1, L0_gnn_W2, L0_gnn_W3, L0_gnn_U1_0, L0_gnn_U1_1, L0_gnn_U2_0, L0_gnn_U2_1, L0_gnn_gamma, L0_gnn_beta, L1_gnn_W_q, L1_gnn_b_q, L1_gnn_W_k, L1_gnn_b_k, L1_gnn_W_v, L1_gnn_b_v, L2_gnn_rel_pair_index, L2_gnn_Wq, L2_gnn_bq, L2_gnn_Wk, L2_gnn_bk, L3_gnn_W, L3_gnn_a1, L3_gnn_a2, L3_gnn_W1, L3_gnn_b1, L3_gnn_W2, L3_gnn_b2, L3_gnn_W3, L3_gnn_b3, L3_gnn_W4, L3_gnn_b4):
    import jax
    import jax.numpy as jnp

    def _L0_gnn_ref(X, S, W1, W2, W3, U1_0, U1_1, U2_0, U2_1, gamma, beta):
        import jax, jax.numpy as jnp
        import numpy as np
        D_IN, D_ATTN, STEPS = (512, 64, 2)
        P_TOP, TAU, LN_EPS = (0.9, 1.0, 1e-05)
        N = 2048

        def _xavier(key, shape):
            fan_in, fan_out = (shape[0], shape[1])
            lim = jnp.sqrt(6.0 / (fan_in + fan_out))
            return jax.random.uniform(key, shape, jnp.float32, -lim, lim)

        def _adj_from_feats(Xa, W1, W2, W3):
            Q = Xa @ W1
            K = Xa @ W3
            logits = Q @ W2 @ K.T / TAU
            n = logits.shape[1]
            order = jnp.argsort(-logits, axis=1)
            vals = jnp.take_along_axis(logits, order, axis=1)
            probs = jax.nn.softmax(vals, axis=1)
            csum = jnp.cumsum(probs, axis=1)
            k_i = jnp.sum(csum < P_TOP, axis=1) + 1
            keep = jnp.arange(n)[None, :] < k_i[:, None]
            masked_sorted = jnp.where(keep, vals, -jnp.inf)
            rows = jnp.arange(n)[:, None]
            masked = jnp.full_like(logits, -jnp.inf).at[rows, order].set(masked_sorted)
            return jax.nn.softmax(masked, axis=1)
        n = X.shape[0]
        S = S + jnp.eye(n, dtype=X.dtype)
        R = S / jnp.clip(S.sum(axis=1, keepdims=True), 1e-12)
        Z = jnp.zeros_like(X)
        Xf, Xa = (X, X)
        U1s, U2s = ((U1_0, U1_1), (U2_0, U2_1))
        for s in range(STEPS):
            A = _adj_from_feats(Xa, W1, W2, W3)
            Xf = R @ Xf
            Xa = A @ Xa
            Z = Z + (Xf @ U1s[s] + Xa @ U2s[s])
        Y = X + Z
        mu = Y.mean(axis=-1, keepdims=True)
        var = Y.var(axis=-1, keepdims=True)
        return (Y - mu) * jax.lax.rsqrt(var + LN_EPS) * gamma + beta

    def _L1_gnn_ref(sent_embed, adj_tensor, W_q, b_q, W_k, b_k, W_v, b_v):
        import jax, jax.numpy as jnp
        import numpy as np
        import math
        SENT_DIM = 512
        N_SENT = 2048
        q = sent_embed @ W_q.T + b_q
        k = sent_embed @ W_k.T + b_k
        v = sent_embed @ W_v.T + b_v
        scale = 1.0 / math.sqrt(sent_embed.shape[-1])
        z = scale * (q @ k.T)
        spare_z = z * adj_tensor
        spare_z = jnp.where(spare_z == 0.0, jnp.asarray(-10000.0, spare_z.dtype), spare_z)
        attn = jax.nn.softmax(spare_z, axis=1)
        out = attn @ v
        return jax.nn.relu(out)

    def _L2_gnn_ref(inst_feature, aggregator_matrix, rel_pair_index, Wq, bq, Wk, bk):
        import jax, jax.numpy as jnp
        import numpy as np
        N, H, E, HEADS = (1500, 512, 10000, 8)
        DK = H // HEADS
        n = inst_feature.shape[0]
        sub = rel_pair_index[:, 0]
        obj = rel_pair_index[:, 1]
        q = (inst_feature[sub] @ Wq.T + bq).reshape(-1, HEADS, DK)
        k = (inst_feature[obj] @ Wk.T + bk).reshape(-1, HEADS, DK)
        att = ((q * k).sum(-1) / np.sqrt(DK)).T.astype(inst_feature.dtype)
        scores = jnp.zeros((HEADS, n, n), dtype=inst_feature.dtype)
        scores = scores.at[:, sub, obj].set(att)
        mask = (1.0 - aggregator_matrix).astype(bool)
        scores = jnp.where(mask[None], -jnp.inf, scores)
        di = jnp.arange(n)
        scores = scores.at[:, di, di].set(1e-07)
        attn = jax.nn.softmax(scores, axis=2)
        aggregator_factor = attn.sum(axis=0) / HEADS
        return aggregator_factor @ inst_feature

    def _L3_gnn_ref(x, adj, W, a1, a2, W1, b1, W2, b2, W3, b3, W4, b4):
        import jax, jax.numpy as jnp
        import numpy as np
        ALPHA = 0.2
        NEG = -9000000000000000.0
        N, NFEAT, NHID, NHEADS = (2048, 512, 64, 8)
        EMB = NHID * NHEADS
        Wh = jnp.einsum('nf,hfd->hnd', x, W)
        e_src = jnp.einsum('hnd,hd->hn', Wh, a1)
        e_dst = jnp.einsum('hnd,hd->hn', Wh, a2)
        e = jax.nn.leaky_relu(e_src[:, :, None] + e_dst[:, None, :], ALPHA)
        e = jnp.where(adj[None] > 0, e, NEG)
        att = jax.nn.softmax(e, axis=-1)
        h = jnp.einsum('hnm,hmd->hnd', att, Wh)
        h = jax.nn.elu(h)
        enc = jnp.transpose(h, (1, 0, 2)).reshape(x.shape[0], -1)
        out = jax.nn.relu(enc @ W1.T + b1)
        out = jax.nn.relu(out @ W2.T + b2)
        out = jax.nn.relu(out @ W3.T + b3)
        out = out @ W4.T + b4
        return out
    h = jnp.maximum(_layernorm(x, axis=-1), 0.0)
    x = x + _L0_gnn_ref(h, adj, L0_gnn_W1, L0_gnn_W2, L0_gnn_W3, L0_gnn_U1_0, L0_gnn_U1_1, L0_gnn_U2_0, L0_gnn_U2_1, L0_gnn_gamma, L0_gnn_beta)
    h = jnp.maximum(_layernorm(x, axis=-1), 0.0)
    x = x + _L1_gnn_ref(h, adj, L1_gnn_W_q, L1_gnn_b_q, L1_gnn_W_k, L1_gnn_b_k, L1_gnn_W_v, L1_gnn_b_v)
    h = jnp.maximum(_layernorm(x, axis=-1), 0.0)
    x = x + _L2_gnn_ref(h, adj, L2_gnn_rel_pair_index, L2_gnn_Wq, L2_gnn_bq, L2_gnn_Wk, L2_gnn_bk)
    h = jnp.maximum(_layernorm(x, axis=-1), 0.0)
    x = x + _L3_gnn_ref(h, adj, L3_gnn_W, L3_gnn_a1, L3_gnn_a2, L3_gnn_W1, L3_gnn_b1, L3_gnn_W2, L3_gnn_b2, L3_gnn_W3, L3_gnn_b3, L3_gnn_W4, L3_gnn_b4)
    return x

_drawn_inputs = setup_inputs


def setup_inputs(seed=0):
    import zlib

    import numpy as np

    out = dict(_drawn_inputs(seed))
    spreads = {'L0_gnn_gamma': (1.0, 0.2),
     'L0_gnn_beta': (0.0, 0.1),
     'L2_gnn_bq': (0.0, 0.1),
     'L2_gnn_bk': (0.0, 0.1),
     'L3_gnn_b1': (0.0, 0.8),
     'L3_gnn_b2': (0.0, 0.8),
     'L3_gnn_b3': (0.0, 0.357),
     'L3_gnn_b4': (0.0, 0.1)}
    factors = {'L1_gnn_W_q': 8.0,
     'L1_gnn_b_q': 44.165,
     'L1_gnn_W_k': 8.0,
     'L1_gnn_b_k': 64.0,
     'L1_gnn_b_v': 5.359,
     'L3_gnn_W': 2.769,
     'L3_gnn_a1': 8.0,
     'L3_gnn_a2': 8.0,
     'L3_gnn_W1': 2.687}
    for name, (base, spread) in spreads.items():
        noise = np.random.default_rng([zlib.crc32(name.encode()), seed]).standard_normal(out[name].shape)
        drawn = base * np.exp(spread * noise) if base else spread * noise
        out[name] = jnp.asarray(drawn.astype(out[name].dtype))
    for name, factor in factors.items():
        out[name] = (out[name] * factor).astype(out[name].dtype)
    return out
```

```python
from contextlib import ExitStack
import math

import concourse.bass as bass
from concourse import mybir

F32 = mybir.dt.float32
BF16 = mybir.dt.bfloat16
I32 = mybir.dt.int32
ALU = mybir.AluOpType
ACT = mybir.ActivationFunctionType
AX = mybir.AxisListType

P = 128
EPS = 1e-5
TOP_P = 0.9
BISECT_STEPS = 22


class Chain:

    def __init__(self, eng, sem):
        self.eng, self.sem, self.n = eng, sem, 0

    def __call__(self, ins):
        self.n += 1
        ins.then_inc(self.sem, 1)
        self.eng.wait_ge(self.sem, self.n)

    def last_of(self, group):
        for ins in group:
            self.n += 1
            ins.then_inc(self.sem, 1)
        self.eng.wait_ge(self.sem, self.n)


def make_identity(nc, pool, ident, made):
    nc.gpsimd.memset(ident[:], 0.0).then_inc(made, 1)
    pool.wait_ge(made, 1)
    nc.gpsimd.affine_select(out=ident[:], in_=ident[:], compare_op=ALU.not_equal, fill=1.0, base=0,
                            pattern=[[-1, P]], channel_multiplier=1).then_inc(made, 1)


def layer_norm_batch(nc, chain, src, dst, stats, mv, rstd, sqrt_asked, sqrt_done, turn, relu, act_turn=None):
    T = src.shape[1]
    chain.last_of([nc.vector.bn_stats(stats[:, t, :], src[:, t, :]) for t in range(T)])
    chain.last_of([nc.vector.bn_aggr(mv[:, t, :], stats[:, t, :]) for t in range(T)])
    nc.vector.tensor_scalar(rstd[:, 0, :], mv[:, :, 1], EPS, None, ALU.add).then_inc(sqrt_asked, 1)
    chain.eng.wait_ge(sqrt_done, turn + 1)
    chain(nc.vector.reciprocal(rstd[:, 2, :], rstd[:, 1, :]))
    chain.last_of([nc.vector.tensor_scalar(dst[:, t, :], src[:, t, :], mv[:, t, 0:1], rstd[:, 2, t:t + 1],
                                           ALU.subtract, ALU.mult) for t in range(T)])
    if relu:
        chain(nc.vector.tensor_scalar(dst[:, :, :], dst[:, :, :], 0.0, None, ALU.max))


def layer_norm_sqrt(nc, act, rstd, sqrt_asked, sqrt_done, turn):
    act.wait_ge(sqrt_asked, turn + 1)
    nc.scalar.activation(rstd[:, 1, :], rstd[:, 0, :], ACT.Sqrt).then_inc(sqrt_done, 1)


def build(nc, io, out):
    N, D = io["x"].shape
    A = io["l0_w1"].shape[1]
    NT, KT = N // P, D // P
    HEADS, HID = io["l3_a1"].shape

    scratch = lambda name, shape=(N, D): nc.dram_tensor(name, list(shape), F32).ap()
    y_dram = [scratch(f"y{s}_scratch") for s in range(2)]
    xf_dram, x1_dram, x2_dram, l2_dram, x3_dram = (scratch(n) for n in ("xf", "x1", "x2", "l2", "x3"))
    src_dram = scratch("src", (HEADS, N))
    tiled = lambda ap: ap.rearrange("(n p) d -> p n d", p=P)

    with ExitStack() as whole:
        hold = lambda n, s, d=F32: whole.enter_context(nc.sbuf_tensor(n, s, d))
        ident, ones_row = hold("ident", [P, P]), hold("ones_row", [1, P])
        inv_degree, ones_seen = hold("inv_degree", [P, NT]), hold("ones_seen", [P, NT + 1])
        has_ones = hold("has_ones", [P, 1], I32)
        with ExitStack() as scope:
            sb = lambda n, s, d=F32: scope.enter_context(nc.sbuf_tensor(n, s, d))
            XA = [sb("feat0", [P, NT, D]), sb("feat1", [P, NT, D])]
            QK = [sb("qk0", [P, N]), sb("qk1", [P, N])]
            w1, w3 = sb("w1", [P, KT, A]), sb("w3", [P, KT, A])
            w2 = sb("w2", [A, A])
            used_sems = norm_phase(nc, io, XA[0], QK[0], (w1, w2, w3), ident, ones_row, inv_degree, ones_seen, has_ones, tiled)
            for s in range(2):
                graph_step(nc, io, s, XA, QK, (w1, w2, w3), ident, inv_degree, y_dram, xf_dram, tiled)
        with ExitStack() as scope:
            sb = lambda n, s, d=F32: scope.enter_context(nc.sbuf_tensor(n, s, d))
            qT, kT, V = sb("qT", [P, KT, N]), sb("kT", [P, KT, N]), sb("V", [P, NT, D])
            project_phase(nc, io, used_sems, qT, kT, V, ident, ones_row, y_dram[1], x1_dram, tiled)
            attention_phase(nc, io, qT, kT, V, ident, x1_dram, x2_dram, l2_dram, tiled)
        joined = nc.values_load(has_ones[0:1, 0:1], min_val=0, max_val=N * N,
                                skip_runtime_bounds_check_because="a count of the entries of adj")
        with nc.If(joined != 0):
            relation_phase(nc, io, ident, l2_dram, tiled)
        with ExitStack() as scope:
            sb = lambda n, s, d=F32: scope.enter_context(nc.sbuf_tensor(n, s, d))
            enc = sb("enc", [P, NT, D])
            with ExitStack() as inner:
                sb = lambda n, s, d=F32: inner.enter_context(nc.sbuf_tensor(n, s, d))
                Wh = sb("Wh", [P, NT, HEADS, HID + 1])
                edge = sb("edge", [P, NT, N], BF16)
                dst, dst_low, dst_neg = (sb(n, [P, NT, HEADS]) for n in ("dst", "dst_low", "dst_neg"))
                src_bias = sb("src_bias", [P, HEADS])
                heads_phase(nc, io, Wh, edge, dst, dst_low, dst_neg, src_bias, ident, x2_dram, l2_dram, x3_dram, src_dram, tiled)
                gat_phase(nc, Wh, edge, dst, dst_low, dst_neg, src_bias, enc, src_dram)
            mlp_phase(nc, io, enc, ident, ones_row, x3_dram, out, tiled)


def project_qk_pe(nc, pe, XT, w, ps, q_row, filled, emptied, n, q_copied):
    w1, w2, w3 = w
    KT = w1.shape[1]
    for which in (w3, w1):
        if n:
            pe.wait_ge(emptied, n)
        for k in range(KT):
            mm = nc.tensor.matmul(ps[0:64, :], which[:, k, :], XT[:, k, :], start=(k == 0), stop=(k == KT - 1))
        mm.then_inc(filled, 1)
        n += 1
    pe.wait_ge(emptied, n)
    nc.tensor.matmul(ps[0:64, :], w2[:, :], q_row[:, :], start=True, stop=True).then_inc(filled, 1)
    return n + 1


def project_qk_act(nc, act, ps, q_row, QK, g, filled, emptied, n):
    for dst in (QK[0:64, g * 512:(g + 1) * 512], q_row[:, :], QK[64:128, g * 512:(g + 1) * 512]):
        act.wait_ge(filled, n + 1)
        nc.scalar.copy(dst, ps[0:64, :]).then_inc(emptied, 1)
        n += 1
    return n


def norm_phase(nc, io, H, QK, w, ident, ones_row, inv_degree, ones_seen, has_ones, tiled):
    N, D = io["x"].shape
    NT, KT, T = N // P, D // P, 4
    G = NT // T
    with ExitStack() as scope:
        sb = lambda n, s, d=F32: scope.enter_context(nc.sbuf_tensor("a_" + n, s, d))
        sems = []

        def sem(n):
            sems.append(scope.enter_context(nc.semaphore("a_" + n)))
            return sems[-1]

        xin = sb("xin", [P, NT, D])
        adj_rows = sb("adj_rows", [P, 2, N])
        XT = sb("XT", [P, KT, 512])
        q_row = sb("q_row", [64, 512])
        stats, mv, rstd = sb("stats", [P, T, 6]), sb("mv", [P, T, 2]), sb("rstd", [P, 3, T])
        junk, junk2 = sb("junk", [P, N], BF16), sb("junk2", [P, N], BF16)
        degree, ones_all = sb("degree", [P, NT]), sb("ones_all", [P, 1])
        psT = [scope.enter_context(nc.psum_tensor(f"a_psT{b}", [P, 512], F32)) for b in range(2)]
        psQ = scope.enter_context(nc.psum_tensor("a_psQ", [P, 512], F32))

        x_in = [sem(f"x_in{g}") for g in range(G)]
        w_in = sem("w_in")
        adj_in = [sem(f"adj_in{b}") for b in range(2)]
        adj_summed, adj_counted = sem("adj_summed"), sem("adj_counted")
        ones_added, ones_spread = sem("ones_added"), sem("ones_spread")
        id_made, chain_s = sem("id_made"), sem("chain")
        sqrt_asked, sqrt_done, h_ready = sem("sqrt_asked"), sem("sqrt_done"), sem("h_ready")
        t_filled, t_emptied, q_filled, q_emptied = sem("t_filled"), sem("t_emptied"), sem("q_filled"), sem("q_emptied")
        block = scope.enter_context(nc.Block())

        @block.sync
        def _(sp):
            for g in range(G):
                sp.dma_start(xin[:, g * T:(g + 1) * T, :], tiled(io["x"])[:, g * T:(g + 1) * T, :]).then_inc(x_in[g], 16)
            for t, name in zip(w, ("l0_w1", "l0_w2", "l0_w3")):
                src = io[name] if name == "l0_w2" else io[name].rearrange("(k p) a -> p k a", p=P)
                sp.dma_start(t[:], src).then_inc(w_in, 16)
            for i in range(NT):
                if i >= 2:
                    sp.wait_ge(adj_summed, i - 1)
                    sp.wait_ge(adj_counted, i - 1)
                sp.dma_start(adj_rows[:, i % 2, :], io["adj"][i * P:(i + 1) * P, :]).then_inc(adj_in[i % 2], 16)

        @block.gpsimd
        def _(pool):
            make_identity(nc, pool, ident, id_made)
            nc.gpsimd.memset(ones_row[:], 1.0).then_inc(id_made, 1)
            pool.wait_ge(ones_added, 1)
            nc.gpsimd.partition_all_reduce(ones_all[:], ones_seen[:, NT:NT + 1], P,
                                           bass.bass_isa.ReduceOp.add).then_inc(ones_spread, 1)

        @block.vector
        def _(dve):
            chain = Chain(dve, chain_s)
            for g in range(G):
                dve.wait_ge(x_in[g], 16)
                layer_norm_batch(nc, chain, xin[:, g * T:(g + 1) * T, :], H[:, g * T:(g + 1) * T, :], stats, mv, rstd,
                                 sqrt_asked, sqrt_done, g, relu=True)
                dve.sem_inc(h_ready, 1)
            for i in range(NT):
                dve.wait_ge(adj_in[i % 2], 16 * (i // 2 + 1))
                if i:
                    dve.wait_ge(adj_counted, i)
                ins = nc.vector.tensor_scalar(junk2[:, :], adj_rows[:, i % 2, :], 1.0, 0.0, ALU.is_equal, ALU.add,
                                              accum_out=ones_seen[:, i:i + 1])
                ins.then_inc(adj_counted, 1)
            dve.wait_ge(adj_counted, NT)
            nc.vector.tensor_reduce(ones_seen[:, NT:NT + 1], ones_seen[:, 0:NT], AX.X, ALU.add).then_inc(ones_added, 1)
            dve.wait_ge(ones_spread, 1)
            chain(nc.vector.tensor_copy(has_ones[:], ones_all[:]))
            dve.wait_ge(adj_summed, NT)
            chain(nc.vector.tensor_scalar(degree[:, :], degree[:, :], 1.0, 1e-12, ALU.add, ALU.max))
            chain(nc.vector.reciprocal(inv_degree[:, :], degree[:, :]))

        @block.scalar
        def _(act):
            for g in range(G):
                layer_norm_sqrt(nc, act, rstd, sqrt_asked, sqrt_done, g)
            nT = nQ = 0
            for g in range(G):
                for k in range(KT):
                    act.wait_ge(t_filled, nT + 1)
                    if k == 0 and g:
                        act.wait_ge(q_filled, nQ)
                    nc.scalar.copy(XT[:, k, :], psT[nT % 2][:, :]).then_inc(t_emptied, 1)
                    nT += 1
                nQ = project_qk_act(nc, act, psQ, q_row, QK, g, q_filled, q_emptied, nQ)
            for i in range(NT):
                act.wait_ge(adj_in[i % 2], 16 * (i // 2 + 1))
                if i:
                    act.wait_ge(adj_summed, i)
                nc.scalar.activation(junk[:, :], adj_rows[:, i % 2, :], ACT.Copy,
                                     accum_out=degree[:, i:i + 1]).then_inc(adj_summed, 1)

        @block.tensor
        def _(pe):
            pe.wait_ge(id_made, 3)
            pe.wait_ge(w_in, 48)
            nT = nQ = 0
            for g in range(G):
                pe.wait_ge(h_ready, g + 1)
                for k in range(KT):
                    if nT >= 2:
                        pe.wait_ge(t_emptied, nT - 1)
                    for t in range(T):
                        tr = nc.tensor.transpose(psT[nT % 2][:, t * P:(t + 1) * P], H[:, g * T + t, k * P:(k + 1) * P], ident[:, :])
                    tr.then_inc(t_filled, 1)
                    nT += 1
                pe.wait_ge(t_emptied, nT)
                nQ = project_qk_pe(nc, pe, XT, w, psQ, q_row, q_filled, q_emptied, nQ, None)
    return range(min(x.num for x in sems), max(x.num for x in sems) + 1)


def graph_step(nc, io, s, XA, QK, w, ident, inv_degree, y_dram, xf_dram, tiled):
    N, D = io["x"].shape
    NT, KT, T = N // P, D // P, 4
    G, CH = NT // T, N // 512
    last_step = s == 1
    Xa, Xn = XA[s], XA[1 - s]
    Xf = XA[0]
    own = QK[s]
    with ExitStack() as scope:
        sb = lambda n, sh, d=F32: scope.enter_context(nc.sbuf_tensor(f"g{s}_{n}", sh, d))
        sem = lambda n: scope.enter_context(nc.semaphore(f"g{s}_{n}"))
        if last_step:
            Xn = None
            xa_row = QK[0][:, 0:2 * D].rearrange("p (b d) -> p b d", b=2)
            y_before = QK[0][:, 2 * D:4 * D].rearrange("p (b d) -> p b d", b=2)
        prob = sb("prob", [P, 2 * T, N])
        PT = sb("PT", [P, 2, 512])
        adj_T = sb("adj_T", [P, 3, NT // 2, P])
        u1, u2 = sb("u1", [P, KT, D]), sb("u2", [P, KT, D])
        XfT, XaT = sb("XfT", [P, T, KT, P]), sb("XaT", [P, KT, T * P])
        q_tile = sb("q_tile", [64, 2, P])
        y_row = sb("y_row", [P, D])
        xf_row = sb("xf_row", [P, 2, D])
        q_row = None if last_step else sb("q_row", [64, 512])
        junk = sb("junk", [P, N], mybir.dt.uint8)
        neg_max, total, kept, inv_kept = (sb(n, [P, NT]) for n in ("neg_max", "total", "kept", "inv_kept"))
        factors = sb("factors", [P, BISECT_STEPS])
        floor, trial, mass, goal, step_up = (sb(n, [P, T]) for n in ("floor", "trial", "mass", "goal", "step_up"))
        psL = scope.enter_context(nc.psum_tensor(f"g{s}_psL", [P, N], F32))
        psT = [scope.enter_context(nc.psum_tensor(f"g{s}_psT{b}", [P, 512], F32)) for b in range(2)]
        psO = scope.enter_context(nc.psum_tensor(f"g{s}_psO", [P, 512], F32))
        psY = scope.enter_context(nc.psum_tensor(f"g{s}_psY", [P, 512], F32))

        adj_in, adj_used = [sem(f"adj_in{b}") for b in range(3)], sem("adj_used")
        u_in, xf_in = sem("u_in"), sem("xf_in")
        yin = [sem(f"y_in{b}") for b in range(2)]
        q_staged = sem("q_staged")
        scores_done, max_done, exp_done, mask_done, inv_done = (sem(n) for n in ("scores_done", "max_done", "exp_done", "mask_done", "inv_done"))
        t_filled, t_emptied, pt_used = sem("t_filled"), sem("t_emptied"), sem("pt_used")
        o_emptied, y_filled, y_emptied = sem("o_emptied"), sem("y_filled"), sem("y_emptied")
        y_out, xf_out = sem("y_out"), [sem(f"xf_out{b}") for b in range(2)]
        chain_s = sem("chain")
        block = scope.enter_context(nc.Block())

        def order():
            for t in range(T):
                yield "scores", t
            for g in range(G + 1):
                for t in range(T):
                    if g:
                        yield "attend", (g - 1) * T + t
                    if g < G:
                        yield "relate", g * T + t
                    if g + 1 < G:
                        yield "scores", (g + 1) * T + t
                if g and not last_step:
                    yield "project", g - 1

        O_turn, Y_turn = {}, {}
        uses = 0
        for what, i in order():
            if what in ("attend", "relate"):
                O_turn[what, i] = len(O_turn)
            if what in ("attend", "project"):
                Y_turn[what, i] = uses
                uses += 1 if what == "attend" else 3

        def store_y(sp, i):
            sp.wait_ge(y_emptied, Y_turn["attend", i] + 1)
            sp.dma_start(tiled(y_dram[s])[:, i, :], y_row[:, :]).then_inc(y_out, 16)

        def store_xf(sp, i):
            sp.wait_ge(o_emptied, O_turn["relate", i] + 1)
            sp.dma_start(tiled(xf_dram)[:, i, :], xf_row[:, i % 2, :]).then_inc(xf_out[i % 2], 16)

        @block.sync
        def _(sp):
            if last_step:
                sp.dma_start(Xf[:, :, :], tiled(xf_dram)).then_inc(xf_in, 16)
            for t, name in ((u1, f"l0_u1_{s}"), (u2, f"l0_u2_{s}")):
                sp.dma_start(t[:], io[name].rearrange("(k p) a -> p k a", p=P)).then_inc(u_in, 16)
            for what, i in order():
                if what == "relate":
                    for half in range(2):
                        n = 2 * i + half
                        if n >= 3:
                            sp.wait_ge(adj_used, n - 2)
                        sp.dma_start(adj_T[:, n % 3, :, :], io["adj_t"][i, :, half * NT // 2:(half + 1) * NT // 2, :])\
                            .then_inc(adj_in[n % 3], 16)
                    if not last_step and i >= 1:
                        store_xf(sp, i - 1)
                if what == "attend":
                    if last_step:
                        if i >= 2:
                            sp.wait_ge(y_filled, Y_turn["attend", i - 2] + 1)
                        sp.dma_start(y_before[:, i % 2, :], tiled(y_dram[0])[:, i, :]).then_inc(yin[i % 2], 16)
                    if i >= 1:
                        store_y(sp, i - 1)
            if not last_step:
                store_xf(sp, NT - 1)
            store_y(sp, NT - 1)
            sp.wait_ge(y_out, 16 * NT)
            if not last_step:
                for b in range(2):
                    sp.wait_ge(xf_out[b], 16 * NT // 2)


        @block.gpsimd
        def _(pool):
            for i in range(NT):
                if i >= 2:
                    pool.wait_ge(scores_done, i - 1)
                nc.gpsimd.tensor_copy(q_tile[:, i % 2, :], own[64:128, i * P:(i + 1) * P]).then_inc(q_staged, 1)

        @block.vector
        def _(dve):
            chain = Chain(dve, chain_s)
            width = -math.log((1 - TOP_P) / N * 0.99) + 1e-3
            chain.last_of([nc.vector.memset(factors[:, k:k + 1], math.exp(width / 2 ** (k + 1)))
                           for k in range(BISECT_STEPS)])

            def row_max(i):
                dve.wait_ge(scores_done, i + 1)
                nc.vector.tensor_reduce(neg_max[:, i:i + 1], psL[:, :], AX.X, ALU.max, negate=True).then_inc(max_done, 1)

            def bisect(g, k0, k1):
                base, per = chain.n, T + 4
                with dve.Fori(0, k1 - k0) as r:
                    n = [0]

                    def link(ins):
                        n[0] += 1
                        ins.then_inc(chain_s, 1)
                        dve.wait_ge(chain_s, r * per + (base + n[0]))

                    link(nc.vector.tensor_scalar(trial[:, :], floor[:, :], factors[:, bass.ds(r + k0, 1)], None, ALU.mult))
                    for t in range(T):
                        slot = (g * T + t) % (2 * T)
                        link(nc.vector.scalar_tensor_tensor(
                            out=junk[:, :], in0=prob[:, slot, :], scalar=trial[:, t:t + 1], in1=prob[:, slot, :],
                            op0=ALU.is_ge, op1=ALU.mult, accum_out=mass[:, t:t + 1]))
                    link(nc.vector.tensor_tensor(step_up[:, :], mass[:, :], goal[:, :], ALU.is_ge))
                    link(nc.vector.tensor_tensor(step_up[:, :], step_up[:, :], trial[:, :], ALU.mult))
                    link(nc.vector.tensor_tensor(floor[:, :], floor[:, :], step_up[:, :], ALU.max))
                chain.n = base + per * (k1 - k0)

            for t in range(T):
                row_max(t)
            cuts = [5, 10, 15, 20, BISECT_STEPS]
            for g in range(G):
                dve.wait_ge(exp_done, (g + 1) * T)
                both = slice(g * T, (g + 1) * T)
                chain(nc.vector.tensor_scalar(goal[:, :], total[:, both], TOP_P, None, ALU.mult))
                chain(nc.vector.tensor_scalar(floor[:, :], total[:, both], (1 - TOP_P) / N * 0.99, None, ALU.mult))
                for n, (a, b) in enumerate(zip([0] + cuts, cuts)):
                    bisect(g, a, b)
                    if g + 1 < G and n < T:
                        row_max((g + 1) * T + n)
                for t in range(T):
                    i = g * T + t
                    row = prob[:, i % (2 * T), :]
                    nc.vector.scalar_tensor_tensor(out=row, in0=row, scalar=floor[:, t:t + 1], in1=row, op0=ALU.is_ge,
                                                   op1=ALU.mult, accum_out=kept[:, i:i + 1]).then_inc(mask_done, 1)
                dve.wait_ge(mask_done, (g + 1) * T)
                nc.vector.reciprocal(inv_kept[:, both], kept[:, both]).then_inc(inv_done, 1)

        @block.scalar
        def _(act):
            nT = nO = nY = nPT = 0

            def from_T(dst, scale=None):
                nonlocal nT
                act.wait_ge(t_filled, nT + 1)
                nc.scalar.copy(dst, psT[nT % 2][:, :] if len(dst.shape) == 2 else
                               psT[nT % 2][:, :].rearrange("p (k i) -> p k i", k=KT)).then_inc(t_emptied, 1)
                nT += 1

            for what, i in order():
                if what == "scores":
                    act.wait_ge(max_done, i + 1)
                    if i >= 2 * T:
                        act.wait_ge(pt_used, (i - 2 * T + 1) * CH)
                    nc.scalar.activation(prob[:, i % (2 * T), :], psL[:, :], ACT.Exp, bias=neg_max[:, i:i + 1],
                                         accum_out=total[:, i:i + 1]).then_inc(exp_done, 1)
                elif what == "relate":
                    act.wait_ge(adj_used, 2 * i + 2)
                    if not last_step and i >= 2:
                        act.wait_ge(xf_out[i % 2], 16 * (i // 2))
                    nc.scalar.activation(xf_row[:, i % 2, :], psO[:, :], ACT.Copy,
                                         scale=inv_degree[:, i:i + 1]).then_inc(o_emptied, 1)
                    nO += 1
                    if i >= T:
                        act.wait_ge(y_filled, Y_turn["attend", i - T] + 1)
                    from_T(XfT[:, i % T, :, :])
                elif what == "attend":
                    for c in range(CH):
                        if nPT >= 2:
                            act.wait_ge(pt_used, nPT - 1)
                        from_T(PT[:, nPT % 2, :])
                        nPT += 1
                    act.wait_ge(pt_used, nPT)
                    act.wait_ge(inv_done, i // T + 1)
                    row = xa_row[:, i % 2, :] if last_step else Xn[:, i, :]
                    nc.scalar.activation(row, psO[:, :], ACT.Copy, scale=inv_kept[:, i:i + 1]).then_inc(o_emptied, 1)
                    nO += 1
                    if i % T == 0 and i and not last_step:
                        act.wait_ge(y_filled, nY)
                    elif last_step and i >= T:
                        act.wait_ge(y_filled, Y_turn["attend", i - T] + 1)
                    from_T(XaT[:, :, (i % T) * P:(i % T + 1) * P])
                    act.wait_ge(y_filled, nY + 1)
                    if i:
                        act.wait_ge(y_out, 16 * i)
                    nc.scalar.copy(y_row[:, :], psY[:, :]).then_inc(y_emptied, 1)
                    nY += 1
                elif what == "project":
                    nY = project_qk_act(nc, act, psY, q_row, QK[1], i, y_filled, y_emptied, nY)

        @block.tensor
        def _(pe):
            nT = nO = nY = nPT = 0

            def to_T(srcs):
                nonlocal nT
                if nT >= 2:
                    pe.wait_ge(t_emptied, nT - 1)
                for n, src in enumerate(srcs):
                    tr = nc.tensor.transpose(psT[nT % 2][:, n * P:(n + 1) * P], src, ident[:, :])
                tr.then_inc(t_filled, 1)
                nT += 1

            for what, i in order():
                if what == "scores":
                    pe.wait_ge(q_staged, i + 1)
                    if i:
                        pe.wait_ge(exp_done, i)
                    for c in range(CH):
                        mm = nc.tensor.matmul(psL[:, c * 512:(c + 1) * 512], q_tile[:, i % 2, :],
                                              own[0:64, c * 512:(c + 1) * 512], start=True, stop=True)
                    mm.then_inc(scores_done, 1)
                elif what == "relate":
                    if i == 0:
                        if last_step:
                            pe.wait_ge(xf_in, 16)
                        pe.wait_ge(u_in, 32)
                    if nO:
                        pe.wait_ge(o_emptied, nO)
                    nc.tensor.matmul(psO[:, :], ident[:, :], Xf[:, i, :], start=True, stop=False)
                    for half in range(2):
                        n = 2 * i + half
                        pe.wait_ge(adj_in[n % 3], 16 * (n // 3 + 1))
                        for jj in range(NT // 2):
                            j = half * NT // 2 + jj
                            mm = nc.tensor.matmul(psO[:, :], adj_T[:, n % 3, jj, :], Xf[:, j, :],
                                                  start=False, stop=(j == NT - 1))
                        mm.then_inc(adj_used, 1)
                    nO += 1
                    pe.wait_ge(o_emptied, nO)
                    to_T([xf_row[:, i % 2, k * P:(k + 1) * P] for k in range(KT)])
                elif what == "attend":
                    pe.wait_ge(mask_done, i + 1)

                    def transpose_part(c):
                        to_T([prob[:, i % (2 * T), (4 * c + n) * P:(4 * c + n + 1) * P] for n in range(4)])

                    transpose_part(0)
                    for c in range(CH):
                        if c + 1 < CH:
                            transpose_part(c + 1)
                        pe.wait_ge(t_emptied, nT - (1 if c + 1 < CH else 0))
                        if c == 0 and nO:
                            pe.wait_ge(o_emptied, nO)
                        for n in range(4):
                            j = 4 * c + n
                            mm = nc.tensor.matmul(psO[:, :], PT[:, nPT % 2, n * P:(n + 1) * P], Xa[:, j, :],
                                                  start=(j == 0), stop=(j == NT - 1))
                        mm.then_inc(pt_used, 1)
                        nPT += 1
                    nO += 1
                    pe.wait_ge(o_emptied, nO)
                    row = xa_row[:, i % 2, :] if last_step else Xn[:, i, :]
                    to_T([row[:, k * P:(k + 1) * P] for k in range(KT)])
                    if nY:
                        pe.wait_ge(y_emptied, nY)
                    if last_step:
                        pe.wait_ge(yin[i % 2], 16 * (i // 2 + 1))
                    before = y_before[:, i % 2, :] if last_step else Xf[:, i, :]
                    nc.tensor.matmul(psY[:, :], ident[:, :], before, start=True, stop=False)
                    for k in range(KT):
                        nc.tensor.matmul(psY[:, :], XfT[:, i % T, k, :], u1[:, k, :], start=False, stop=False)
                    pe.wait_ge(t_emptied, nT)
                    for k in range(KT):
                        mm = nc.tensor.matmul(psY[:, :], XaT[:, k, (i % T) * P:(i % T + 1) * P], u2[:, k, :],
                                              start=False, stop=(k == KT - 1))
                    mm.then_inc(y_filled, 1)
                    nY += 1
                elif what == "project":
                    nY = project_qk_pe(nc, pe, XaT, w, psY, q_row, y_filled, y_emptied, nY, None)


def project_phase(nc, io, used_sems, qT, kT, V, ident, ones_row, y_dram, x1_dram, tiled):
    N, D = io["x"].shape
    NT, KT, T = N // P, D // P, 4
    G = NT // T
    with ExitStack() as scope:
        sb = lambda n, s, d=F32: scope.enter_context(nc.sbuf_tensor("p_" + n, s, d))
        sem = lambda n: scope.enter_context(nc.semaphore("p_" + n))
        wq, wk, wv = (sb(n, [P, KT, D]) for n in ("wq", "wk", "wv"))
        bq, bk, bv = sb("bq", [P, KT]), sb("bk", [P, KT]), sb("bv", [1, D])
        gamma, beta = sb("gamma", [P, D]), sb("beta", [P, D])
        rows, x_rows, h = sb("rows", [P, T, D]), sb("x_rows", [P, T, D]), sb("h", [P, 2, T, D])
        HT = sb("HT", [P, KT, T * P])
        stats, mv, rstd = sb("stats", [P, T, 6]), sb("mv", [P, T, 2]), sb("rstd", [P, 3, T])
        psT = [scope.enter_context(nc.psum_tensor(f"p_psT{b}", [P, 512], F32)) for b in range(2)]
        psM = [scope.enter_context(nc.psum_tensor(f"p_psM{b}", [P, 512], F32)) for b in range(4)]
        w_in, bias_in, y_in, x_in, x1_out = (sem(n) for n in ("w_in", "bias_in", "y_in", "x_in", "x1_out"))
        y_free, x1_ready, h_ready = sem("y_free"), sem("x1_ready"), sem("h_ready")
        sqrt_asked, sqrt_done, chain_s = sem("sqrt_asked"), sem("sqrt_done"), sem("chain")
        t_filled, t_emptied, m_filled, m_emptied = (sem(n) for n in ("t_filled", "t_emptied", "m_filled", "m_emptied"))
        products = 3 * T
        block = scope.enter_context(nc.Block())

        @block.sync
        def _(sp):
            sp.dma_start(gamma[:], io["l0_gamma"].partition_broadcast(P)).then_inc(bias_in, 16)
            sp.dma_start(beta[:], io["l0_beta"].partition_broadcast(P)).then_inc(bias_in, 16)
            for g in range(G):
                both = slice(g * T, (g + 1) * T)
                if g:
                    sp.wait_ge(y_free, g)
                sp.dma_start(rows[:], tiled(y_dram)[:, both, :]).then_inc(y_in, 16)
                if g:
                    sp.wait_ge(x1_ready, g)
                    sp.dma_start(tiled(x1_dram)[:, (g - 1) * T:g * T, :], x_rows[:]).then_inc(x1_out, 16)
                    sp.wait_ge(x1_out, 16 * g)
                    sp.wait_ge(h_ready, g)
                sp.dma_start(x_rows[:], tiled(io["x"])[:, both, :]).then_inc(x_in, 16)
                if g == 0:
                    for t, name in ((wq, "l1_wq"), (wk, "l1_wk"), (wv, "l1_wv")):
                        sp.dma_start(t[:], io[name].rearrange("(k p) n -> p k n", p=P)).then_inc(w_in, 16)
                    sp.dma_start(bq[:], io["l1_bq"]).then_inc(bias_in, 16)
                    sp.dma_start(bk[:], io["l1_bk"]).then_inc(bias_in, 16)
                    sp.dma_start(bv[:], io["l1_bv"].partition_broadcast(1)).then_inc(bias_in, 16)
            sp.wait_ge(x1_ready, G)
            sp.dma_start(tiled(x1_dram)[:, (G - 1) * T:, :], x_rows[:]).then_inc(x1_out, 16)
            sp.wait_ge(x1_out, 16 * G)

        @block.gpsimd
        def _(pool):
            pool.sem_clear(used_sems)

        @block.vector
        def _(dve):
            chain = Chain(dve, chain_s)
            turn = 0
            for g in range(G):
                dve.wait_ge(y_in, 16 * (g + 1))
                layer_norm_batch(nc, chain, rows, rows, stats, mv, rstd, sqrt_asked, sqrt_done, turn, relu=False)
                turn += 1
                if g == 0:
                    dve.wait_ge(bias_in, 80)
                chain.last_of([nc.vector.tensor_tensor(rows[:, t, :], rows[:, t, :], gamma[:], ALU.mult) for t in range(T)])
                chain.last_of([nc.vector.tensor_tensor(rows[:, t, :], rows[:, t, :], beta[:], ALU.add) for t in range(T)])
                dve.wait_ge(x_in, 16 * (g + 1))
                nc.vector.tensor_tensor(x_rows[:], x_rows[:], rows[:], ALU.add).then_inc(x1_ready, 1)
                dve.wait_ge(x1_ready, g + 1)
                dve.sem_inc(y_free, 1)
                if g >= 2:
                    dve.wait_ge(t_filled, (g - 1) * KT)
                layer_norm_batch(nc, chain, x_rows, h[:, g % 2, :, :], stats, mv, rstd, sqrt_asked, sqrt_done, turn, relu=True)
                turn += 1
                dve.sem_inc(h_ready, 1)

        @block.scalar
        def _(act):
            n = 0

            def move(g):
                nonlocal n
                for k in range(KT):
                    act.wait_ge(t_filled, g * KT + k + 1)
                    if g and k == 0:
                        act.wait_ge(m_filled, g * products)
                    nc.scalar.copy(HT[:, k, :], psT[k % 2][:, :]).then_inc(t_emptied, 1)
                if g == 0:
                    act.wait_ge(bias_in, 80)
                for dst, bias in ((qT, bq), (kT, bk)):
                    for m in range(KT):
                        act.wait_ge(m_filled, n + 1)
                        nc.scalar.activation(dst[:, m, g * 512:(g + 1) * 512], psM[n % 4][:, :], ACT.Identity,
                                             bias=bias[:, m:m + 1]).then_inc(m_emptied, 1)
                        n += 1
                for t in range(T):
                    act.wait_ge(m_filled, n + 1)
                    nc.scalar.copy(V[:, g * T + t, :], psM[n % 4][:, :]).then_inc(m_emptied, 1)
                    n += 1

            for g in range(G):
                layer_norm_sqrt(nc, act, rstd, sqrt_asked, sqrt_done, 2 * g)
                layer_norm_sqrt(nc, act, rstd, sqrt_asked, sqrt_done, 2 * g + 1)
                if g:
                    move(g - 1)
            move(G - 1)

        @block.tensor
        def _(pe):
            n = 0

            def bank():
                if n >= 4:
                    pe.wait_ge(m_emptied, n - 3)
                return psM[n % 4]

            for g in range(G):
                pe.wait_ge(h_ready, g + 1)
                for k in range(KT):
                    if g * KT + k >= 2:
                        pe.wait_ge(t_emptied, g * KT + k - 1)
                    for t in range(T):
                        tr = nc.tensor.transpose(psT[k % 2][:, t * P:(t + 1) * P], h[:, g % 2, t, k * P:(k + 1) * P], ident[:])
                    tr.then_inc(t_filled, 1)
                pe.wait_ge(t_emptied, (g + 1) * KT)
                if g == 0:
                    pe.wait_ge(w_in, 48)
                    pe.wait_ge(bias_in, 80)
                for weight in (wq, wk):
                    for m in range(KT):
                        ps = bank()
                        for k in range(KT):
                            mm = nc.tensor.matmul(ps[:, :], weight[:, k, m * P:(m + 1) * P], HT[:, k, :], start=(k == 0), stop=(k == KT - 1))
                        mm.then_inc(m_filled, 1)
                        n += 1
                for t in range(T):
                    ps = bank()
                    nc.tensor.matmul(ps[:, :], ones_row[:, :], bv[:, :], start=True, stop=False)
                    for k in range(KT):
                        mm = nc.tensor.matmul(ps[:, :], HT[:, k, t * P:(t + 1) * P], wv[:, k, :], start=False, stop=(k == KT - 1))
                    mm.then_inc(m_filled, 1)
                    n += 1


def attention_phase(nc, io, qT, kT, V, ident, x1_dram, x2_dram, l2_dram, tiled):
    N, D = io["x"].shape
    NT, KT, T = N // P, D // P, 4
    CH = N // 512
    scale = 1.0 / math.sqrt(D)
    with ExitStack() as scope:
        sb = lambda n, s, d=F32: scope.enter_context(nc.sbuf_tensor("t_" + n, s, d))
        sem = lambda n: scope.enter_context(nc.semaphore("t_" + n))
        adj_rows, score, void = sb("adj_rows", [P, 2, N]), sb("score", [P, 2, N]), sb("void", [P, N])
        PT = sb("PT", [P, 4, 512])
        x_rows, h = sb("x_rows", [P, T, D]), sb("h", [P, T, D])
        o_row = sb("o_row", [P, 2, D])
        stats, mv, rstd = sb("stats", [P, T, 6]), sb("mv", [P, T, 2]), sb("rstd", [P, 3, T])
        row_max, neg_max, total, inv_total = (sb(n, [P, NT]) for n in ("row_max", "neg_max", "total", "inv_total"))
        psL = scope.enter_context(nc.psum_tensor("t_psL", [P, N], F32))
        psT = [scope.enter_context(nc.psum_tensor(f"t_psT{b}", [P, 512], F32)) for b in range(2)]
        psO = scope.enter_context(nc.psum_tensor("t_psO", [P, 512], F32))
        adj_in, x1_in, x2_out = [sem(f"adj_in{b}") for b in range(2)], sem("x1_in"), sem("x2_out")
        scores_done, scaled, max_done, exp_done, inv_done = (sem(n) for n in ("scores_done", "scaled", "max_done", "exp_done", "inv_done"))
        t_filled, t_emptied, pt_used, o_emptied, x2_ready, h_ready = (sem(n) for n in ("t_filled", "t_emptied", "pt_used", "o_emptied", "x2_ready", "h_ready"))
        sqrt_asked, sqrt_done, chain_s = sem("sqrt_asked"), sem("sqrt_done"), sem("chain")
        block = scope.enter_context(nc.Block())

        @block.sync
        def _(sp):
            def store(g):
                sp.wait_ge(h_ready, g + 1)
                sp.dma_start(tiled(x2_dram)[:, g * T:(g + 1) * T, :], x_rows[:]).then_inc(x2_out, 16)
                sp.dma_start(tiled(l2_dram)[:, g * T:(g + 1) * T, :], h[:]).then_inc(x2_out, 16)

            for i in range(NT):
                if i >= 2:
                    sp.wait_ge(scaled, i - 1)
                sp.dma_start(adj_rows[:, i % 2, :], io["adj"][i * P:(i + 1) * P, :]).then_inc(adj_in[i % 2], 16)
                if i % T == 2:
                    g = i // T
                    if g:
                        store(g - 1)
                        sp.wait_ge(x2_out, 32 * g)
                    sp.dma_start(x_rows[:], tiled(x1_dram)[:, g * T:(g + 1) * T, :]).then_inc(x1_in, 16)
            store(NT // T - 1)
            sp.wait_ge(x2_out, 32 * NT // T)

        @block.vector
        def _(dve):
            chain = Chain(dve, chain_s)
            for i in range(NT + 1):
                if i < NT:
                    s_i = score[:, i % 2, :]
                    dve.wait_ge(scores_done, i + 1)
                    dve.wait_ge(adj_in[i % 2], 16 * (i // 2 + 1))
                    if i >= 2:
                        dve.wait_ge(t_filled, (i - 1) * CH)
                    nc.vector.scalar_tensor_tensor(out=s_i, in0=psL[:, :], scalar=scale, in1=adj_rows[:, i % 2, :],
                                                   op0=ALU.mult, op1=ALU.mult).then_inc(scaled, 1)
                    dve.wait_ge(scaled, i + 1)
                    chain(nc.vector.tensor_scalar(void[:, :], s_i, 0.0, -10000.0, ALU.is_equal, ALU.mult))
                    chain(nc.vector.tensor_tensor_reduce(out=s_i, in0=s_i, in1=void[:, :], scale=1.0, scalar=-3.0e38,
                                                         op0=ALU.add, op1=ALU.max, accum_out=row_max[:, i:i + 1]))
                    nc.vector.tensor_scalar(neg_max[:, i:i + 1], row_max[:, i:i + 1], -1.0, None, ALU.mult).then_inc(max_done, 1)
                if i:
                    j = i - 1
                    dve.wait_ge(exp_done, j + 1)
                    nc.vector.reciprocal(inv_total[:, j:j + 1], total[:, j:j + 1]).then_inc(inv_done, 1)
                if i >= 2 or i == NT:
                    for j in ([i - 2] if i < NT else [i - 2, i - 1]):
                        g, t = j // T, j % T
                        if t == 0:
                            dve.wait_ge(x1_in, 16 * (g + 1))
                        dve.wait_ge(o_emptied, j + 1)
                        nc.vector.tensor_tensor(x_rows[:, t, :], x_rows[:, t, :], o_row[:, j % 2, :], ALU.add).then_inc(x2_ready, 1)
                        if t == T - 1:
                            dve.wait_ge(x2_ready, j + 1)
                            if g:
                                dve.wait_ge(x2_out, 32 * g)
                            layer_norm_batch(nc, chain, x_rows, h, stats, mv, rstd, sqrt_asked, sqrt_done, g, relu=True)
                            dve.sem_inc(h_ready, 1)

        @block.scalar
        def _(act):
            nT = 0
            for i in range(NT + 1):
                if i < NT:
                    act.wait_ge(max_done, i + 1)
                    s_i = score[:, i % 2, :]
                    nc.scalar.activation(s_i, s_i, ACT.Exp, bias=neg_max[:, i:i + 1], accum_out=total[:, i:i + 1]).then_inc(exp_done, 1)
                if i:
                    j = i - 1
                    for c in range(CH):
                        if nT >= 4:
                            act.wait_ge(pt_used, nT - 3)
                        act.wait_ge(t_filled, nT + 1)
                        nc.scalar.copy(PT[:, nT % 4, :], psT[nT % 2][:, :]).then_inc(t_emptied, 1)
                        nT += 1
                    act.wait_ge(pt_used, nT)
                    act.wait_ge(inv_done, j + 1)
                    if j >= 2:
                        act.wait_ge(x2_ready, j - 1)
                    nc.scalar.activation(o_row[:, j % 2, :], psO[:, :], ACT.Relu, scale=inv_total[:, j:j + 1]).then_inc(o_emptied, 1)
                if i >= 2 and (i - 2) % T == T - 1:
                    layer_norm_sqrt(nc, act, rstd, sqrt_asked, sqrt_done, (i - 2) // T)
            layer_norm_sqrt(nc, act, rstd, sqrt_asked, sqrt_done, NT // T - 1)

        @block.tensor
        def _(pe):
            nT = nPT = 0

            def transpose_part(i, c):
                nonlocal nT
                if nT >= 2:
                    pe.wait_ge(t_emptied, nT - 1)
                for n in range(4):
                    tr = nc.tensor.transpose(psT[nT % 2][:, n * P:(n + 1) * P],
                                             score[:, i % 2, (4 * c + n) * P:(4 * c + n + 1) * P], ident[:])
                tr.then_inc(t_filled, 1)
                nT += 1

            for i in range(NT + 1):
                if i < NT:
                    if i:
                        pe.wait_ge(scaled, i)
                    for c in range(CH):
                        for k in range(KT):
                            mm = nc.tensor.matmul(psL[:, c * 512:(c + 1) * 512], qT[:, k, i * P:(i + 1) * P],
                                                  kT[:, k, c * 512:(c + 1) * 512], start=(k == 0), stop=(k == KT - 1))
                    mm.then_inc(scores_done, 1)
                if i:
                    j = i - 1
                    pe.wait_ge(exp_done, j + 1)
                    transpose_part(j, 0)
                    for c in range(CH):
                        if c + 1 < CH:
                            transpose_part(j, c + 1)
                        pe.wait_ge(t_emptied, nT - (1 if c + 1 < CH else 0))
                        if c == 0 and j:
                            pe.wait_ge(o_emptied, j)
                        for n in range(4):
                            m = 4 * c + n
                            mm = nc.tensor.matmul(psO[:, :], PT[:, nPT % 4, n * P:(n + 1) * P], V[:, m, :],
                                                  start=(m == 0), stop=(m == NT - 1))
                        mm.then_inc(pt_used, 1)
                        nPT += 1


VOID = -1.0e30


def relation_phase(nc, io, ident, l2_dram, tiled):
    N, D = io["x"].shape
    NT, KT, T = N // P, D // P, 4
    G, CH = NT // T, N // 512
    E_ROWS, E_COLS = io["l2_pairs"].shape[0:2]
    HEADS, HID = io["l3_a1"].shape
    with ExitStack() as scope:
        sb = lambda n, s, d=F32: scope.enter_context(nc.sbuf_tensor("r_" + n, s, d))
        sem = lambda n: scope.enter_context(nc.semaphore("r_" + n))
        h_rows = sb("h_rows", [P, NT, D])
        qT, kT = sb("qT", [P, KT, N]), sb("kT", [P, KT, N])
        pairs_in = sb("pairs_in", [E_ROWS, E_COLS, 2], I32)
        pairs = sb("pairs", [E_ROWS, 2, E_COLS])
        tile_ids, row_id = sb("tile_ids", [P, P]), sb("row_id", [P, 1])
        column_id, none = sb("column_id", [P, N]), sb("none", [E_ROWS, 512], BF16)
        q_head = sb("q_head", [P, HEADS, P])
        with ExitStack() as inner:
            sbi = lambda n, s, d=F32: inner.enter_context(nc.sbuf_tensor("r_" + n, s, d))
            wq, wk, bq, bk = sbi("wq", [P, KT, D]), sbi("wk", [P, KT, D]), sbi("bq", [P, KT]), sbi("bk", [P, KT])
            HT = sbi("HT", [P, KT, T * P])
            psT = [inner.enter_context(nc.psum_tensor(f"r_psT{b}", [P, 512], F32)) for b in range(2)]
            psM = [inner.enter_context(nc.psum_tensor(f"r_psM{b}", [P, 512], F32)) for b in range(2)]
            loaded, t_filled, t_emptied = (inner.enter_context(nc.semaphore("r_" + n)) for n in ("loaded", "t_filled", "t_emptied"))
            m_filled, m_emptied = (inner.enter_context(nc.semaphore("r_" + n)) for n in ("m_filled", "m_emptied"))
            block = inner.enter_context(nc.Block())

            @block.sync
            def _(sp):
                sp.dma_start(h_rows[:], tiled(l2_dram)).then_inc(loaded, 16)
                for t, name in ((wq, "l2_wq"), (wk, "l2_wk")):
                    sp.dma_start(t[:], io[name].rearrange("(k p) n -> p k n", p=P)).then_inc(loaded, 16)
                for t, name in ((bq, "l2_bq"), (bk, "l2_bk"), (pairs_in, "l2_pairs")):
                    sp.dma_start(t[:], io[name]).then_inc(loaded, 16)

            @block.gpsimd
            def _(pool):
                for ids, step, rows in ((column_id, [1, N], 0), (tile_ids, [1, P], 0), (row_id, [1, 1], 1)):
                    nc.gpsimd.iota(ids[:], [step], base=0 if ids is column_id else -P, channel_multiplier=rows,
                                   allow_small_or_imprecise_dtypes=True)
                nc.gpsimd.memset(none[:], 0.0)
                nc.gpsimd.memset(q_head[:], 0.0)

            @block.vector
            def _(dve):
                dve.wait_ge(loaded, 96)
                nc.vector.tensor_copy(pairs[:].rearrange("p s e -> p e s"), pairs_in[:])

            @block.tensor
            def _(pe):
                pe.wait_ge(loaded, 96)
                nT = nM = 0
                for g in range(G):
                    if g:
                        pe.wait_ge(t_emptied, nT)
                    for k in range(KT):
                        if nT >= 2:
                            pe.wait_ge(t_emptied, nT - 1)
                        for t in range(T):
                            tr = nc.tensor.transpose(psT[nT % 2][:, t * P:(t + 1) * P], h_rows[:, g * T + t, k * P:(k + 1) * P], ident[:])
                        tr.then_inc(t_filled, 1)
                        nT += 1
                    pe.wait_ge(t_emptied, nT)
                    for weight in (wq, wk):
                        for m in range(KT):
                            if nM >= 2:
                                pe.wait_ge(m_emptied, nM - 1)
                            for k in range(KT):
                                mm = nc.tensor.matmul(psM[nM % 2][:, :], weight[:, k, m * P:(m + 1) * P], HT[:, k, :],
                                                      start=(k == 0), stop=(k == KT - 1))
                            mm.then_inc(m_filled, 1)
                            nM += 1

            @block.scalar
            def _(act):
                nT = nM = 0
                act.wait_ge(loaded, 96)
                for g in range(G):
                    for k in range(KT):
                        act.wait_ge(t_filled, nT + 1)
                        if g and k == 0:
                            act.wait_ge(m_filled, nM)
                        nc.scalar.copy(HT[:, k, :], psT[nT % 2][:, :]).then_inc(t_emptied, 1)
                        nT += 1
                    for dst, bias in ((qT, bq), (kT, bk)):
                        for m in range(KT):
                            act.wait_ge(m_filled, nM + 1)
                            nc.scalar.activation(dst[:, m, g * 512:(g + 1) * 512], psM[nM % 2][:, :], ACT.Identity,
                                                 bias=bias[:, m:m + 1]).then_inc(m_emptied, 1)
                            nM += 1

        adj_row, score, agg = (sb(n, [P, N]) for n in ("adj_row", "score", "agg"))
        own, listed, base = (sb(n, [P, N]) for n in ("own", "listed", "base"))
        hot_sub, hot_obj = sb("hot_sub", [E_ROWS, P], BF16), sb("hot_obj", [E_ROWS, N], BF16)
        agg_T, out_row = sb("agg_T", [P, NT, P]), sb("out_row", [P, D])
        neg_max, total, weight = sb("neg_max", [P, 1]), sb("total", [P, 1]), sb("weight", [P, 1])
        psL = scope.enter_context(nc.psum_tensor("r_psL", [P, N], F32))
        psT = [scope.enter_context(nc.psum_tensor(f"r_psA{b}", [P, 512], F32)) for b in range(2)]
        psO = scope.enter_context(nc.psum_tensor("r_psO", [P, 512], F32))
        chain_s = sem("chain")
        turn_open, adj_loaded, stored = sem("turn_open"), sem("adj_loaded"), sem("stored")
        hot_ready, hot_used, counted = sem("hot_ready"), sem("hot_used"), sem("counted")
        q_staged, base_ready, scores_done, max_done, exp_done, head_added = (
            sem(n) for n in ("q_staged", "base_ready", "scores_done", "max_done", "exp_done", "head_added"))
        t_filled, t_emptied, o_filled, o_emptied = (sem(n) for n in ("u_filled", "u_emptied", "o_filled", "o_emptied"))
        block = scope.enter_context(nc.Block())

        @block.sync
        def _(sp):
            sp.sem_inc(turn_open, 1)
            with sp.Fori(0, NT) as i:
                sp.dma_start(adj_row[:], io["adj"][bass.ds(i * P, P), :]).then_inc(adj_loaded, 16)
                sp.wait_ge(o_emptied, i + 1)
                sp.dma_start(l2_dram[bass.ds(i * P, P), :], out_row[:]).then_inc(stored, 16)
                sp.wait_ge(stored, i * 16 + 16)
                sp.sem_inc(turn_open, 1)

        @block.gpsimd
        def _(pool):
            with pool.Fori(0, NT) as i:
                pool.wait_ge(turn_open, i + 1)
                for odd in range(2):
                    rows = slice(odd * HID, (odd + 1) * HID)
                    nc.gpsimd.tensor_copy(q_head[rows, odd::2, :], qT[rows, :, bass.ds(i * P, P)]).then_inc(q_staged, 1)

        @block.vector
        def _(dve):
            steps = 2 + 7 + 4 * HEADS + 1
            with dve.Fori(0, NT) as i:
                n = [0]

                def link(ins):
                    n[0] += 1
                    ins.then_inc(chain_s, 1)
                    dve.wait_ge(chain_s, i * steps + n[0])

                dve.wait_ge(turn_open, i + 1)
                link(nc.vector.tensor_scalar(tile_ids[:], tile_ids[:], float(P), None, ALU.add))
                link(nc.vector.tensor_scalar(row_id[:], row_id[:], float(P), None, ALU.add))
                n[0] += 1
                nc.vector.memset(agg[:], 0.0).then_inc(chain_s, 1)
                with dve.Fori(0, E_COLS) as e:
                    dve.wait_ge(hot_used, i * E_COLS + e + 1)
                    nc.vector.tensor_scalar(hot_sub[:], tile_ids[0:E_ROWS, :], pairs[:, 0, bass.ds(e, 1)], None,
                                            ALU.is_equal).then_inc(hot_ready, 1)
                    nc.vector.tensor_scalar(hot_obj[:], column_id[0:E_ROWS, :], pairs[:, 1, bass.ds(e, 1)], None,
                                            ALU.is_equal).then_inc(hot_ready, 1)
                dve.wait_ge(counted, i + 1)
                link(nc.vector.tensor_scalar(own[:], column_id[:], row_id[:], None, ALU.is_equal))
                dve.wait_ge(adj_loaded, i * 16 + 16)
                link(nc.vector.tensor_scalar(adj_row[:], adj_row[:], 1.0, None, ALU.is_equal))
                link(nc.vector.scalar_tensor_tensor(out=listed[:], in0=psL[:], scalar=0.0, in1=adj_row[:],
                                                    op0=ALU.is_gt, op1=ALU.mult))
                link(nc.vector.scalar_tensor_tensor(out=listed[:], in0=own[:], scalar=0.0, in1=listed[:],
                                                    op0=ALU.is_equal, op1=ALU.mult))
                link(nc.vector.tensor_tensor(base[:], adj_row[:], own[:], ALU.max))
                link(nc.vector.tensor_scalar(base[:], base[:], 1.0, -VOID, ALU.subtract, ALU.mult))
                link(nc.vector.scalar_tensor_tensor(out=base[:], in0=own[:], scalar=1e-7, in1=base[:],
                                                    op0=ALU.mult, op1=ALU.add))
                dve.sem_inc(base_ready, 1)
                for h in range(HEADS):
                    dve.wait_ge(scores_done, i * HEADS + (h + 1))
                    link(nc.vector.scalar_tensor_tensor(out=score[:], in0=psL[:], scalar=1.0 / math.sqrt(HID), in1=listed[:],
                                                        op0=ALU.mult, op1=ALU.mult))
                    link(nc.vector.tensor_tensor(score[:], score[:], base[:], ALU.add))
                    nc.vector.tensor_reduce(neg_max[:], score[:], AX.X, ALU.max, negate=True).then_inc(max_done, 1)
                    dve.wait_ge(exp_done, i * HEADS + (h + 1))
                    link(nc.vector.tensor_scalar(total[:], total[:], float(HEADS), None, ALU.mult))
                    link(nc.vector.reciprocal(weight[:], total[:]))
                    nc.vector.scalar_tensor_tensor(out=agg[:], in0=score[:], scalar=weight[:], in1=agg[:],
                                                   op0=ALU.mult, op1=ALU.add).then_inc(head_added, 1)
                    dve.wait_ge(head_added, i * HEADS + (h + 1))

        @block.scalar
        def _(act):
            with act.Fori(0, NT) as i:
                for h in range(HEADS):
                    act.wait_ge(max_done, i * HEADS + (h + 1))
                    nc.scalar.activation(score[:], score[:], ACT.Exp, bias=neg_max[:], accum_out=total[:]).then_inc(exp_done, 1)
                for c in range(CH):
                    act.wait_ge(t_filled, i * CH + (c + 1))
                    nc.scalar.copy(agg_T[:, 4 * c:4 * c + 4, :], psT[c % 2][:, :].rearrange("p (n r) -> p n r", n=4)).then_inc(t_emptied, 1)
                act.wait_ge(o_filled, i + 1)
                nc.scalar.copy(out_row[:], psO[:]).then_inc(o_emptied, 1)

        @block.tensor
        def _(pe):
            pe.sem_inc(hot_used, 1)

            def add_nothing(start, stop):
                for c in range(CH):
                    mm = nc.tensor.matmul(psL[:, c * 512:(c + 1) * 512], none[:, 0:P], none[:], start=start, stop=stop)
                return mm

            with pe.Fori(0, NT) as i:
                pe.wait_ge(turn_open, i + 1)
                add_nothing(True, False)
                with pe.Fori(0, E_COLS) as e:
                    pe.wait_ge(hot_ready, i * (2 * E_COLS) + e * 2 + 2)
                    for c in range(CH):
                        mm = nc.tensor.matmul(psL[:, c * 512:(c + 1) * 512], hot_sub[:], hot_obj[:, c * 512:(c + 1) * 512],
                                              start=False, stop=False)
                    mm.then_inc(hot_used, 1)
                add_nothing(False, True).then_inc(counted, 1)
                pe.wait_ge(q_staged, i * 2 + 2)
                pe.wait_ge(base_ready, i + 1)
                for h in range(HEADS):
                    if h:
                        pe.wait_ge(max_done, i * HEADS + h)
                    for c in range(CH):
                        mm = nc.tensor.matmul(psL[:, c * 512:(c + 1) * 512], q_head[:, h, :], kT[:, h * HID // P, c * 512:(c + 1) * 512],
                                              start=True, stop=True)
                    mm.then_inc(scores_done, 1)
                pe.wait_ge(head_added, i * HEADS + HEADS)
                for c in range(CH):
                    if c >= 2:
                        pe.wait_ge(t_emptied, i * CH + (c - 1))
                    for n in range(4):
                        tr = nc.tensor.transpose(psT[c % 2][:, n * P:(n + 1) * P], agg[:, (4 * c + n) * P:(4 * c + n + 1) * P], ident[:])
                    tr.then_inc(t_filled, 1)
                pe.wait_ge(t_emptied, i * CH + CH)
                for j in range(NT):
                    mm = nc.tensor.matmul(psO[:], agg_T[:, j, :], h_rows[:, j, :], start=(j == 0), stop=(j == NT - 1))
                mm.then_inc(o_filled, 1)


def heads_phase(nc, io, Wh, edge, dst, dst_low, dst_neg, src_bias, ident, x2_dram, l2_dram, x3_dram, src_dram, tiled):
    N, D = io["x"].shape
    NT, KT, T = N // P, D // P, 4
    G = NT // T
    HEADS, HID = io["l3_a1"].shape
    with ExitStack() as scope:
        sb = lambda n, s, d=F32: scope.enter_context(nc.sbuf_tensor("h_" + n, s, d))
        sem = lambda n: scope.enter_context(nc.semaphore("h_" + n))
        w = sb("w", [P, KT, D])
        a1, a2 = sb("a1", [P, D]), sb("a2", [P, D])
        x_rows, l_rows = sb("x_rows", [P, T, D]), sb("l_rows", [P, T, D])
        HT = sb("HT", [P, KT, T * P])
        adj_T = sb("adj_T", [P, 2, NT, P])
        prod = sb("prod", [P, HEADS, HID])
        src, src_T = sb("src", [P, NT, HEADS]), sb("src_T", [HEADS, N])
        top, top_all = sb("top", [P, HEADS]), sb("top_all", [P, HEADS])
        stats, mv, rstd = sb("stats", [P, T, 6]), sb("mv", [P, T, 2]), sb("rstd", [P, 3, T])
        psT = [scope.enter_context(nc.psum_tensor(f"h_psT{b}", [P, 512], F32)) for b in range(2)]
        psM = [scope.enter_context(nc.psum_tensor(f"h_psM{b}", [P, 512], F32)) for b in range(2)]
        psS = [scope.enter_context(nc.psum_tensor(f"h_psS{b}", [HEADS, 512], F32)) for b in range(2)]
        w_in, x_in, x3_out, adj_in = sem("w_in"), sem("x_in"), sem("x3_out"), [sem(f"adj_in{b}") for b in range(2)]
        x3_ready, h_ready, edge_done, src_out = sem("x3_ready"), sem("h_ready"), sem("edge_done"), sem("src_out")
        sqrt_asked, sqrt_done, chain_s = sem("sqrt_asked"), sem("sqrt_done"), sem("chain")
        t_filled, t_emptied, m_filled, m_emptied = (sem(n) for n in ("t_filled", "t_emptied", "m_filled", "m_emptied"))
        one_set, src_done, s_filled, s_emptied = sem("one_set"), sem("src_done"), sem("s_filled"), sem("s_emptied")
        top_done, top_spread, bias_done = sem("top_done"), sem("top_spread"), sem("bias_done")
        block = scope.enter_context(nc.Block())

        @block.sync
        def _(sp):
            sp.dma_start(x_rows[:], tiled(x2_dram)[:, 0:T, :]).then_inc(x_in, 16)
            sp.dma_start(l_rows[:], tiled(l2_dram)[:, 0:T, :]).then_inc(x_in, 16)
            sp.dma_start(w[:], io["l3_w"].rearrange("(k p) n -> p k n", p=P)).then_inc(w_in, 16)
            sp.dma_start(a1[:], io["l3_a1"].rearrange("h d -> (h d)").partition_broadcast(P)).then_inc(w_in, 16)
            sp.dma_start(a2[:], io["l3_a2"].rearrange("h d -> (h d)").partition_broadcast(P)).then_inc(w_in, 16)
            for g in range(G):
                for i in range(g * T, (g + 1) * T):
                    if i >= 2:
                        sp.wait_ge(edge_done, i - 1)
                    sp.dma_start(adj_T[:, i % 2, :, :], io["adj_t"][:, :, i, :].rearrange("n p c -> p n c")).then_inc(adj_in[i % 2], 16)
                sp.wait_ge(x3_ready, g + 1)
                sp.dma_start(tiled(x3_dram)[:, g * T:(g + 1) * T, :], x_rows[:]).then_inc(x3_out, 16)
                if g + 1 < G:
                    sp.wait_ge(x3_out, 16 * (g + 1))
                    sp.wait_ge(t_filled, (g + 1) * KT)
                    sp.dma_start(x_rows[:], tiled(x2_dram)[:, (g + 1) * T:(g + 2) * T, :]).then_inc(x_in, 16)
                    sp.dma_start(l_rows[:], tiled(l2_dram)[:, (g + 1) * T:(g + 2) * T, :]).then_inc(x_in, 16)
            sp.wait_ge(s_emptied, N // 512)
            sp.dma_start(src_dram, src_T[:]).then_inc(src_out, 16)
            sp.wait_ge(src_out, 16)
            sp.wait_ge(x3_out, 16 * G)

        @block.gpsimd
        def _(pool):
            nc.gpsimd.memset(Wh[:, :, :, HID:HID + 1], 1.0).then_inc(one_set, 1)
            pool.wait_ge(top_done, 1)
            nc.gpsimd.partition_all_reduce(top_all[:], top[:], P, bass.bass_isa.ReduceOp.max).then_inc(top_spread, 1)

        @block.vector
        def _(dve):
            chain = Chain(dve, chain_s)

            def parts(i):
                dve.wait_ge(m_emptied, i + 1)
                for a, dest in ((a1, src), (a2, dst)):
                    chain(nc.vector.tensor_tensor(prod[:], Wh[:, i, :, 0:HID], a[:].rearrange("p (h d) -> p h d", h=HEADS), ALU.mult))
                    chain(nc.vector.tensor_reduce(dest[:, i, :], prod[:], AX.X, ALU.add))

            for g in range(G):
                dve.wait_ge(x_in, 32 * (g + 1))
                nc.vector.tensor_tensor(x_rows[:], x_rows[:], l_rows[:], ALU.add).then_inc(x3_ready, 1)
                dve.wait_ge(x3_ready, g + 1)
                layer_norm_batch(nc, chain, x_rows, l_rows, stats, mv, rstd, sqrt_asked, sqrt_done, g, relu=True)
                dve.sem_inc(h_ready, 1)
                for i in range(g * T, (g + 1) * T):
                    dve.wait_ge(adj_in[i % 2], 16 * (i // 2 + 1))
                    nc.vector.tensor_scalar(edge[:, i, :], adj_T[:, i % 2, :, :].rearrange("p n c -> p (n c)"), 0.0, None,
                                            ALU.is_gt).then_inc(edge_done, 1)
                if g == 0:
                    dve.wait_ge(w_in, 48)
                for i in range(g * T, (g + 1) * T):
                    parts(i)
            dve.sem_inc(src_done, 1)
            nc.vector.tensor_reduce(top[:], dst[:].rearrange("p n h -> p h n"), AX.X, ALU.max).then_inc(top_done, 1)
            dve.wait_ge(top_spread, 1)
            chain.last_of([nc.vector.tensor_tensor(dst[:, i, :], dst[:, i, :], top_all[:], ALU.subtract) for i in range(NT)])
            chain(nc.vector.tensor_scalar(dst_low[:], dst[:], SLOPE, -SHIFT, ALU.mult, ALU.add))
            chain(nc.vector.tensor_scalar(dst[:], dst[:], SHIFT, None, ALU.add))
            chain(nc.vector.tensor_scalar(src_bias[:], top_all[:], 1 - SLOPE, -2 * SHIFT, ALU.mult, ALU.add))
            dve.sem_inc(bias_done, 1)
            dve.wait_ge(s_emptied, N // 512 + 2)
            chain(nc.vector.tensor_scalar(dst_neg[:], dst_low[:], -1.0, None, ALU.mult))

        @block.scalar
        def _(act):
            act.wait_ge(one_set, 1)
            for g in range(G):
                layer_norm_sqrt(nc, act, rstd, sqrt_asked, sqrt_done, g)
                for k in range(KT):
                    act.wait_ge(t_filled, g * KT + k + 1)
                    if g and k == 0:
                        act.wait_ge(m_filled, g * T)
                    nc.scalar.copy(HT[:, k, :], psT[k % 2][:, :]).then_inc(t_emptied, 1)
                for i in range(g * T, (g + 1) * T):
                    act.wait_ge(m_filled, i + 1)
                    nc.scalar.copy(Wh[:, i, :, 0:HID], psM[i % 2][:, :].rearrange("p (h d) -> p h d", h=HEADS)).then_inc(m_emptied, 1)
            for c in range(N // 512):
                act.wait_ge(s_filled, c + 1)
                nc.scalar.copy(src_T[:, c * 512:(c + 1) * 512], psS[c % 2][:, :]).then_inc(s_emptied, 1)
            act.wait_ge(bias_done, 1)
            for t in (dst, dst_low):
                nc.scalar.activation(t[:], t[:], ACT.Exp).then_inc(s_emptied, 1)

        @block.tensor
        def _(pe):
            for g in range(G):
                pe.wait_ge(h_ready, g + 1)
                for k in range(KT):
                    if g * KT + k >= 2:
                        pe.wait_ge(t_emptied, g * KT + k - 1)
                    for t in range(T):
                        tr = nc.tensor.transpose(psT[k % 2][:, t * P:(t + 1) * P], l_rows[:, t, k * P:(k + 1) * P], ident[:])
                    tr.then_inc(t_filled, 1)
                pe.wait_ge(t_emptied, (g + 1) * KT)
                if g == 0:
                    pe.wait_ge(w_in, 48)
                for t in range(T):
                    i = g * T + t
                    if i >= 2:
                        pe.wait_ge(m_emptied, i - 1)
                    for k in range(KT):
                        mm = nc.tensor.matmul(psM[i % 2][:, :], HT[:, k, t * P:(t + 1) * P], w[:, k, :], start=(k == 0), stop=(k == KT - 1))
                    mm.then_inc(m_filled, 1)
            pe.wait_ge(src_done, 1)
            for c in range(N // 512):
                if c >= 2:
                    pe.wait_ge(s_emptied, c - 1)
                for n in range(4):
                    tr = nc.tensor.transpose(psS[c % 2][:, n * P:(n + 1) * P], src[:, 4 * c + n, :], ident[:])
                tr.then_inc(s_filled, 1)


SLOPE = 0.2
SHIFT = 40.0


def gat_phase(nc, Wh, edge, dst, dst_low, dst_neg, src_bias, enc, src_dram):
    _, NT, HEADS, W1 = Wh.shape
    HID, N = W1 - 1, edge.shape[2]
    PER = 512 // W1
    BANKS = -(-NT // PER)
    with ExitStack() as scope:
        sb = lambda n, s, d=F32: scope.enter_context(nc.sbuf_tensor("e_" + n, s, d))
        sem = lambda n: scope.enter_context(nc.semaphore("e_" + n))
        source = sb("source", [P, 2, N])
        above, prob = sb("above", [P, 2, N]), sb("prob", [P, 2, N])
        inv = sb("inv", [P, NT])
        acc = [[scope.enter_context(nc.psum_tensor(f"e_acc{b}{k}", [P, 512], F32)) for k in range(BANKS)] for b in range(2)]
        src_in, src_ready = [sem(f"src_in{b}") for b in range(2)], sem("src_ready")
        above_done, prob_done, prob_used, inv_done, acc_emptied = (sem(n) for n in ("above_done", "prob_done", "prob_used", "inv_done", "acc_emptied"))
        block = scope.enter_context(nc.Block())

        def sums(b, k):
            n = min(PER, NT - k * PER)
            return acc[b][k][:, 0:n * W1].rearrange("p (n w) -> p n w", w=W1), slice(k * PER, k * PER + n)

        @block.sync
        def _(sp):
            for h in range(HEADS):
                if h >= 2:
                    sp.wait_ge(above_done, (h - 1) * NT)
                sp.dma_start(source[:, h % 2, :], src_dram[h].partition_broadcast(P)).then_inc(src_in[h % 2], 16)

        @block.scalar
        def _(act):
            for h in range(HEADS):
                act.wait_ge(src_in[h % 2], 16 * (h // 2 + 1))
                row = source[:, h % 2, :]
                nc.scalar.activation(row, row, ACT.Exp, scale=1 - SLOPE, bias=src_bias[:, h:h + 1]).then_inc(src_ready, 1)
                act.wait_ge(src_ready, h + 1)
                for j in range(NT):
                    n = h * NT + j
                    if n >= 2:
                        act.wait_ge(prob_done, n - 1)
                    nc.scalar.activation(above[:, n % 2, :], row, ACT.Relu, scale=dst[:, j, h:h + 1],
                                         bias=dst_neg[:, j, h:h + 1]).then_inc(above_done, 1)

        @block.vector
        def _(dve):
            def take(h):
                b = h % 2
                dve.wait_ge(prob_used, (h + 1) * NT)
                for k in range(BANKS):
                    s, tiles = sums(b, k)
                    nc.vector.reciprocal(inv[:, tiles], s[:, :, HID]).then_inc(inv_done, 1)
                dve.wait_ge(inv_done, (h + 1) * BANKS)
                for k in range(BANKS):
                    s, tiles = sums(b, k)
                    n = s.shape[1]
                    nc.vector.tensor_tensor(enc[:, tiles, h * HID:(h + 1) * HID], s[:, :, 0:HID],
                                            inv[:, tiles].unsqueeze(2).broadcast_to([P, n, HID]), ALU.mult).then_inc(acc_emptied, 1)

            for h in range(HEADS):
                for j in range(NT):
                    n = h * NT + j
                    dve.wait_ge(above_done, n + 1)
                    if n >= 2:
                        dve.wait_ge(prob_used, n - 1)
                    nc.vector.scalar_tensor_tensor(out=prob[:, n % 2, :], in0=above[:, n % 2, :], scalar=dst_low[:, j, h:h + 1],
                                                   in1=edge[:, j, :], op0=ALU.add, op1=ALU.mult).then_inc(prob_done, 1)
                    if h and j == 2:
                        take(h - 1)
            take(HEADS - 1)

        @block.tensor
        def _(pe):
            for h in range(HEADS):
                if h >= 2:
                    pe.wait_ge(acc_emptied, (h - 1) * BANKS)
                for j in range(NT):
                    n = h * NT + j
                    pe.wait_ge(prob_done, n + 1)
                    for i in range(NT):
                        k, m = i // PER, i % PER
                        mm = nc.tensor.matmul(acc[h % 2][k][:, m * W1:(m + 1) * W1], prob[:, n % 2, i * P:(i + 1) * P], Wh[:, j, h, :],
                                              start=(j == 0 and m == 0), stop=(j == NT - 1), skip_group_check=True)
                    mm.then_inc(prob_used, 1)


def mlp_phase(nc, io, enc, ident, ones_row, x3_dram, out, tiled):
    _, NT, D = enc.shape
    KT, T = D // P, 4
    G = NT // T
    widths = [io[f"l3_w{n}"].shape[1] for n in range(1, 5)]
    with ExitStack() as scope:
        sb = lambda n, s, d=F32: scope.enter_context(nc.sbuf_tensor("f_" + n, s, d))
        sem = lambda n: scope.enter_context(nc.semaphore("f_" + n))
        w, b = [], []
        for n in range(1, 5):
            rows, cols = io[f"l3_w{n}"].shape
            w.append(sb(f"w{n}", [P, rows // P, cols]))
            b.append(sb(f"b{n}", [P, cols // P] if n < 4 else [1, cols]))
        low, lifted, act_in = sb("low", [P, T, D]), sb("lifted", [P, T, D]), sb("act_in", [P, 2, T, D])
        x_rows = sb("x_rows", [P, 2, T, D])
        o_rows = sb("o_rows", [P, 2, D])
        layers = [sb("layer0", [P, KT, 512])] + [sb(f"layer{n}", [P, widths[n - 1] // P, 512]) for n in range(1, 4)]
        psT = [scope.enter_context(nc.psum_tensor(f"f_psT{k}", [P, 512], F32)) for k in range(2)]
        psM = [scope.enter_context(nc.psum_tensor(f"f_psM{k}", [P, 512], F32)) for k in range(4)]
        w_in, x_in, o_out = sem("w_in"), [sem(f"x_in{k}") for k in range(2)], [sem(f"o_out{k}") for k in range(2)]
        low_done, exp_done, elu_done, chain_s = sem("low_done"), sem("exp_done"), sem("elu_done"), sem("chain")
        t_filled, t_emptied, m_filled, m_emptied = (sem(n) for n in ("t_filled", "t_emptied", "m_filled", "m_emptied"))
        sizes = [widths[n] // P for n in range(3)]
        block = scope.enter_context(nc.Block())
        per_batch = sum(sizes) + T

        def store(sp, g):
            for t in range(T):
                i = g * T + t
                sp.wait_ge(m_emptied, g * per_batch + sum(sizes) + t + 1)
                sp.dma_start(tiled(out)[:, i, :], o_rows[:, i % 2, :]).then_inc(o_out[i % 2], 16)

        @block.sync
        def _(sp):
            for n in range(4):
                sp.dma_start(w[n][:], io[f"l3_w{n + 1}"].rearrange("(k p) n -> p k n", p=P)).then_inc(w_in, 16)
                sp.dma_start(b[n][:], io[f"l3_b{n + 1}"]).then_inc(w_in, 16)
            for g in range(G):
                if g >= 2:
                    sp.wait_ge(m_filled, (g - 1) * per_batch)
                sp.dma_start(x_rows[:, g % 2, :, :], tiled(x3_dram)[:, g * T:(g + 1) * T, :]).then_inc(x_in[g % 2], 16)
                if g:
                    store(sp, g - 1)
            store(sp, G - 1)
            for k in range(2):
                sp.wait_ge(o_out[k], 16 * NT // 2)

        @block.vector
        def _(dve):
            chain = Chain(dve, chain_s)
            for g in range(G):
                part = enc[:, g * T:(g + 1) * T, :]
                if g:
                    dve.wait_ge(elu_done, g)
                nc.vector.tensor_scalar(low[:], part, 0.0, None, ALU.min).then_inc(low_done, 1)
                chain(nc.vector.tensor_scalar(lifted[:], part, 0.0, -1.0, ALU.max, ALU.add))
                dve.wait_ge(exp_done, g + 1)
                if g >= 2:
                    dve.wait_ge(t_filled, (g - 1) * KT)
                nc.vector.tensor_tensor(act_in[:, g % 2, :, :], low[:], lifted[:], ALU.add).then_inc(elu_done, 1)

        @block.scalar
        def _(act):
            n = 0
            act.wait_ge(w_in, 128)

            def elu_exp(g):
                act.wait_ge(low_done, g + 1)
                nc.scalar.activation(low[:], low[:], ACT.Exp).then_inc(exp_done, 1)

            elu_exp(0)
            for g in range(G):
                if g + 1 < G:
                    elu_exp(g + 1)
                for k in range(KT):
                    act.wait_ge(t_filled, g * KT + k + 1)
                    nc.scalar.copy(layers[0][:, k, :], psT[k % 2][:, :]).then_inc(t_emptied, 1)
                for layer in range(3):
                    for m in range(sizes[layer]):
                        act.wait_ge(m_filled, n + 1)
                        nc.scalar.activation(layers[layer + 1][:, m, :], psM[n % 4][:, :], ACT.Relu,
                                             bias=b[layer][:, m:m + 1]).then_inc(m_emptied, 1)
                        n += 1
                for t in range(T):
                    i = g * T + t
                    act.wait_ge(m_filled, n + 1)
                    if i >= 2:
                        act.wait_ge(o_out[i % 2], 16 * (i // 2))
                    nc.scalar.copy(o_rows[:, i % 2, :], psM[n % 4][:, :]).then_inc(m_emptied, 1)
                    n += 1

        @block.tensor
        def _(pe):
            n = 0

            def bank():
                if n >= 4:
                    pe.wait_ge(m_emptied, n - 3)
                return psM[n % 4]

            pe.wait_ge(w_in, 128)
            for g in range(G):
                pe.wait_ge(elu_done, g + 1)
                for k in range(KT):
                    if g * KT + k >= 2:
                        pe.wait_ge(t_emptied, g * KT + k - 1)
                    for t in range(T):
                        tr = nc.tensor.transpose(psT[k % 2][:, t * P:(t + 1) * P], act_in[:, g % 2, t, k * P:(k + 1) * P], ident[:])
                    tr.then_inc(t_filled, 1)
                pe.wait_ge(t_emptied, (g + 1) * KT)
                for layer in range(3):
                    for m in range(sizes[layer]):
                        ps = bank()
                        K = layers[layer].shape[1]
                        for k in range(K):
                            mm = nc.tensor.matmul(ps[:, :], w[layer][:, k, m * P:(m + 1) * P], layers[layer][:, k, :],
                                                  start=(k == 0), stop=(k == K - 1))
                        mm.then_inc(m_filled, 1)
                        n += 1
                    pe.wait_ge(m_emptied, n)
                pe.wait_ge(x_in[g % 2], 16 * (g // 2 + 1))
                for t in range(T):
                    ps = bank()
                    nc.tensor.matmul(ps[:, :], ident[:], x_rows[:, g % 2, t, :], start=True, stop=False)
                    nc.tensor.matmul(ps[:, :], ones_row[:, :], b[3][:, :], start=False, stop=False)
                    for k in range(2):
                        mm = nc.tensor.matmul(ps[:, :], layers[3][:, k, t * P:(t + 1) * P], w[3][:, k, :],
                                              start=False, stop=(k == 1))
                    mm.then_inc(m_filled, 1)
                    n += 1


def laid_out(np, v):
    adj = v["adj"]
    n = adj.shape[0] // P
    heads, d, hid = v["L3_gnn_W"].shape
    columns = lambda b: b.reshape(-1, P).T
    out = {
        "x": v["x"], "adj": adj, "adj_t": adj.reshape(n, P, n, P).transpose(0, 3, 2, 1),
        "l0_w1": v["L0_gnn_W1"], "l0_w2": v["L0_gnn_W2"], "l0_w3": v["L0_gnn_W3"],
        "l0_u1_0": v["L0_gnn_U1_0"], "l0_u1_1": v["L0_gnn_U1_1"], "l0_u2_0": v["L0_gnn_U2_0"], "l0_u2_1": v["L0_gnn_U2_1"],
        "l0_gamma": v["L0_gnn_gamma"], "l0_beta": v["L0_gnn_beta"],
        "l1_wq": v["L1_gnn_W_q"].T, "l1_wk": v["L1_gnn_W_k"].T, "l1_wv": v["L1_gnn_W_v"].T,
        "l1_bq": columns(v["L1_gnn_b_q"]), "l1_bk": columns(v["L1_gnn_b_k"]), "l1_bv": v["L1_gnn_b_v"],
        "l2_wq": v["L2_gnn_Wq"].T, "l2_wk": v["L2_gnn_Wk"].T, "l2_bq": columns(v["L2_gnn_bq"]), "l2_bk": columns(v["L2_gnn_bk"]),
        "l2_pairs": v["L2_gnn_rel_pair_index"].reshape(125, -1, 2),
        "l3_w": v["L3_gnn_W"].transpose(1, 0, 2).reshape(d, heads * hid), "l3_a1": v["L3_gnn_a1"], "l3_a2": v["L3_gnn_a2"],
    }
    for k in range(1, 5):
        out[f"l3_w{k}"] = v[f"L3_gnn_W{k}"].T
        out[f"l3_b{k}"] = columns(v[f"L3_gnn_b{k}"]) if k < 4 else v["L3_gnn_b4"].reshape(1, -1)
    return {name: np.ascontiguousarray(a) for name, a in out.items()}


def kernel(**inputs):
    import numpy as _np
    import concourse.bacc as _bacc
    from concourse import mybir as _mybir
    from concourse.bass_utils import run_bass_kernel_spmd as _run

    nc = _bacc.Bacc("TRN2", target_bir_lowering=False, num_devices=1)
    arrays = laid_out(_np, {k: _np.asarray(v) for k, v in inputs.items()})
    io = {k: nc.dram_tensor(f"in_{k}_dram", a.shape, _mybir.dt.from_np(a.dtype), kind="ExternalInput").ap()
          for k, a in arrays.items()}
    out = nc.dram_tensor("out_dram", inputs["x"].shape, F32, kind="ExternalOutput").ap()
    build(nc, io, out)
    r = _run(nc, [{f"in_{k}_dram": a for k, a in arrays.items()}], core_ids=[0])
    return r.results[0]["out_dram"]
```

```python
from contextlib import ExitStack
import math

import concourse.bass as bass
from concourse import mybir

F32 = mybir.dt.float32
BF16 = mybir.dt.bfloat16
I32 = mybir.dt.int32
ALU = mybir.AluOpType
ACT = mybir.ActivationFunctionType
AX = mybir.AxisListType

P = 128
EPS = 1e-5
TOP_P = 0.9
BISECT_STEPS = 21


class Chain:

    def __init__(self, eng, sem):
        self.eng, self.sem, self.n = eng, sem, 0

    def __call__(self, ins):
        self.n += 1
        ins.then_inc(self.sem, 1)
        self.eng.wait_ge(self.sem, self.n)

    def last_of(self, group):
        for ins in group:
            self.n += 1
            ins.then_inc(self.sem, 1)
        self.eng.wait_ge(self.sem, self.n)


def make_identity(nc, pool, ident, made):
    nc.gpsimd.memset(ident[:], 0.0).then_inc(made, 1)
    pool.wait_ge(made, 1)
    nc.gpsimd.affine_select(out=ident[:], in_=ident[:], compare_op=ALU.not_equal, fill=1.0, base=0,
                            pattern=[[-1, P]], channel_multiplier=1).then_inc(made, 1)


def layer_norm_batch(nc, chain, src, dst, stats, mv, rstd, sqrt_asked, sqrt_done, turn, relu, act_turn=None):
    T = src.shape[1]
    chain.last_of([nc.vector.bn_stats(stats[:, t, :], src[:, t, :]) for t in range(T)])
    chain.last_of([nc.vector.bn_aggr(mv[:, t, :], stats[:, t, :]) for t in range(T)])
    nc.vector.tensor_scalar(rstd[:, 0, :], mv[:, :, 1], EPS, None, ALU.add).then_inc(sqrt_asked, 1)
    chain.eng.wait_ge(sqrt_done, turn + 1)
    chain(nc.vector.reciprocal(rstd[:, 2, :], rstd[:, 1, :]))
    chain.last_of([nc.vector.tensor_scalar(dst[:, t, :], src[:, t, :], mv[:, t, 0:1], rstd[:, 2, t:t + 1],
                                           ALU.subtract, ALU.mult) for t in range(T)])
    if relu:
        chain(nc.vector.tensor_scalar(dst[:, :, :], dst[:, :, :], 0.0, None, ALU.max))


def layer_norm_sqrt(nc, act, rstd, sqrt_asked, sqrt_done, turn):
    act.wait_ge(sqrt_asked, turn + 1)
    nc.scalar.activation(rstd[:, 1, :], rstd[:, 0, :], ACT.Sqrt).then_inc(sqrt_done, 1)


def build(nc, io, out):
    N, D = io["x"].shape
    A = io["l0_w1"].shape[1]
    NT, KT = N // P, D // P
    HEADS, HID = io["l3_a1"].shape

    scratch = lambda name, shape=(N, D): nc.dram_tensor(name, list(shape), F32).ap()
    y_dram = [scratch(f"y{s}_scratch") for s in range(2)]
    xf_dram, x1_dram, x2_dram, l2_dram, x3_dram = (scratch(n) for n in ("xf", "x1", "x2", "l2", "x3"))
    src_dram = scratch("src", (HEADS, N))
    tiled = lambda ap: ap.rearrange("(n p) d -> p n d", p=P)

    with ExitStack() as whole:
        hold = lambda n, s, d=F32: whole.enter_context(nc.sbuf_tensor(n, s, d))
        ident, ones_row = hold("ident", [P, P]), hold("ones_row", [1, P])
        inv_degree, ones_seen = hold("inv_degree", [P, NT]), hold("ones_seen", [P, NT + 1])
        has_ones = hold("has_ones", [P, 1], I32)
        with ExitStack() as scope:
            sb = lambda n, s, d=F32: scope.enter_context(nc.sbuf_tensor(n, s, d))
            XA = [sb("feat0", [P, NT, D]), sb("feat1", [P, NT, D])]
            QK = [sb("qk0", [P, N]), sb("qk1", [P, N])]
            w1, w3 = sb("w1", [P, KT, A]), sb("w3", [P, KT, A])
            w2 = sb("w2", [A, A])
            first_sem = norm_phase(nc, io, XA[0], QK[0], (w1, w2, w3), ident, ones_row, inv_degree, ones_seen, has_ones, tiled)
            for s in range(2):
                last_sem = graph_step(nc, io, s, XA, QK, (w1, w2, w3), ident, inv_degree, y_dram, xf_dram, tiled)
        with ExitStack() as scope:
            sb = lambda n, s, d=F32: scope.enter_context(nc.sbuf_tensor(n, s, d))
            qT, kT, V = sb("qT", [P, KT, N]), sb("kT", [P, KT, N]), sb("V", [P, NT, D])
            project_phase(nc, io, range(first_sem, last_sem), qT, kT, V, ident, ones_row, y_dram[1], x1_dram, tiled)
            attention_phase(nc, io, qT, kT, V, ident, x1_dram, x2_dram, l2_dram, tiled)
        joined = nc.values_load(has_ones[0:1, 0:1], min_val=0, max_val=N * N,
                                skip_runtime_bounds_check_because="a count of the entries of adj")
        with nc.If(joined != 0):
            relation_phase(nc, io, ident, l2_dram, tiled)
        with ExitStack() as scope:
            sb = lambda n, s, d=F32: scope.enter_context(nc.sbuf_tensor(n, s, d))
            enc = sb("enc", [P, NT, D])
            with ExitStack() as inner:
                sb = lambda n, s, d=F32: inner.enter_context(nc.sbuf_tensor(n, s, d))
                Wh = sb("Wh", [P, NT, HEADS, HID + 1])
                edge = sb("edge", [P, NT, N], BF16)
                dst, dst_low, dst_neg = (sb(n, [P, NT, HEADS]) for n in ("dst", "dst_low", "dst_neg"))
                src_bias = sb("src_bias", [P, HEADS])
                heads_phase(nc, io, Wh, edge, dst, dst_low, dst_neg, src_bias, ident, x2_dram, l2_dram, x3_dram, src_dram, tiled)
                gat_phase(nc, ident, Wh, edge, dst, dst_low, dst_neg, src_bias, enc, src_dram)
            mlp_phase(nc, io, enc, ident, ones_row, x3_dram, out, tiled)


def project_qk_pe(nc, pe, XT, w, ps, q_row, filled, emptied, n, q_copied):
    w1, w2, w3 = w
    KT = w1.shape[1]
    for which in (w3, w1):
        if n:
            pe.wait_ge(emptied, n)
        for k in range(KT):
            mm = nc.tensor.matmul(ps[0:64, :], which[:, k, :], XT[:, k, :], start=(k == 0), stop=(k == KT - 1))
        mm.then_inc(filled, 1)
        n += 1
    pe.wait_ge(emptied, n)
    nc.tensor.matmul(ps[0:64, :], w2[:, :], q_row[:, :], start=True, stop=True).then_inc(filled, 1)
    return n + 1


def project_qk_act(nc, act, ps, q_row, QK, g, filled, emptied, n):
    for dst in (QK[0:64, g * 512:(g + 1) * 512], q_row[:, :], QK[64:128, g * 512:(g + 1) * 512]):
        act.wait_ge(filled, n + 1)
        nc.scalar.copy(dst, ps[0:64, :]).then_inc(emptied, 1)
        n += 1
    return n


def norm_phase(nc, io, H, QK, w, ident, ones_row, inv_degree, ones_seen, has_ones, tiled):
    N, D = io["x"].shape
    NT, KT, T = N // P, D // P, 4
    G = NT // T
    with ExitStack() as scope:
        sb = lambda n, s, d=F32: scope.enter_context(nc.sbuf_tensor("a_" + n, s, d))
        sem = lambda n: scope.enter_context(nc.semaphore("a_" + n))
        xin = sb("xin", [P, NT, D])
        adj_rows = sb("adj_rows", [P, 2, N])
        XT = sb("XT", [P, KT, 512])
        q_row = sb("q_row", [64, 512])
        stats, mv, rstd = sb("stats", [P, T, 6]), sb("mv", [P, T, 2]), sb("rstd", [P, 3, T])
        junk, junk2 = sb("junk", [P, N], BF16), sb("junk2", [P, N], BF16)
        degree, ones_all = sb("degree", [P, NT]), sb("ones_all", [P, 1])
        psT = [scope.enter_context(nc.psum_tensor(f"a_psT{b}", [P, 512], F32)) for b in range(2)]
        psQ = scope.enter_context(nc.psum_tensor("a_psQ", [P, 512], F32))

        x_in = [sem(f"x_in{g}") for g in range(G)]
        first_sem = x_in[0].num
        w_in = sem("w_in")
        adj_in = [sem(f"adj_in{b}") for b in range(2)]
        adj_summed, adj_counted = sem("adj_summed"), sem("adj_counted")
        ones_added, ones_spread = sem("ones_added"), sem("ones_spread")
        id_made, chain_s = sem("id_made"), sem("chain")
        sqrt_asked, sqrt_done, h_ready = sem("sqrt_asked"), sem("sqrt_done"), sem("h_ready")
        t_filled, t_emptied, q_filled, q_emptied = sem("t_filled"), sem("t_emptied"), sem("q_filled"), sem("q_emptied")
        block = scope.enter_context(nc.Block())

        @block.sync
        def _(sp):
            for g in range(G):
                sp.dma_start(xin[:, g * T:(g + 1) * T, :], tiled(io["x"])[:, g * T:(g + 1) * T, :]).then_inc(x_in[g], 16)
            for t, name in zip(w, ("l0_w1", "l0_w2", "l0_w3")):
                src = io[name] if name == "l0_w2" else io[name].rearrange("(k p) a -> p k a", p=P)
                sp.dma_start(t[:], src).then_inc(w_in, 16)
            for i in range(NT):
                if i >= 2:
                    sp.wait_ge(adj_summed, i - 1)
                    sp.wait_ge(adj_counted, i - 1)
                sp.dma_start(adj_rows[:, i % 2, :], io["adj"][i * P:(i + 1) * P, :]).then_inc(adj_in[i % 2], 16)

        @block.gpsimd
        def _(pool):
            make_identity(nc, pool, ident, id_made)
            nc.gpsimd.memset(ones_row[:], 1.0).then_inc(id_made, 1)
            pool.wait_ge(ones_added, 1)
            nc.gpsimd.partition_all_reduce(ones_all[:], ones_seen[:, NT:NT + 1], P,
                                           bass.bass_isa.ReduceOp.add).then_inc(ones_spread, 1)

        @block.vector
        def _(dve):
            chain = Chain(dve, chain_s)
            for g in range(G):
                dve.wait_ge(x_in[g], 16)
                layer_norm_batch(nc, chain, xin[:, g * T:(g + 1) * T, :], H[:, g * T:(g + 1) * T, :], stats, mv, rstd,
                                 sqrt_asked, sqrt_done, g, relu=True)
                dve.sem_inc(h_ready, 1)
            for i in range(NT):
                dve.wait_ge(adj_in[i % 2], 16 * (i // 2 + 1))
                if i:
                    dve.wait_ge(adj_counted, i)
                ins = nc.vector.tensor_scalar(junk2[:, :], adj_rows[:, i % 2, :], 1.0, 0.0, ALU.is_equal, ALU.add,
                                              accum_out=ones_seen[:, i:i + 1])
                ins.then_inc(adj_counted, 1)
            dve.wait_ge(adj_counted, NT)
            nc.vector.tensor_reduce(ones_seen[:, NT:NT + 1], ones_seen[:, 0:NT], AX.X, ALU.add).then_inc(ones_added, 1)
            dve.wait_ge(ones_spread, 1)
            chain(nc.vector.tensor_copy(has_ones[:], ones_all[:]))
            dve.wait_ge(adj_summed, NT)
            chain(nc.vector.tensor_scalar(degree[:, :], degree[:, :], 1.0, 1e-12, ALU.add, ALU.max))
            chain(nc.vector.reciprocal(inv_degree[:, :], degree[:, :]))

        @block.scalar
        def _(act):
            for g in range(G):
                layer_norm_sqrt(nc, act, rstd, sqrt_asked, sqrt_done, g)
            nT = nQ = 0
            for g in range(G):
                for k in range(KT):
                    act.wait_ge(t_filled, nT + 1)
                    if k == 0 and g:
                        act.wait_ge(q_filled, nQ)
                    nc.scalar.copy(XT[:, k, :], psT[nT % 2][:, :]).then_inc(t_emptied, 1)
                    nT += 1
                nQ = project_qk_act(nc, act, psQ, q_row, QK, g, q_filled, q_emptied, nQ)
            for i in range(NT):
                act.wait_ge(adj_in[i % 2], 16 * (i // 2 + 1))
                if i:
                    act.wait_ge(adj_summed, i)
                nc.scalar.activation(junk[:, :], adj_rows[:, i % 2, :], ACT.Copy,
                                     accum_out=degree[:, i:i + 1]).then_inc(adj_summed, 1)

        @block.tensor
        def _(pe):
            pe.wait_ge(id_made, 3)
            pe.wait_ge(w_in, 48)
            nT = nQ = 0
            for g in range(G):
                pe.wait_ge(h_ready, g + 1)
                for k in range(KT):
                    if nT >= 2:
                        pe.wait_ge(t_emptied, nT - 1)
                    for t in range(T):
                        tr = nc.tensor.transpose(psT[nT % 2][:, t * P:(t + 1) * P], H[:, g * T + t, k * P:(k + 1) * P], ident[:, :])
                    tr.then_inc(t_filled, 1)
                    nT += 1
                pe.wait_ge(t_emptied, nT)
                nQ = project_qk_pe(nc, pe, XT, w, psQ, q_row, q_filled, q_emptied, nQ, None)
    return first_sem


def graph_step(nc, io, s, XA, QK, w, ident, inv_degree, y_dram, xf_dram, tiled):
    N, D = io["x"].shape
    NT, KT, T = N // P, D // P, 4
    G, CH = NT // T, N // 512
    last_step = s == 1
    Xa, Xn = XA[s], XA[1 - s]
    Xf = XA[0]
    own = QK[s]
    with ExitStack() as scope:
        sb = lambda n, sh, d=F32: scope.enter_context(nc.sbuf_tensor(f"g{s}_{n}", sh, d))
        sem = lambda n: scope.enter_context(nc.semaphore(f"g{s}_{n}"))
        if last_step:
            Xn = None
            xa_row = QK[0][:, 0:2 * D].rearrange("p (b d) -> p b d", b=2)
            y_before = QK[0][:, 2 * D:4 * D].rearrange("p (b d) -> p b d", b=2)
        prob = sb("prob", [P, 2 * T, N])
        PT = sb("PT", [P, 2, 512])
        PARTS, RING = 4, 5
        PART = NT // PARTS
        adj_T = sb("adj_T", [P, RING, PART, P])
        u1, u2 = sb("u1", [P, KT, D]), sb("u2", [P, KT, D])
        XfT, XaT = sb("XfT", [P, T, KT, P]), sb("XaT", [P, KT, T * P])
        q_tile = sb("q_tile", [64, 2, P])
        y_row = sb("y_row", [P, D])
        xf_row = sb("xf_row", [P, 2, D])
        q_row = y_row[0:64, :]
        junk, junk_act = sb("junk", [P, 2, N], mybir.dt.uint8), sb("junk_act", [P, N], mybir.dt.uint8)
        (neg_trial, goal_2, excess, balance, above_2, lack, reached, factor, n_column) = (
            sb(n, [P, 1]) for n in ("neg_trial", "goal_2", "excess", "balance", "above_2", "lack", "reached", "factor", "n_column"))
        spread, middle = sb("spread", [P, BISECT_STEPS]), sb("middle", [P, BISECT_STEPS])
        neg_max, total, kept, inv_kept = (sb(n, [P, NT]) for n in ("neg_max", "total", "kept", "inv_kept"))
        factors = sb("factors", [P, BISECT_STEPS])
        floor = sb("floor", [P, T])
        trial, mass, goal, step_up = (sb(n, [P, T - 1]) for n in ("trial", "mass", "goal", "step_up"))
        psum = scope.enter_context(nc.psum_tensor(f"g{s}_psum", [P, 2 * N], F32))
        psL = [psum[:, 0:N], psum[:, N:2 * N]]
        psT = [psum[:, N + b * 512:N + (b + 1) * 512] for b in range(2)]
        psS = [psum[:, N + b * 512:N + (b + 1) * 512] for b in range(2, 4)]
        L = lambda i: psL[i % 2 if i < T else 0]

        adj_in, adj_used = [sem(f"adj_in{b}") for b in range(RING)], sem("adj_used")
        u_in, xf_in = sem("u_in"), sem("xf_in")
        yin = [sem(f"y_in{b}") for b in range(2)]
        q_staged = sem("q_staged")
        scores_done, max_done, exp_done, mask_done, inv_done = (sem(n) for n in ("scores_done", "max_done", "exp_done", "mask_done", "inv_done"))
        t_filled, t_emptied, pt_used = sem("t_filled"), sem("t_emptied"), sem("pt_used")
        s_filled, s_emptied = sem("s_filled"), sem("s_emptied")
        y_out, xf_out = sem("y_out"), [sem(f"xf_out{b}") for b in range(2)]
        act_floor, act_chain = sem("act_floor"), sem("act_chain")
        floor_read = sem("floor_read")
        columns_set = sem("columns_set")
        first_sem = adj_in[0].num
        chain_s = sem("chain")
        block = scope.enter_context(nc.Block())
        FIRST_UP = math.exp((-math.log((1 - TOP_P) / N * 0.99) + 1e-3) / 2)
        LEAST = (1 - TOP_P) / N * 0.99
        cuts = [3, 9, 15, BISECT_STEPS]
        ACT_TILE = T - 1
        MORE = 3

        def order():
            for t in range(T):
                yield "scores", t
                yield "exp", t
            for g in range(G + 1):
                for t in range(T):
                    if g:
                        yield "attend", (g - 1) * T + t
                    if g < G:
                        yield "relate", g * T + t
                    if g:
                        yield "turn Xa", (g - 1) * T + t
                    if g + 1 < G:
                        yield "scores", (g + 1) * T + t
                    if g:
                        yield "add", (g - 1) * T + t
                    if g < G:
                        yield "turn Xf", g * T + t
                    if g + 1 < G:
                        yield "exp", (g + 1) * T + t
                if g and not last_step:
                    yield "project", g - 1

        turn = {}
        uses = 0
        for what, i in order():
            if what in ("attend", "relate", "add", "project"):
                turn[what, i] = uses
                uses += 3 if what == "project" else 1

        def store_y(sp, i):
            sp.wait_ge(s_emptied, turn["add", i] + 1)
            sp.dma_start(tiled(y_dram[s])[:, i, :], y_row[:, :]).then_inc(y_out, 16)

        def store_xf(sp, i):
            sp.wait_ge(s_emptied, turn["relate", i] + 1)
            sp.dma_start(tiled(xf_dram)[:, i, :], xf_row[:, i % 2, :]).then_inc(xf_out[i % 2], 16)

        @block.sync
        def _(sp):
            if last_step:
                sp.dma_start(Xf[:, :, :], tiled(xf_dram)).then_inc(xf_in, 16)
            for t, name in ((u1, f"l0_u1_{s}"), (u2, f"l0_u2_{s}")):
                sp.dma_start(t[:], io[name].rearrange("(k p) a -> p k a", p=P)).then_inc(u_in, 16)
            for what, i in order():
                if what == "relate":
                    for part in range(PARTS):
                        n = PARTS * i + part
                        if n >= RING:
                            sp.wait_ge(adj_used, n - RING + 1)
                        sp.dma_start(adj_T[:, n % RING, :, :], io["adj_t"][i, :, part * PART:(part + 1) * PART, :])\
                            .then_inc(adj_in[n % RING], 16)
                    if not last_step and i >= 1:
                        store_xf(sp, i - 1)
                if what == "attend":
                    if last_step:
                        if i >= 2:
                            sp.wait_ge(s_filled, turn["add", i - 2] + 1)
                        sp.dma_start(y_before[:, i % 2, :], tiled(y_dram[0])[:, i, :]).then_inc(yin[i % 2], 16)
                    if i >= 1:
                        store_y(sp, i - 1)
            if not last_step:
                store_xf(sp, NT - 1)
            store_y(sp, NT - 1)
            sp.wait_ge(y_out, 16 * NT)
            if not last_step:
                for b in range(2):
                    sp.wait_ge(xf_out[b], 16 * NT // 2)


        @block.gpsimd
        def _(pool):
            for i in range(NT):
                if i >= 2:
                    pool.wait_ge(scores_done, i - 1)
                nc.gpsimd.tensor_copy(q_tile[:, i % 2, :], own[64:128, i * P:(i + 1) * P]).then_inc(q_staged, 1)

        @block.vector
        def _(dve):
            chain = Chain(dve, chain_s)
            width = -math.log(LEAST) + 1e-3
            up = [math.exp(width / 2 ** (k + 1)) for k in range(BISECT_STEPS)]
            chain.last_of([nc.vector.memset(factors[:, k:k + 1], up[k]) for k in range(BISECT_STEPS)])
            for k in range(BISECT_STEPS):
                reached_by = up[k + 1] if k + 1 < BISECT_STEPS else 1.0 - 2e-6
                missed_by = reached_by / up[k]
                nc.vector.memset(spread[:, k:k + 1], (reached_by - missed_by) / 2)
                nc.vector.memset(middle[:, k:k + 1], (reached_by + missed_by) / 2)
            nc.vector.memset(n_column[:, :], float(N)).then_inc(columns_set, 1)

            def row_max(i):
                dve.wait_ge(scores_done, i + 1)
                nc.vector.tensor_reduce(neg_max[:, i:i + 1], L(i), AX.X, ALU.max, negate=True).then_inc(max_done, 1)

            def bisect(g, k0, k1):
                base, per = chain.n, ACT_TILE + 4
                with dve.Fori(0, (k1 - k0) // MORE) as r:
                    n = [0]

                    def link(ins, wait=True):
                        n[0] += 1
                        ins.then_inc(chain_s, 1)
                        if wait:
                            dve.wait_ge(chain_s, r * (MORE * per) + (base + n[0]))

                    for m in range(MORE):
                        link(nc.vector.tensor_scalar(trial[:, :], floor[:, 0:ACT_TILE], factors[:, bass.ds(r * MORE + (k0 + m), 1)],
                                                     None, ALU.mult))
                        for t in range(ACT_TILE):
                            slot = (g * T + t) % (2 * T)
                            link(nc.vector.scalar_tensor_tensor(
                                out=junk[:, t % 2, :], in0=prob[:, slot, :], scalar=trial[:, t:t + 1],
                                in1=prob[:, slot, :], op0=ALU.is_ge, op1=ALU.mult, accum_out=mass[:, t:t + 1]),
                                 wait=t)
                        link(nc.vector.tensor_tensor(step_up[:, :], mass[:, :], goal[:, :], ALU.is_ge))
                        link(nc.vector.tensor_tensor(step_up[:, :], step_up[:, :], trial[:, :], ALU.mult))
                        link(nc.vector.tensor_tensor(floor[:, 0:ACT_TILE], floor[:, 0:ACT_TILE], step_up[:, :], ALU.max))
                chain.n = base + per * (k1 - k0)

            def mask(i):
                row = prob[:, i % (2 * T), :]
                nc.vector.scalar_tensor_tensor(out=row, in0=row, scalar=floor[:, i % T:i % T + 1], in1=row, op0=ALU.is_ge,
                                               op1=ALU.mult, accum_out=kept[:, i:i + 1]).then_inc(mask_done, 1)
                dve.wait_ge(mask_done, i + 1)
                nc.vector.reciprocal(inv_kept[:, i:i + 1], kept[:, i:i + 1]).then_inc(inv_done, 1)

            for t in range(T):
                row_max(t)
            for g in range(G):
                dve.wait_ge(exp_done, (g + 1) * T)
                both = slice(g * T, g * T + ACT_TILE)
                chain(nc.vector.tensor_scalar(goal[:, :], total[:, both], TOP_P, None, ALU.mult))
                chain(nc.vector.tensor_scalar(floor[:, 0:ACT_TILE], total[:, both], LEAST, None, ALU.mult))
                for t in range(T):
                    bisect(g, cuts[t - 1] if t else 0, cuts[t])
                    if t == T - 1:
                        mask(g * T)
                    if g + 1 < G:
                        row_max((g + 1) * T + t)
                for t in range(1, ACT_TILE):
                    mask(g * T + t)
                dve.wait_ge(act_floor, g + 1)
                chain(nc.vector.tensor_scalar(floor[:, ACT_TILE:T], neg_trial[:, :], -1.0, None, ALU.mult))
                dve.sem_inc(floor_read, 1)
                mask(g * T + ACT_TILE)

        @block.scalar
        def _(act):
            nT = nPT = 0
            chain = Chain(act, act_chain)

            def from_T(dst, scale=None):
                nonlocal nT
                act.wait_ge(t_filled, nT + 1)
                nc.scalar.copy(dst, psT[nT % 2][:, :] if len(dst.shape) == 2 else
                               psT[nT % 2][:, :].rearrange("p (k i) -> p k i", k=KT)).then_inc(t_emptied, 1)
                nT += 1

            def bisect_until(n):
                nonlocal steps_done
                for n in range(steps_done, n):
                    g, k = divmod(n, BISECT_STEPS)
                    i = g * T + ACT_TILE
                    p = prob[:, i % (2 * T), :]
                    if k == 0:
                        if g:
                            act.wait_ge(floor_read, g)
                        else:
                            act.wait_ge(columns_set, 1)
                        act.wait_ge(exp_done, i + 1)
                        chain(nc.scalar.mul(neg_trial[:, :], total[:, i:i + 1], -LEAST * FIRST_UP))
                        chain(nc.scalar.mul(goal_2[:, :], total[:, i:i + 1], 2 * TOP_P))
                    chain(nc.scalar.activation(junk_act[:, :], p, ACT.Relu, bias=neg_trial[:, :], accum_out=excess[:, :]))
                    chain(nc.scalar.activation(junk_act[:, :], p, ACT.Sign, bias=neg_trial[:, :], accum_out=balance[:, :]))
                    chain(nc.scalar.activation(above_2[:, :], balance[:, :], ACT.Identity, bias=n_column[:, :]))
                    chain(nc.scalar.activation(lack[:, :], above_2[:, :], ACT.Identity, scale=neg_trial[:, :], bias=goal_2[:, :]))
                    chain(nc.scalar.activation(reached[:, :], lack[:, :], ACT.Sign, scale=-0.5, bias=excess[:, :]))
                    chain(nc.scalar.activation(factor[:, :], reached[:, :], ACT.Identity, scale=spread[:, k:k + 1],
                                               bias=middle[:, k:k + 1]))
                    last = nc.scalar.activation(neg_trial[:, :], neg_trial[:, :], ACT.Copy, scale=factor[:, :])
                    if k + 1 < BISECT_STEPS:
                        chain(last)
                    else:
                        last.then_inc(act_floor, 1)
                    steps_done = n + 1

            def pace(t, part):
                if period < G:
                    bisect_until(period * BISECT_STEPS + round(BISECT_STEPS * (t + part) / T))

            def empty(what, i, dst, scale=None):
                act.wait_ge(s_filled, turn[what, i] + 1)
                nc.scalar.activation(dst, psS[turn[what, i] % 2][:, :], ACT.Copy,
                                     **({} if scale is None else {"scale": scale})).then_inc(s_emptied, 1)

            steps_done = period = 0
            for what, i in order():
                t = i % T
                if what == "scores":
                    if i >= T:
                        pace(t, 1)
                elif what == "exp":
                    act.wait_ge(max_done, i + 1)
                    if i >= 2 * T:
                        act.wait_ge(pt_used, (i - 2 * T + 1) * CH)
                    nc.scalar.activation(prob[:, i % (2 * T), :], L(i), ACT.Exp, bias=neg_max[:, i:i + 1],
                                         accum_out=total[:, i:i + 1]).then_inc(exp_done, 1)
                elif what == "relate":
                    pace(t, 0.85)
                    if not last_step and i >= 2:
                        act.wait_ge(xf_out[i % 2], 16 * (i // 2))
                    act.wait_ge(s_filled, turn[what, i] + 1)
                    empty(what, i, xf_row[:, i % 2, :], inv_degree[:, i:i + 1])
                elif what == "turn Xf":
                    if i >= T:
                        act.wait_ge(s_filled, turn["add", i - T] + 1)
                    from_T(XfT[:, t, :, :])
                    pace(t, 1)
                    if t == T - 1:
                        period += 1
                elif what == "attend":
                    for c in range(CH):
                        if nPT >= 2:
                            act.wait_ge(pt_used, nPT - 1)
                        from_T(PT[:, nPT % 2, :])
                        nPT += 1
                        if c % 2:
                            pace(t, 0.12 * c)
                    act.wait_ge(inv_done, i + 1)
                    empty(what, i, xa_row[:, i % 2, :] if last_step else Xn[:, i, :], inv_kept[:, i:i + 1])
                elif what == "turn Xa":
                    if t == 0 and i and not last_step:
                        act.wait_ge(s_filled, turn["project", i // T - 1] + 3)
                    elif last_step and i >= T:
                        act.wait_ge(s_filled, turn["add", i - T] + 1)
                    from_T(XaT[:, :, t * P:(t + 1) * P])
                elif what == "add":
                    if i:
                        act.wait_ge(y_out, 16 * i)
                    empty(what, i, y_row[:, :])
                elif what == "project":
                    act.wait_ge(y_out, 16 * T * (i + 1))
                    n = turn[what, i]
                    for m, dst in enumerate((QK[1][0:64, i * 512:(i + 1) * 512], q_row, QK[1][64:128, i * 512:(i + 1) * 512])):
                        act.wait_ge(s_filled, n + m + 1)
                        nc.scalar.copy(dst, psS[(n + m) % 2][0:64, :]).then_inc(s_emptied, 1)

        @block.tensor
        def _(pe):
            nT = nPT = 0

            def to_T(srcs):
                nonlocal nT
                if nT >= 2:
                    pe.wait_ge(t_emptied, nT - 1)
                for n, src in enumerate(srcs):
                    tr = nc.tensor.transpose(psT[nT % 2][:, n * P:(n + 1) * P], src, ident[:, :])
                tr.then_inc(t_filled, 1)
                nT += 1

            def bank(what, i, more=0):
                n = turn[what, i] + more
                if n >= 2:
                    pe.wait_ge(s_emptied, n - 1)
                return psS[n % 2]

            for what, i in order():
                t = i % T
                if what == "relate" and i == 0:
                    pe.wait_ge(exp_done, T)
                if what == "scores":
                    pe.wait_ge(q_staged, i + 1)
                    if i >= 2:
                        pe.wait_ge(exp_done, i - 1 if i < T else i)
                    for c in range(CH):
                        mm = nc.tensor.matmul(L(i)[:, c * 512:(c + 1) * 512], q_tile[:, i % 2, :],
                                              own[0:64, c * 512:(c + 1) * 512], start=True, stop=True)
                    mm.then_inc(scores_done, 1)
                elif what == "relate":
                    if i == 0:
                        if last_step:
                            pe.wait_ge(xf_in, 16)
                        pe.wait_ge(u_in, 32)
                    ps = bank(what, i)
                    nc.tensor.matmul(ps[:, :], ident[:, :], Xf[:, i, :], start=True, stop=False)
                    for part in range(PARTS):
                        n = PARTS * i + part
                        pe.wait_ge(adj_in[n % RING], 16 * (n // RING + 1))
                        for jj in range(PART):
                            j = part * PART + jj
                            mm = nc.tensor.matmul(ps[:, :], adj_T[:, n % RING, jj, :], Xf[:, j, :],
                                                  start=False, stop=(j == NT - 1))
                        if part < PARTS - 1:
                            mm.then_inc(adj_used, 1)
                    mm.then_inc(s_filled, 1)
                elif what == "turn Xf":
                    pe.wait_ge(s_emptied, turn["relate", i] + 1)
                    pe.sem_inc(adj_used, 1)
                    to_T([xf_row[:, i % 2, k * P:(k + 1) * P] for k in range(KT)])
                elif what == "attend":
                    pe.wait_ge(mask_done, i + 1)

                    def transpose_part(c):
                        to_T([prob[:, i % (2 * T), (4 * c + n) * P:(4 * c + n + 1) * P] for n in range(4)])

                    transpose_part(0)
                    for c in range(CH):
                        if c + 1 < CH:
                            transpose_part(c + 1)
                        pe.wait_ge(t_emptied, nT - (1 if c + 1 < CH else 0))
                        if c == 0:
                            ps = bank(what, i)
                        for n in range(4):
                            j = 4 * c + n
                            mm = nc.tensor.matmul(ps[:, :], PT[:, nPT % 2, n * P:(n + 1) * P], Xa[:, j, :],
                                                  start=(j == 0), stop=(j == NT - 1))
                        if c + 1 < CH:
                            mm.then_inc(pt_used, 1)
                        nPT += 1
                    mm.then_inc(s_filled, 1)
                    pe.wait_ge(s_filled, turn[what, i] + 1)
                    pe.sem_inc(pt_used, 1)
                elif what == "turn Xa":
                    pe.wait_ge(s_emptied, turn["attend", i] + 1)
                    row = xa_row[:, i % 2, :] if last_step else Xn[:, i, :]
                    to_T([row[:, k * P:(k + 1) * P] for k in range(KT)])
                    xa_turned = nT
                elif what == "add":
                    if last_step:
                        pe.wait_ge(yin[i % 2], 16 * (i // 2 + 1))
                    before = y_before[:, i % 2, :] if last_step else Xf[:, i, :]
                    ps = bank(what, i)
                    nc.tensor.matmul(ps[:, :], ident[:, :], before, start=True, stop=False)
                    for k in range(KT):
                        nc.tensor.matmul(ps[:, :], XfT[:, t, k, :], u1[:, k, :], start=False, stop=False)
                    pe.wait_ge(t_emptied, xa_turned)
                    for k in range(KT):
                        mm = nc.tensor.matmul(ps[:, :], XaT[:, k, t * P:(t + 1) * P], u2[:, k, :],
                                              start=False, stop=(k == KT - 1))
                    mm.then_inc(s_filled, 1)
                elif what == "project":
                    for m, which in enumerate((w[2], w[0])):
                        ps = bank(what, i, m)
                        for k in range(KT):
                            mm = nc.tensor.matmul(ps[0:64, :], which[:, k, :], XaT[:, k, :], start=(k == 0), stop=(k == KT - 1))
                        mm.then_inc(s_filled, 1)
                    ps = bank(what, i, 2)
                    pe.wait_ge(s_emptied, turn[what, i] + 2)
                    nc.tensor.matmul(ps[0:64, :], w[1][:, :], q_row, start=True, stop=True).then_inc(s_filled, 1)
    return first_sem


def project_phase(nc, io, used_sems, qT, kT, V, ident, ones_row, y_dram, x1_dram, tiled):
    N, D = io["x"].shape
    NT, KT, T = N // P, D // P, 4
    G = NT // T
    with ExitStack() as scope:
        sb = lambda n, s, d=F32: scope.enter_context(nc.sbuf_tensor("p_" + n, s, d))
        sem = lambda n: scope.enter_context(nc.semaphore("p_" + n))
        wq, wk, wv = (sb(n, [P, KT, D]) for n in ("wq", "wk", "wv"))
        bq, bk, bv = sb("bq", [P, KT]), sb("bk", [P, KT]), sb("bv", [1, D])
        gamma, beta = sb("gamma", [P, D]), sb("beta", [P, D])
        rows, x_rows, h = sb("rows", [P, T, D]), sb("x_rows", [P, T, D]), sb("h", [P, 2, T, D])
        HT = sb("HT", [P, KT, T * P])
        stats, mv, rstd = sb("stats", [P, T, 6]), sb("mv", [P, T, 2]), sb("rstd", [P, 3, T])
        psT = [scope.enter_context(nc.psum_tensor(f"p_psT{b}", [P, 512], F32)) for b in range(2)]
        psM = [scope.enter_context(nc.psum_tensor(f"p_psM{b}", [P, 512], F32)) for b in range(4)]
        w_in, bias_in, y_in, x_in, x1_out = (sem(n) for n in ("w_in", "bias_in", "y_in", "x_in", "x1_out"))
        y_free, x1_ready, h_ready = sem("y_free"), sem("x1_ready"), sem("h_ready")
        sqrt_asked, sqrt_done, chain_s = sem("sqrt_asked"), sem("sqrt_done"), sem("chain")
        t_filled, t_emptied, m_filled, m_emptied = (sem(n) for n in ("t_filled", "t_emptied", "m_filled", "m_emptied"))
        products = 3 * T
        block = scope.enter_context(nc.Block())

        @block.sync
        def _(sp):
            sp.dma_start(gamma[:], io["l0_gamma"].partition_broadcast(P)).then_inc(bias_in, 16)
            sp.dma_start(beta[:], io["l0_beta"].partition_broadcast(P)).then_inc(bias_in, 16)
            for g in range(G):
                both = slice(g * T, (g + 1) * T)
                if g:
                    sp.wait_ge(y_free, g)
                sp.dma_start(rows[:], tiled(y_dram)[:, both, :]).then_inc(y_in, 16)
                if g:
                    sp.wait_ge(x1_ready, g)
                    sp.dma_start(tiled(x1_dram)[:, (g - 1) * T:g * T, :], x_rows[:]).then_inc(x1_out, 16)
                    sp.wait_ge(x1_out, 16 * g)
                    sp.wait_ge(h_ready, g)
                sp.dma_start(x_rows[:], tiled(io["x"])[:, both, :]).then_inc(x_in, 16)
                if g == 0:
                    for t, name in ((wq, "l1_wq"), (wk, "l1_wk"), (wv, "l1_wv")):
                        sp.dma_start(t[:], io[name].rearrange("(k p) n -> p k n", p=P)).then_inc(w_in, 16)
                    sp.dma_start(bq[:], io["l1_bq"]).then_inc(bias_in, 16)
                    sp.dma_start(bk[:], io["l1_bk"]).then_inc(bias_in, 16)
                    sp.dma_start(bv[:], io["l1_bv"].partition_broadcast(1)).then_inc(bias_in, 16)
            sp.wait_ge(x1_ready, G)
            sp.dma_start(tiled(x1_dram)[:, (G - 1) * T:, :], x_rows[:]).then_inc(x1_out, 16)
            sp.wait_ge(x1_out, 16 * G)

        @block.gpsimd
        def _(pool):
            pool.sem_clear(used_sems)

        @block.vector
        def _(dve):
            chain = Chain(dve, chain_s)
            turn = 0
            for g in range(G):
                dve.wait_ge(y_in, 16 * (g + 1))
                layer_norm_batch(nc, chain, rows, rows, stats, mv, rstd, sqrt_asked, sqrt_done, turn, relu=False)
                turn += 1
                if g == 0:
                    dve.wait_ge(bias_in, 80)
                chain.last_of([nc.vector.tensor_tensor(rows[:, t, :], rows[:, t, :], gamma[:], ALU.mult) for t in range(T)])
                chain.last_of([nc.vector.tensor_tensor(rows[:, t, :], rows[:, t, :], beta[:], ALU.add) for t in range(T)])
                dve.wait_ge(x_in, 16 * (g + 1))
                nc.vector.tensor_tensor(x_rows[:], x_rows[:], rows[:], ALU.add).then_inc(x1_ready, 1)
                dve.wait_ge(x1_ready, g + 1)
                dve.sem_inc(y_free, 1)
                if g >= 2:
                    dve.wait_ge(t_filled, (g - 1) * KT)
                layer_norm_batch(nc, chain, x_rows, h[:, g % 2, :, :], stats, mv, rstd, sqrt_asked, sqrt_done, turn, relu=True)
                turn += 1
                dve.sem_inc(h_ready, 1)

        @block.scalar
        def _(act):
            n = 0

            def move(g):
                nonlocal n
                for k in range(KT):
                    act.wait_ge(t_filled, g * KT + k + 1)
                    if g and k == 0:
                        act.wait_ge(m_filled, g * products)
                    nc.scalar.copy(HT[:, k, :], psT[k % 2][:, :]).then_inc(t_emptied, 1)
                if g == 0:
                    act.wait_ge(bias_in, 80)
                for dst, bias in ((qT, bq), (kT, bk)):
                    for m in range(KT):
                        act.wait_ge(m_filled, n + 1)
                        nc.scalar.activation(dst[:, m, g * 512:(g + 1) * 512], psM[n % 4][:, :], ACT.Identity,
                                             bias=bias[:, m:m + 1]).then_inc(m_emptied, 1)
                        n += 1
                for t in range(T):
                    act.wait_ge(m_filled, n + 1)
                    nc.scalar.copy(V[:, g * T + t, :], psM[n % 4][:, :]).then_inc(m_emptied, 1)
                    n += 1

            for g in range(G):
                layer_norm_sqrt(nc, act, rstd, sqrt_asked, sqrt_done, 2 * g)
                layer_norm_sqrt(nc, act, rstd, sqrt_asked, sqrt_done, 2 * g + 1)
                if g:
                    move(g - 1)
            move(G - 1)

        @block.tensor
        def _(pe):
            n = 0

            def bank():
                if n >= 4:
                    pe.wait_ge(m_emptied, n - 3)
                return psM[n % 4]

            for g in range(G):
                pe.wait_ge(h_ready, g + 1)
                for k in range(KT):
                    if g * KT + k >= 2:
                        pe.wait_ge(t_emptied, g * KT + k - 1)
                    for t in range(T):
                        tr = nc.tensor.transpose(psT[k % 2][:, t * P:(t + 1) * P], h[:, g % 2, t, k * P:(k + 1) * P], ident[:])
                    tr.then_inc(t_filled, 1)
                pe.wait_ge(t_emptied, (g + 1) * KT)
                if g == 0:
                    pe.wait_ge(w_in, 48)
                    pe.wait_ge(bias_in, 80)
                for weight in (wq, wk):
                    for m in range(KT):
                        ps = bank()
                        for k in range(KT):
                            mm = nc.tensor.matmul(ps[:, :], weight[:, k, m * P:(m + 1) * P], HT[:, k, :], start=(k == 0), stop=(k == KT - 1))
                        mm.then_inc(m_filled, 1)
                        n += 1
                for t in range(T):
                    ps = bank()
                    nc.tensor.matmul(ps[:, :], ones_row[:, :], bv[:, :], start=True, stop=False)
                    for k in range(KT):
                        mm = nc.tensor.matmul(ps[:, :], HT[:, k, t * P:(t + 1) * P], wv[:, k, :], start=False, stop=(k == KT - 1))
                    mm.then_inc(m_filled, 1)
                    n += 1


def attention_phase(nc, io, qT, kT, V, ident, x1_dram, x2_dram, l2_dram, tiled):
    N, D = io["x"].shape
    NT, KT, T = N // P, D // P, 4
    CH = N // 512
    scale = 1.0 / math.sqrt(D)
    with ExitStack() as scope:
        sb = lambda n, s, d=F32: scope.enter_context(nc.sbuf_tensor("t_" + n, s, d))
        sem = lambda n: scope.enter_context(nc.semaphore("t_" + n))
        adj_rows, score, void = sb("adj_rows", [P, 2, N]), sb("score", [P, 2, N]), sb("void", [P, N])
        PT = sb("PT", [P, 4, 512])
        x_rows, h = sb("x_rows", [P, T, D]), sb("h", [P, T, D])
        o_row = sb("o_row", [P, 2, D])
        stats, mv, rstd = sb("stats", [P, T, 6]), sb("mv", [P, T, 2]), sb("rstd", [P, 3, T])
        row_max, neg_max, total, inv_total = (sb(n, [P, NT]) for n in ("row_max", "neg_max", "total", "inv_total"))
        psL = scope.enter_context(nc.psum_tensor("t_psL", [P, N], F32))
        psT = [scope.enter_context(nc.psum_tensor(f"t_psT{b}", [P, 512], F32)) for b in range(2)]
        psO = scope.enter_context(nc.psum_tensor("t_psO", [P, 512], F32))
        adj_in, x1_in, x2_out = [sem(f"adj_in{b}") for b in range(2)], sem("x1_in"), sem("x2_out")
        scores_done, scaled, max_done, exp_done, inv_done = (sem(n) for n in ("scores_done", "scaled", "max_done", "exp_done", "inv_done"))
        t_filled, t_emptied, pt_used, o_emptied, x2_ready, h_ready = (sem(n) for n in ("t_filled", "t_emptied", "pt_used", "o_emptied", "x2_ready", "h_ready"))
        sqrt_asked, sqrt_done, chain_s = sem("sqrt_asked"), sem("sqrt_done"), sem("chain")
        block = scope.enter_context(nc.Block())

        @block.sync
        def _(sp):
            def store(g):
                sp.wait_ge(h_ready, g + 1)
                sp.dma_start(tiled(x2_dram)[:, g * T:(g + 1) * T, :], x_rows[:]).then_inc(x2_out, 16)
                sp.dma_start(tiled(l2_dram)[:, g * T:(g + 1) * T, :], h[:]).then_inc(x2_out, 16)

            for i in range(NT):
                if i >= 2:
                    sp.wait_ge(scaled, i - 1)
                sp.dma_start(adj_rows[:, i % 2, :], io["adj"][i * P:(i + 1) * P, :]).then_inc(adj_in[i % 2], 16)
                if i % T == 2:
                    g = i // T
                    if g:
                        store(g - 1)
                        sp.wait_ge(x2_out, 32 * g)
                    sp.dma_start(x_rows[:], tiled(x1_dram)[:, g * T:(g + 1) * T, :]).then_inc(x1_in, 16)
            store(NT // T - 1)
            sp.wait_ge(x2_out, 32 * NT // T)

        @block.vector
        def _(dve):
            chain = Chain(dve, chain_s)
            for i in range(NT + 1):
                if i < NT:
                    s_i = score[:, i % 2, :]
                    dve.wait_ge(scores_done, i + 1)
                    dve.wait_ge(adj_in[i % 2], 16 * (i // 2 + 1))
                    if i >= 2:
                        dve.wait_ge(t_filled, (i - 1) * CH)
                    nc.vector.scalar_tensor_tensor(out=s_i, in0=psL[:, :], scalar=scale, in1=adj_rows[:, i % 2, :],
                                                   op0=ALU.mult, op1=ALU.mult).then_inc(scaled, 1)
                    dve.wait_ge(scaled, i + 1)
                    chain(nc.vector.tensor_scalar(void[:, :], s_i, 0.0, -10000.0, ALU.is_equal, ALU.mult))
                    chain(nc.vector.tensor_tensor_reduce(out=s_i, in0=s_i, in1=void[:, :], scale=1.0, scalar=-3.0e38,
                                                         op0=ALU.add, op1=ALU.max, accum_out=row_max[:, i:i + 1]))
                    nc.vector.tensor_scalar(neg_max[:, i:i + 1], row_max[:, i:i + 1], -1.0, None, ALU.mult).then_inc(max_done, 1)
                if i:
                    j = i - 1
                    dve.wait_ge(exp_done, j + 1)
                    nc.vector.reciprocal(inv_total[:, j:j + 1], total[:, j:j + 1]).then_inc(inv_done, 1)
                if i >= 2 or i == NT:
                    for j in ([i - 2] if i < NT else [i - 2, i - 1]):
                        g, t = j // T, j % T
                        if t == 0:
                            dve.wait_ge(x1_in, 16 * (g + 1))
                        dve.wait_ge(o_emptied, j + 1)
                        nc.vector.tensor_tensor(x_rows[:, t, :], x_rows[:, t, :], o_row[:, j % 2, :], ALU.add).then_inc(x2_ready, 1)
                        if t == T - 1:
                            dve.wait_ge(x2_ready, j + 1)
                            if g:
                                dve.wait_ge(x2_out, 32 * g)
                            layer_norm_batch(nc, chain, x_rows, h, stats, mv, rstd, sqrt_asked, sqrt_done, g, relu=True)
                            dve.sem_inc(h_ready, 1)

        @block.scalar
        def _(act):
            nT = 0
            for i in range(NT + 1):
                if i:
                    j = i - 1
                    for c in range(CH):
                        if nT >= 4:
                            act.wait_ge(pt_used, nT - 3)
                        act.wait_ge(t_filled, nT + 1)
                        nc.scalar.copy(PT[:, nT % 4, :], psT[nT % 2][:, :]).then_inc(t_emptied, 1)
                        nT += 1
                if i < NT:
                    act.wait_ge(max_done, i + 1)
                    s_i = score[:, i % 2, :]
                    nc.scalar.activation(s_i, s_i, ACT.Exp, bias=neg_max[:, i:i + 1], accum_out=total[:, i:i + 1]).then_inc(exp_done, 1)
                if i:
                    act.wait_ge(pt_used, nT)
                    act.wait_ge(inv_done, j + 1)
                    if j >= 2:
                        act.wait_ge(x2_ready, j - 1)
                    nc.scalar.activation(o_row[:, j % 2, :], psO[:, :], ACT.Relu, scale=inv_total[:, j:j + 1]).then_inc(o_emptied, 1)
                if i >= 2 and (i - 2) % T == T - 1:
                    layer_norm_sqrt(nc, act, rstd, sqrt_asked, sqrt_done, (i - 2) // T)
            layer_norm_sqrt(nc, act, rstd, sqrt_asked, sqrt_done, NT // T - 1)

        @block.tensor
        def _(pe):
            nT = nPT = 0

            def transpose_part(i, c):
                nonlocal nT
                if nT >= 2:
                    pe.wait_ge(t_emptied, nT - 1)
                for n in range(4):
                    tr = nc.tensor.transpose(psT[nT % 2][:, n * P:(n + 1) * P],
                                             score[:, i % 2, (4 * c + n) * P:(4 * c + n + 1) * P], ident[:])
                tr.then_inc(t_filled, 1)
                nT += 1

            for i in range(NT + 1):
                if i < NT:
                    if i:
                        pe.wait_ge(scaled, i)
                    for c in range(CH):
                        for k in range(KT):
                            mm = nc.tensor.matmul(psL[:, c * 512:(c + 1) * 512], qT[:, k, i * P:(i + 1) * P],
                                                  kT[:, k, c * 512:(c + 1) * 512], start=(k == 0), stop=(k == KT - 1))
                    mm.then_inc(scores_done, 1)
                if i:
                    j = i - 1
                    pe.wait_ge(exp_done, j + 1)
                    transpose_part(j, 0)
                    for c in range(CH):
                        if c + 1 < CH:
                            transpose_part(j, c + 1)
                        pe.wait_ge(t_emptied, nT - (1 if c + 1 < CH else 0))
                        if c == 0 and j:
                            pe.wait_ge(o_emptied, j)
                        for n in range(4):
                            m = 4 * c + n
                            mm = nc.tensor.matmul(psO[:, :], PT[:, nPT % 4, n * P:(n + 1) * P], V[:, m, :],
                                                  start=(m == 0), stop=(m == NT - 1))
                        mm.then_inc(pt_used, 1)
                        nPT += 1


VOID = -1.0e30


def relation_phase(nc, io, ident, l2_dram, tiled):
    N, D = io["x"].shape
    NT, KT, T = N // P, D // P, 4
    G, CH = NT // T, N // 512
    E_ROWS, E_COLS = io["l2_pairs"].shape[0:2]
    HEADS, HID = io["l3_a1"].shape
    with ExitStack() as scope:
        sb = lambda n, s, d=F32: scope.enter_context(nc.sbuf_tensor("r_" + n, s, d))
        sem = lambda n: scope.enter_context(nc.semaphore("r_" + n))
        h_rows = sb("h_rows", [P, NT, D])
        qT, kT = sb("qT", [P, KT, N]), sb("kT", [P, KT, N])
        pairs_in = sb("pairs_in", [E_ROWS, E_COLS, 2], I32)
        pairs = sb("pairs", [E_ROWS, 2, E_COLS])
        tile_ids, row_id = sb("tile_ids", [P, P]), sb("row_id", [P, 1])
        column_id, none = sb("column_id", [P, N]), sb("none", [E_ROWS, 512], BF16)
        q_head = sb("q_head", [P, HEADS, P])
        with ExitStack() as inner:
            sbi = lambda n, s, d=F32: inner.enter_context(nc.sbuf_tensor("r_" + n, s, d))
            wq, wk, bq, bk = sbi("wq", [P, KT, D]), sbi("wk", [P, KT, D]), sbi("bq", [P, KT]), sbi("bk", [P, KT])
            HT = sbi("HT", [P, KT, T * P])
            psT = [inner.enter_context(nc.psum_tensor(f"r_psT{b}", [P, 512], F32)) for b in range(2)]
            psM = [inner.enter_context(nc.psum_tensor(f"r_psM{b}", [P, 512], F32)) for b in range(2)]
            loaded, t_filled, t_emptied = (inner.enter_context(nc.semaphore("r_" + n)) for n in ("loaded", "t_filled", "t_emptied"))
            m_filled, m_emptied = (inner.enter_context(nc.semaphore("r_" + n)) for n in ("m_filled", "m_emptied"))
            block = inner.enter_context(nc.Block())

            @block.sync
            def _(sp):
                sp.dma_start(h_rows[:], tiled(l2_dram)).then_inc(loaded, 16)
                for t, name in ((wq, "l2_wq"), (wk, "l2_wk")):
                    sp.dma_start(t[:], io[name].rearrange("(k p) n -> p k n", p=P)).then_inc(loaded, 16)
                for t, name in ((bq, "l2_bq"), (bk, "l2_bk"), (pairs_in, "l2_pairs")):
                    sp.dma_start(t[:], io[name]).then_inc(loaded, 16)

            @block.gpsimd
            def _(pool):
                for ids, step, rows in ((column_id, [1, N], 0), (tile_ids, [1, P], 0), (row_id, [1, 1], 1)):
                    nc.gpsimd.iota(ids[:], [step], base=0 if ids is column_id else -P, channel_multiplier=rows,
                                   allow_small_or_imprecise_dtypes=True)
                nc.gpsimd.memset(none[:], 0.0)
                nc.gpsimd.memset(q_head[:], 0.0)

            @block.vector
            def _(dve):
                dve.wait_ge(loaded, 96)
                nc.vector.tensor_copy(pairs[:].rearrange("p s e -> p e s"), pairs_in[:])

            @block.tensor
            def _(pe):
                pe.wait_ge(loaded, 96)
                nT = nM = 0
                for g in range(G):
                    if g:
                        pe.wait_ge(t_emptied, nT)
                    for k in range(KT):
                        if nT >= 2:
                            pe.wait_ge(t_emptied, nT - 1)
                        for t in range(T):
                            tr = nc.tensor.transpose(psT[nT % 2][:, t * P:(t + 1) * P], h_rows[:, g * T + t, k * P:(k + 1) * P], ident[:])
                        tr.then_inc(t_filled, 1)
                        nT += 1
                    pe.wait_ge(t_emptied, nT)
                    for weight in (wq, wk):
                        for m in range(KT):
                            if nM >= 2:
                                pe.wait_ge(m_emptied, nM - 1)
                            for k in range(KT):
                                mm = nc.tensor.matmul(psM[nM % 2][:, :], weight[:, k, m * P:(m + 1) * P], HT[:, k, :],
                                                      start=(k == 0), stop=(k == KT - 1))
                            mm.then_inc(m_filled, 1)
                            nM += 1

            @block.scalar
            def _(act):
                nT = nM = 0
                act.wait_ge(loaded, 96)
                for g in range(G):
                    for k in range(KT):
                        act.wait_ge(t_filled, nT + 1)
                        if g and k == 0:
                            act.wait_ge(m_filled, nM)
                        nc.scalar.copy(HT[:, k, :], psT[nT % 2][:, :]).then_inc(t_emptied, 1)
                        nT += 1
                    for dst, bias in ((qT, bq), (kT, bk)):
                        for m in range(KT):
                            act.wait_ge(m_filled, nM + 1)
                            nc.scalar.activation(dst[:, m, g * 512:(g + 1) * 512], psM[nM % 2][:, :], ACT.Identity,
                                                 bias=bias[:, m:m + 1]).then_inc(m_emptied, 1)
                            nM += 1

        adj_row, score, agg = (sb(n, [P, N]) for n in ("adj_row", "score", "agg"))
        own, listed, base = (sb(n, [P, N]) for n in ("own", "listed", "base"))
        hot_sub, hot_obj = sb("hot_sub", [E_ROWS, P], BF16), sb("hot_obj", [E_ROWS, N], BF16)
        agg_T, out_row = sb("agg_T", [P, NT, P]), sb("out_row", [P, D])
        neg_max, total, weight = sb("neg_max", [P, 1]), sb("total", [P, 1]), sb("weight", [P, 1])
        psL = scope.enter_context(nc.psum_tensor("r_psL", [P, N], F32))
        psT = [scope.enter_context(nc.psum_tensor(f"r_psA{b}", [P, 512], F32)) for b in range(2)]
        psO = scope.enter_context(nc.psum_tensor("r_psO", [P, 512], F32))
        chain_s = sem("chain")
        turn_open, adj_loaded, stored = sem("turn_open"), sem("adj_loaded"), sem("stored")
        hot_ready, hot_used, counted = sem("hot_ready"), sem("hot_used"), sem("counted")
        q_staged, base_ready, scores_done, max_done, exp_done, head_added = (
            sem(n) for n in ("q_staged", "base_ready", "scores_done", "max_done", "exp_done", "head_added"))
        t_filled, t_emptied, o_filled, o_emptied = (sem(n) for n in ("u_filled", "u_emptied", "o_filled", "o_emptied"))
        block = scope.enter_context(nc.Block())

        @block.sync
        def _(sp):
            sp.sem_inc(turn_open, 1)
            with sp.Fori(0, NT) as i:
                sp.dma_start(adj_row[:], io["adj"][bass.ds(i * P, P), :]).then_inc(adj_loaded, 16)
                sp.wait_ge(o_emptied, i + 1)
                sp.dma_start(l2_dram[bass.ds(i * P, P), :], out_row[:]).then_inc(stored, 16)
                sp.wait_ge(stored, i * 16 + 16)
                sp.sem_inc(turn_open, 1)

        @block.gpsimd
        def _(pool):
            with pool.Fori(0, NT) as i:
                pool.wait_ge(turn_open, i + 1)
                for odd in range(2):
                    rows = slice(odd * HID, (odd + 1) * HID)
                    nc.gpsimd.tensor_copy(q_head[rows, odd::2, :], qT[rows, :, bass.ds(i * P, P)]).then_inc(q_staged, 1)

        @block.vector
        def _(dve):
            steps = 2 + 7 + 4 * HEADS + 1
            with dve.Fori(0, NT) as i:
                n = [0]

                def link(ins):
                    n[0] += 1
                    ins.then_inc(chain_s, 1)
                    dve.wait_ge(chain_s, i * steps + n[0])

                dve.wait_ge(turn_open, i + 1)
                link(nc.vector.tensor_scalar(tile_ids[:], tile_ids[:], float(P), None, ALU.add))
                link(nc.vector.tensor_scalar(row_id[:], row_id[:], float(P), None, ALU.add))
                n[0] += 1
                nc.vector.memset(agg[:], 0.0).then_inc(chain_s, 1)
                with dve.Fori(0, E_COLS) as e:
                    dve.wait_ge(hot_used, i * E_COLS + e + 1)
                    nc.vector.tensor_scalar(hot_sub[:], tile_ids[0:E_ROWS, :], pairs[:, 0, bass.ds(e, 1)], None,
                                            ALU.is_equal).then_inc(hot_ready, 1)
                    nc.vector.tensor_scalar(hot_obj[:], column_id[0:E_ROWS, :], pairs[:, 1, bass.ds(e, 1)], None,
                                            ALU.is_equal).then_inc(hot_ready, 1)
                dve.wait_ge(counted, i + 1)
                link(nc.vector.tensor_scalar(own[:], column_id[:], row_id[:], None, ALU.is_equal))
                dve.wait_ge(adj_loaded, i * 16 + 16)
                link(nc.vector.tensor_scalar(adj_row[:], adj_row[:], 1.0, None, ALU.is_equal))
                link(nc.vector.scalar_tensor_tensor(out=listed[:], in0=psL[:], scalar=0.0, in1=adj_row[:],
                                                    op0=ALU.is_gt, op1=ALU.mult))
                link(nc.vector.scalar_tensor_tensor(out=listed[:], in0=own[:], scalar=0.0, in1=listed[:],
                                                    op0=ALU.is_equal, op1=ALU.mult))
                link(nc.vector.tensor_tensor(base[:], adj_row[:], own[:], ALU.max))
                link(nc.vector.tensor_scalar(base[:], base[:], 1.0, -VOID, ALU.subtract, ALU.mult))
                link(nc.vector.scalar_tensor_tensor(out=base[:], in0=own[:], scalar=1e-7, in1=base[:],
                                                    op0=ALU.mult, op1=ALU.add))
                dve.sem_inc(base_ready, 1)
                for h in range(HEADS):
                    dve.wait_ge(scores_done, i * HEADS + (h + 1))
                    link(nc.vector.scalar_tensor_tensor(out=score[:], in0=psL[:], scalar=1.0 / math.sqrt(HID), in1=listed[:],
                                                        op0=ALU.mult, op1=ALU.mult))
                    link(nc.vector.tensor_tensor(score[:], score[:], base[:], ALU.add))
                    nc.vector.tensor_reduce(neg_max[:], score[:], AX.X, ALU.max, negate=True).then_inc(max_done, 1)
                    dve.wait_ge(exp_done, i * HEADS + (h + 1))
                    link(nc.vector.tensor_scalar(total[:], total[:], float(HEADS), None, ALU.mult))
                    link(nc.vector.reciprocal(weight[:], total[:]))
                    nc.vector.scalar_tensor_tensor(out=agg[:], in0=score[:], scalar=weight[:], in1=agg[:],
                                                   op0=ALU.mult, op1=ALU.add).then_inc(head_added, 1)
                    dve.wait_ge(head_added, i * HEADS + (h + 1))

        @block.scalar
        def _(act):
            with act.Fori(0, NT) as i:
                for h in range(HEADS):
                    act.wait_ge(max_done, i * HEADS + (h + 1))
                    nc.scalar.activation(score[:], score[:], ACT.Exp, bias=neg_max[:], accum_out=total[:]).then_inc(exp_done, 1)
                for c in range(CH):
                    act.wait_ge(t_filled, i * CH + (c + 1))
                    nc.scalar.copy(agg_T[:, 4 * c:4 * c + 4, :], psT[c % 2][:, :].rearrange("p (n r) -> p n r", n=4)).then_inc(t_emptied, 1)
                act.wait_ge(o_filled, i + 1)
                nc.scalar.copy(out_row[:], psO[:]).then_inc(o_emptied, 1)

        @block.tensor
        def _(pe):
            pe.sem_inc(hot_used, 1)

            def add_nothing(start, stop):
                for c in range(CH):
                    mm = nc.tensor.matmul(psL[:, c * 512:(c + 1) * 512], none[:, 0:P], none[:], start=start, stop=stop)
                return mm

            with pe.Fori(0, NT) as i:
                pe.wait_ge(turn_open, i + 1)
                add_nothing(True, False)
                with pe.Fori(0, E_COLS) as e:
                    pe.wait_ge(hot_ready, i * (2 * E_COLS) + e * 2 + 2)
                    for c in range(CH):
                        mm = nc.tensor.matmul(psL[:, c * 512:(c + 1) * 512], hot_sub[:], hot_obj[:, c * 512:(c + 1) * 512],
                                              start=False, stop=False)
                    mm.then_inc(hot_used, 1)
                add_nothing(False, True).then_inc(counted, 1)
                pe.wait_ge(q_staged, i * 2 + 2)
                pe.wait_ge(base_ready, i + 1)
                for h in range(HEADS):
                    if h:
                        pe.wait_ge(max_done, i * HEADS + h)
                    for c in range(CH):
                        mm = nc.tensor.matmul(psL[:, c * 512:(c + 1) * 512], q_head[:, h, :], kT[:, h * HID // P, c * 512:(c + 1) * 512],
                                              start=True, stop=True)
                    mm.then_inc(scores_done, 1)
                pe.wait_ge(head_added, i * HEADS + HEADS)
                for c in range(CH):
                    if c >= 2:
                        pe.wait_ge(t_emptied, i * CH + (c - 1))
                    for n in range(4):
                        tr = nc.tensor.transpose(psT[c % 2][:, n * P:(n + 1) * P], agg[:, (4 * c + n) * P:(4 * c + n + 1) * P], ident[:])
                    tr.then_inc(t_filled, 1)
                pe.wait_ge(t_emptied, i * CH + CH)
                for j in range(NT):
                    mm = nc.tensor.matmul(psO[:], agg_T[:, j, :], h_rows[:, j, :], start=(j == 0), stop=(j == NT - 1))
                mm.then_inc(o_filled, 1)


def heads_phase(nc, io, Wh, edge, dst, dst_low, dst_neg, src_bias, ident, x2_dram, l2_dram, x3_dram, src_dram, tiled):
    N, D = io["x"].shape
    NT, KT, T = N // P, D // P, 4
    G = NT // T
    HEADS, HID = io["l3_a1"].shape
    with ExitStack() as scope:
        sb = lambda n, s, d=F32: scope.enter_context(nc.sbuf_tensor("h_" + n, s, d))
        sem = lambda n: scope.enter_context(nc.semaphore("h_" + n))
        w = sb("w", [P, KT, D])
        a1, a2 = sb("a1", [P, D]), sb("a2", [P, D])
        x_rows, l_rows = sb("x_rows", [P, T, D]), sb("l_rows", [P, T, D])
        HT = sb("HT", [P, KT, T * P])
        adj_T = sb("adj_T", [P, 2, NT, P])
        prod = sb("prod", [P, HEADS, HID])
        src, src_T = sb("src", [P, NT, HEADS]), sb("src_T", [HEADS, N])
        top, top_all = sb("top", [P, HEADS]), sb("top_all", [P, HEADS])
        stats, mv, rstd = sb("stats", [P, T, 6]), sb("mv", [P, T, 2]), sb("rstd", [P, 3, T])
        psT = [scope.enter_context(nc.psum_tensor(f"h_psT{b}", [P, 512], F32)) for b in range(2)]
        psM = [scope.enter_context(nc.psum_tensor(f"h_psM{b}", [P, 512], F32)) for b in range(2)]
        psS = [scope.enter_context(nc.psum_tensor(f"h_psS{b}", [HEADS, 512], F32)) for b in range(2)]
        w_in, x_in, x3_out, adj_in = sem("w_in"), sem("x_in"), sem("x3_out"), [sem(f"adj_in{b}") for b in range(2)]
        x3_ready, h_ready, edge_done, src_out = sem("x3_ready"), sem("h_ready"), sem("edge_done"), sem("src_out")
        sqrt_asked, sqrt_done, chain_s = sem("sqrt_asked"), sem("sqrt_done"), sem("chain")
        t_filled, t_emptied, m_filled, m_emptied = (sem(n) for n in ("t_filled", "t_emptied", "m_filled", "m_emptied"))
        one_set, src_done, s_filled, s_emptied = sem("one_set"), sem("src_done"), sem("s_filled"), sem("s_emptied")
        top_done, top_spread, bias_done = sem("top_done"), sem("top_spread"), sem("bias_done")
        block = scope.enter_context(nc.Block())

        @block.sync
        def _(sp):
            sp.dma_start(x_rows[:], tiled(x2_dram)[:, 0:T, :]).then_inc(x_in, 16)
            sp.dma_start(l_rows[:], tiled(l2_dram)[:, 0:T, :]).then_inc(x_in, 16)
            sp.dma_start(w[:], io["l3_w"].rearrange("(k p) n -> p k n", p=P)).then_inc(w_in, 16)
            sp.dma_start(a1[:], io["l3_a1"].rearrange("h d -> (h d)").partition_broadcast(P)).then_inc(w_in, 16)
            sp.dma_start(a2[:], io["l3_a2"].rearrange("h d -> (h d)").partition_broadcast(P)).then_inc(w_in, 16)
            for g in range(G):
                for i in range(g * T, (g + 1) * T):
                    if i >= 2:
                        sp.wait_ge(edge_done, i - 1)
                    sp.dma_start(adj_T[:, i % 2, :, :], io["adj_t"][:, :, i, :].rearrange("n p c -> p n c")).then_inc(adj_in[i % 2], 16)
                sp.wait_ge(x3_ready, g + 1)
                sp.dma_start(tiled(x3_dram)[:, g * T:(g + 1) * T, :], x_rows[:]).then_inc(x3_out, 16)
                if g + 1 < G:
                    sp.wait_ge(x3_out, 16 * (g + 1))
                    sp.wait_ge(t_filled, (g + 1) * KT)
                    sp.dma_start(x_rows[:], tiled(x2_dram)[:, (g + 1) * T:(g + 2) * T, :]).then_inc(x_in, 16)
                    sp.dma_start(l_rows[:], tiled(l2_dram)[:, (g + 1) * T:(g + 2) * T, :]).then_inc(x_in, 16)
            sp.wait_ge(s_emptied, N // 512)
            sp.dma_start(src_dram, src_T[:]).then_inc(src_out, 16)
            sp.wait_ge(src_out, 16)
            sp.wait_ge(x3_out, 16 * G)

        @block.gpsimd
        def _(pool):
            nc.gpsimd.memset(Wh[:, :, :, HID:HID + 1], 1.0).then_inc(one_set, 1)
            pool.wait_ge(top_done, 1)
            nc.gpsimd.partition_all_reduce(top_all[:], top[:], P, bass.bass_isa.ReduceOp.max).then_inc(top_spread, 1)

        @block.vector
        def _(dve):
            chain = Chain(dve, chain_s)

            def parts(i):
                dve.wait_ge(m_emptied, i + 1)
                for a, dest in ((a1, src), (a2, dst)):
                    chain(nc.vector.tensor_tensor(prod[:], Wh[:, i, :, 0:HID], a[:].rearrange("p (h d) -> p h d", h=HEADS), ALU.mult))
                    chain(nc.vector.tensor_reduce(dest[:, i, :], prod[:], AX.X, ALU.add))

            for g in range(G):
                dve.wait_ge(x_in, 32 * (g + 1))
                nc.vector.tensor_tensor(x_rows[:], x_rows[:], l_rows[:], ALU.add).then_inc(x3_ready, 1)
                dve.wait_ge(x3_ready, g + 1)
                layer_norm_batch(nc, chain, x_rows, l_rows, stats, mv, rstd, sqrt_asked, sqrt_done, g, relu=True)
                dve.sem_inc(h_ready, 1)
                for i in range(g * T, (g + 1) * T):
                    dve.wait_ge(adj_in[i % 2], 16 * (i // 2 + 1))
                    nc.vector.tensor_scalar(edge[:, i, :], adj_T[:, i % 2, :, :].rearrange("p n c -> p (n c)"), 0.0, None,
                                            ALU.is_gt).then_inc(edge_done, 1)
                if g == 0:
                    dve.wait_ge(w_in, 48)
                for i in range(g * T, (g + 1) * T):
                    parts(i)
            dve.sem_inc(src_done, 1)
            nc.vector.tensor_reduce(top[:], dst[:].rearrange("p n h -> p h n"), AX.X, ALU.max).then_inc(top_done, 1)
            dve.wait_ge(top_spread, 1)
            chain.last_of([nc.vector.tensor_tensor(dst[:, i, :], dst[:, i, :], top_all[:], ALU.subtract) for i in range(NT)])
            chain(nc.vector.tensor_scalar(dst_low[:], dst[:], SLOPE, -SHIFT, ALU.mult, ALU.add))
            chain(nc.vector.tensor_scalar(dst[:], dst[:], SHIFT, None, ALU.add))
            chain(nc.vector.tensor_scalar(src_bias[:], top_all[:], 1 - SLOPE, -2 * SHIFT, ALU.mult, ALU.add))
            dve.sem_inc(bias_done, 1)
            dve.wait_ge(s_emptied, N // 512 + 2)
            chain(nc.vector.tensor_scalar(dst_neg[:], dst_low[:], -1.0, None, ALU.mult))

        @block.scalar
        def _(act):
            act.wait_ge(one_set, 1)
            for g in range(G):
                layer_norm_sqrt(nc, act, rstd, sqrt_asked, sqrt_done, g)
                for k in range(KT):
                    act.wait_ge(t_filled, g * KT + k + 1)
                    if g and k == 0:
                        act.wait_ge(m_filled, g * T)
                    nc.scalar.copy(HT[:, k, :], psT[k % 2][:, :]).then_inc(t_emptied, 1)
                for i in range(g * T, (g + 1) * T):
                    act.wait_ge(m_filled, i + 1)
                    nc.scalar.copy(Wh[:, i, :, 0:HID], psM[i % 2][:, :].rearrange("p (h d) -> p h d", h=HEADS)).then_inc(m_emptied, 1)
            for c in range(N // 512):
                act.wait_ge(s_filled, c + 1)
                nc.scalar.copy(src_T[:, c * 512:(c + 1) * 512], psS[c % 2][:, :]).then_inc(s_emptied, 1)
            act.wait_ge(bias_done, 1)
            for t in (dst, dst_low):
                nc.scalar.activation(t[:], t[:], ACT.Exp).then_inc(s_emptied, 1)

        @block.tensor
        def _(pe):
            for g in range(G):
                pe.wait_ge(h_ready, g + 1)
                for k in range(KT):
                    if g * KT + k >= 2:
                        pe.wait_ge(t_emptied, g * KT + k - 1)
                    for t in range(T):
                        tr = nc.tensor.transpose(psT[k % 2][:, t * P:(t + 1) * P], l_rows[:, t, k * P:(k + 1) * P], ident[:])
                    tr.then_inc(t_filled, 1)
                pe.wait_ge(t_emptied, (g + 1) * KT)
                if g == 0:
                    pe.wait_ge(w_in, 48)
                for t in range(T):
                    i = g * T + t
                    if i >= 2:
                        pe.wait_ge(m_emptied, i - 1)
                    for k in range(KT):
                        mm = nc.tensor.matmul(psM[i % 2][:, :], HT[:, k, t * P:(t + 1) * P], w[:, k, :], start=(k == 0), stop=(k == KT - 1))
                    mm.then_inc(m_filled, 1)
            pe.wait_ge(src_done, 1)
            for c in range(N // 512):
                if c >= 2:
                    pe.wait_ge(s_emptied, c - 1)
                for n in range(4):
                    tr = nc.tensor.transpose(psS[c % 2][:, n * P:(n + 1) * P], src[:, 4 * c + n, :], ident[:])
                tr.then_inc(s_filled, 1)


SLOPE = 0.2
SHIFT = 40.0


def gat_phase(nc, ident, Wh, edge, dst, dst_low, dst_neg, src_bias, enc, src_dram):
    _, NT, HEADS, W1 = Wh.shape
    HID, N = W1 - 1, edge.shape[2]
    CH = N // 512
    PER = 512 // W1
    BANKS = -(-NT // PER)
    with ExitStack() as scope:
        sb = lambda n, s, d=F32: scope.enter_context(nc.sbuf_tensor("e_" + n, s, d))
        sem = lambda n: scope.enter_context(nc.semaphore("e_" + n))
        source = sb("source", [P, 2, N])
        above, prob = sb("above", [P, 2, N]), sb("prob", [P, 2, N])
        inv = sb("inv", [P, NT])
        sums_T = sb("sums_T", [W1, N])
        acc = scope.enter_context(nc.psum_tensor("e_acc", [W1, N], F32))
        turned = [scope.enter_context(nc.psum_tensor(f"e_turned{k}", [P, 512], F32)) for k in range(BANKS)]
        src_in, src_ready = [sem(f"src_in{b}") for b in range(2)], sem("src_ready")
        above_done, prob_done, prob_used, inv_done = (sem(n) for n in ("above_done", "prob_done", "prob_used", "inv_done"))
        acc_copied, sums_turned, head_taken = sem("acc_copied"), sem("sums_turned"), sem("head_taken")
        block = scope.enter_context(nc.Block())

        def sums(k):
            n = min(PER, NT - k * PER)
            return turned[k][:, 0:n * W1].rearrange("p (n w) -> p n w", w=W1), slice(k * PER, k * PER + n)

        @block.sync
        def _(sp):
            for h in range(HEADS):
                if h >= 2:
                    sp.wait_ge(above_done, (h - 1) * NT)
                sp.dma_start(source[:, h % 2, :], src_dram[h].partition_broadcast(P)).then_inc(src_in[h % 2], 16)

        @block.scalar
        def _(act):
            def copy_sums(h):
                act.wait_ge(prob_used, (h + 1) * NT)
                if h:
                    act.wait_ge(sums_turned, h)
                for c in range(CH):
                    nc.scalar.copy(sums_T[:, c * 512:(c + 1) * 512], acc[:, c * 512:(c + 1) * 512]).then_inc(acc_copied, 1)

            for h in range(HEADS):
                act.wait_ge(src_in[h % 2], 16 * (h // 2 + 1))
                row = source[:, h % 2, :]
                nc.scalar.activation(row, row, ACT.Exp, scale=1 - SLOPE, bias=src_bias[:, h:h + 1]).then_inc(src_ready, 1)
                act.wait_ge(src_ready, h + 1)
                for j in range(NT):
                    n = h * NT + j
                    if n >= 2:
                        act.wait_ge(prob_done, n - 1)
                    nc.scalar.activation(above[:, n % 2, :], row, ACT.Relu, scale=dst[:, j, h:h + 1],
                                         bias=dst_neg[:, j, h:h + 1]).then_inc(above_done, 1)
                    if h and j == 1:
                        copy_sums(h - 1)
            copy_sums(HEADS - 1)

        @block.vector
        def _(dve):
            def take(h):
                dve.wait_ge(sums_turned, h + 1)
                for k in range(BANKS):
                    part, tiles = sums(k)
                    nc.vector.reciprocal(inv[:, tiles], part[:, :, HID]).then_inc(inv_done, 1)
                dve.wait_ge(inv_done, (h + 1) * BANKS)
                for k in range(BANKS):
                    part, tiles = sums(k)
                    n = part.shape[1]
                    nc.vector.tensor_tensor(enc[:, tiles, h * HID:(h + 1) * HID], part[:, :, 0:HID],
                                            inv[:, tiles].unsqueeze(2).broadcast_to([P, n, HID]), ALU.mult).then_inc(head_taken, 1)

            for h in range(HEADS):
                for j in range(NT):
                    n = h * NT + j
                    dve.wait_ge(above_done, n + 1)
                    if n >= 2:
                        dve.wait_ge(prob_used, n - 1)
                    nc.vector.scalar_tensor_tensor(out=prob[:, n % 2, :], in0=above[:, n % 2, :], scalar=dst_low[:, j, h:h + 1],
                                                   in1=edge[:, j, :], op0=ALU.add, op1=ALU.mult).then_inc(prob_done, 1)
                    if h and j == 4:
                        take(h - 1)
            take(HEADS - 1)

        @block.tensor
        def _(pe):
            def turn_sums(h):
                pe.wait_ge(acc_copied, (h + 1) * CH)
                if h:
                    pe.wait_ge(head_taken, h * BANKS)
                for i in range(NT):
                    k, m = i // PER, i % PER
                    tr = nc.tensor.transpose(turned[k][:, m * W1:(m + 1) * W1], sums_T[:, i * P:(i + 1) * P], ident[0:W1, 0:W1])
                tr.then_inc(sums_turned, 1)

            for h in range(HEADS):
                for j in range(NT):
                    n = h * NT + j
                    pe.wait_ge(prob_done, n + 1)
                    for c in range(CH):
                        if h and j == 0:
                            pe.wait_ge(acc_copied, (h - 1) * CH + c + 1)
                        mm = nc.tensor.matmul(acc[:, c * 512:(c + 1) * 512], Wh[:, j, h, :], prob[:, n % 2, c * 512:(c + 1) * 512],
                                              start=(j == 0), stop=(j == NT - 1))
                    mm.then_inc(prob_used, 1)
                    if h and j == 1:
                        turn_sums(h - 1)
            turn_sums(HEADS - 1)


def mlp_phase(nc, io, enc, ident, ones_row, x3_dram, out, tiled):
    _, NT, D = enc.shape
    KT, T = D // P, 4
    G = NT // T
    widths = [io[f"l3_w{n}"].shape[1] for n in range(1, 5)]
    with ExitStack() as scope:
        sb = lambda n, s, d=F32: scope.enter_context(nc.sbuf_tensor("f_" + n, s, d))
        sem = lambda n: scope.enter_context(nc.semaphore("f_" + n))
        w, b = [], []
        for n in range(1, 5):
            rows, cols = io[f"l3_w{n}"].shape
            w.append(sb(f"w{n}", [P, rows // P, cols]))
            b.append(sb(f"b{n}", [P, cols // P] if n < 4 else [1, cols]))
        low, lifted, act_in = sb("low", [P, T, D]), sb("lifted", [P, T, D]), sb("act_in", [P, 2, T, D])
        x_rows = sb("x_rows", [P, 2, T, D])
        o_rows = sb("o_rows", [P, 2, D])
        layers = [sb("layer0", [P, KT, 512])] + [sb(f"layer{n}", [P, widths[n - 1] // P, 512]) for n in range(1, 4)]
        psT = [scope.enter_context(nc.psum_tensor(f"f_psT{k}", [P, 512], F32)) for k in range(2)]
        psM = [scope.enter_context(nc.psum_tensor(f"f_psM{k}", [P, 512], F32)) for k in range(4)]
        w_in, x_in, o_out = sem("w_in"), [sem(f"x_in{k}") for k in range(2)], [sem(f"o_out{k}") for k in range(2)]
        low_done, exp_done, elu_done, chain_s = sem("low_done"), sem("exp_done"), sem("elu_done"), sem("chain")
        t_filled, t_emptied, m_filled, m_emptied = (sem(n) for n in ("t_filled", "t_emptied", "m_filled", "m_emptied"))
        sizes = [widths[n] // P for n in range(3)]
        block = scope.enter_context(nc.Block())
        per_batch = sum(sizes) + T

        def store(sp, g):
            for t in range(T):
                i = g * T + t
                sp.wait_ge(m_emptied, g * per_batch + sum(sizes) + t + 1)
                sp.dma_start(tiled(out)[:, i, :], o_rows[:, i % 2, :]).then_inc(o_out[i % 2], 16)

        @block.sync
        def _(sp):
            for n in range(4):
                sp.dma_start(w[n][:], io[f"l3_w{n + 1}"].rearrange("(k p) n -> p k n", p=P)).then_inc(w_in, 16)
                sp.dma_start(b[n][:], io[f"l3_b{n + 1}"]).then_inc(w_in, 16)
            for g in range(G):
                if g >= 2:
                    sp.wait_ge(m_filled, (g - 1) * per_batch)
                sp.dma_start(x_rows[:, g % 2, :, :], tiled(x3_dram)[:, g * T:(g + 1) * T, :]).then_inc(x_in[g % 2], 16)
                if g:
                    store(sp, g - 1)
            store(sp, G - 1)
            for k in range(2):
                sp.wait_ge(o_out[k], 16 * NT // 2)

        @block.vector
        def _(dve):
            chain = Chain(dve, chain_s)
            for g in range(G):
                part = enc[:, g * T:(g + 1) * T, :]
                if g:
                    dve.wait_ge(elu_done, g)
                nc.vector.tensor_scalar(low[:], part, 0.0, None, ALU.min).then_inc(low_done, 1)
                chain(nc.vector.tensor_scalar(lifted[:], part, 0.0, -1.0, ALU.max, ALU.add))
                dve.wait_ge(exp_done, g + 1)
                if g >= 2:
                    dve.wait_ge(t_filled, (g - 1) * KT)
                nc.vector.tensor_tensor(act_in[:, g % 2, :, :], low[:], lifted[:], ALU.add).then_inc(elu_done, 1)

        @block.scalar
        def _(act):
            n = 0
            act.wait_ge(w_in, 128)

            def elu_exp(g):
                act.wait_ge(low_done, g + 1)
                nc.scalar.activation(low[:], low[:], ACT.Exp).then_inc(exp_done, 1)

            elu_exp(0)
            for g in range(G):
                if g + 1 < G:
                    elu_exp(g + 1)
                for k in range(KT):
                    act.wait_ge(t_filled, g * KT + k + 1)
                    nc.scalar.copy(layers[0][:, k, :], psT[k % 2][:, :]).then_inc(t_emptied, 1)
                for layer in range(3):
                    for m in range(sizes[layer]):
                        act.wait_ge(m_filled, n + 1)
                        nc.scalar.activation(layers[layer + 1][:, m, :], psM[n % 4][:, :], ACT.Relu,
                                             bias=b[layer][:, m:m + 1]).then_inc(m_emptied, 1)
                        n += 1
                for t in range(T):
                    i = g * T + t
                    act.wait_ge(m_filled, n + 1)
                    if i >= 2:
                        act.wait_ge(o_out[i % 2], 16 * (i // 2))
                    nc.scalar.copy(o_rows[:, i % 2, :], psM[n % 4][:, :]).then_inc(m_emptied, 1)
                    n += 1

        @block.tensor
        def _(pe):
            n = 0

            def bank():
                if n >= 4:
                    pe.wait_ge(m_emptied, n - 3)
                return psM[n % 4]

            pe.wait_ge(w_in, 128)
            for g in range(G):
                pe.wait_ge(elu_done, g + 1)
                for k in range(KT):
                    if g * KT + k >= 2:
                        pe.wait_ge(t_emptied, g * KT + k - 1)
                    for t in range(T):
                        tr = nc.tensor.transpose(psT[k % 2][:, t * P:(t + 1) * P], act_in[:, g % 2, t, k * P:(k + 1) * P], ident[:])
                    tr.then_inc(t_filled, 1)
                pe.wait_ge(t_emptied, (g + 1) * KT)
                for layer in range(3):
                    for m in range(sizes[layer]):
                        ps = bank()
                        K = layers[layer].shape[1]
                        for k in range(K):
                            mm = nc.tensor.matmul(ps[:, :], w[layer][:, k, m * P:(m + 1) * P], layers[layer][:, k, :],
                                                  start=(k == 0), stop=(k == K - 1))
                        mm.then_inc(m_filled, 1)
                        n += 1
                    pe.wait_ge(m_emptied, n)
                pe.wait_ge(x_in[g % 2], 16 * (g // 2 + 1))
                for t in range(T):
                    ps = bank()
                    nc.tensor.matmul(ps[:, :], ident[:], x_rows[:, g % 2, t, :], start=True, stop=False)
                    nc.tensor.matmul(ps[:, :], ones_row[:, :], b[3][:, :], start=False, stop=False)
                    for k in range(2):
                        mm = nc.tensor.matmul(ps[:, :], layers[3][:, k, t * P:(t + 1) * P], w[3][:, k, :],
                                              start=False, stop=(k == 1))
                    mm.then_inc(m_filled, 1)
                    n += 1


def laid_out(np, v):
    adj = v["adj"]
    n = adj.shape[0] // P
    heads, d, hid = v["L3_gnn_W"].shape
    columns = lambda b: b.reshape(-1, P).T
    out = {
        "x": v["x"], "adj": adj, "adj_t": adj.reshape(n, P, n, P).transpose(0, 3, 2, 1),
        "l0_w1": v["L0_gnn_W1"], "l0_w2": v["L0_gnn_W2"], "l0_w3": v["L0_gnn_W3"],
        "l0_u1_0": v["L0_gnn_U1_0"], "l0_u1_1": v["L0_gnn_U1_1"], "l0_u2_0": v["L0_gnn_U2_0"], "l0_u2_1": v["L0_gnn_U2_1"],
        "l0_gamma": v["L0_gnn_gamma"], "l0_beta": v["L0_gnn_beta"],
        "l1_wq": v["L1_gnn_W_q"].T, "l1_wk": v["L1_gnn_W_k"].T, "l1_wv": v["L1_gnn_W_v"].T,
        "l1_bq": columns(v["L1_gnn_b_q"]), "l1_bk": columns(v["L1_gnn_b_k"]), "l1_bv": v["L1_gnn_b_v"],
        "l2_wq": v["L2_gnn_Wq"].T, "l2_wk": v["L2_gnn_Wk"].T, "l2_bq": columns(v["L2_gnn_bq"]), "l2_bk": columns(v["L2_gnn_bk"]),
        "l2_pairs": v["L2_gnn_rel_pair_index"].reshape(125, -1, 2),
        "l3_w": v["L3_gnn_W"].transpose(1, 0, 2).reshape(d, heads * hid), "l3_a1": v["L3_gnn_a1"], "l3_a2": v["L3_gnn_a2"],
    }
    for k in range(1, 5):
        out[f"l3_w{k}"] = v[f"L3_gnn_W{k}"].T
        out[f"l3_b{k}"] = columns(v[f"L3_gnn_b{k}"]) if k < 4 else v["L3_gnn_b4"].reshape(1, -1)
    return {name: np.ascontiguousarray(a) for name, a in out.items()}


def kernel(**inputs):
    import numpy as _np
    import concourse.bacc as _bacc
    from concourse import mybir as _mybir
    from concourse.bass_utils import run_bass_kernel_spmd as _run

    nc = _bacc.Bacc("TRN2", target_bir_lowering=False, num_devices=1)
    arrays = laid_out(_np, {k: _np.asarray(v) for k, v in inputs.items()})
    io = {k: nc.dram_tensor(f"in_{k}_dram", a.shape, _mybir.dt.from_np(a.dtype), kind="ExternalInput").ap()
          for k, a in arrays.items()}
    out = nc.dram_tensor("out_dram", inputs["x"].shape, F32, kind="ExternalOutput").ap()
    build(nc, io, out)
    r = _run(nc, [{f"in_{k}_dram": a for k, a in arrays.items()}], core_ids=[0])
    return r.results[0]["out_dram"]
```

```python
from contextlib import ExitStack
import math

import concourse.bass as bass
from concourse import mybir

F32 = mybir.dt.float32
BF16 = mybir.dt.bfloat16
I32 = mybir.dt.int32
U8 = mybir.dt.uint8
ALU = mybir.AluOpType
ACT = mybir.ActivationFunctionType
AX = mybir.AxisListType

P = 128
EPS = 1e-5
TOP_P = 0.9
BISECT_STEPS = 21


class Chain:

    def __init__(self, eng, sem):
        self.eng, self.sem, self.n = eng, sem, 0

    def __call__(self, ins):
        self.n += 1
        ins.then_inc(self.sem, 1)
        self.eng.wait_ge(self.sem, self.n)

    def last_of(self, group):
        for ins in group:
            self.n += 1
            ins.then_inc(self.sem, 1)
        self.eng.wait_ge(self.sem, self.n)


def make_identity(nc, pool, ident, made):
    nc.gpsimd.memset(ident[:], 0.0).then_inc(made, 1)
    pool.wait_ge(made, 1)
    nc.gpsimd.affine_select(out=ident[:], in_=ident[:], compare_op=ALU.not_equal, fill=1.0, base=0,
                            pattern=[[-1, P]], channel_multiplier=1).then_inc(made, 1)


def layer_norm_batch(nc, chain, src, dst, stats, mv, rstd, sqrt_asked, sqrt_done, turn, relu):
    T = src.shape[1]
    chain.last_of([nc.vector.bn_stats(stats[:, t, :], src[:, t, :]) for t in range(T)])
    chain.last_of([nc.vector.bn_aggr(mv[:, t, :], stats[:, t, :]) for t in range(T)])
    nc.vector.tensor_scalar(rstd[:, 0, :], mv[:, :, 1], EPS, None, ALU.add).then_inc(sqrt_asked, 1)
    chain.eng.wait_ge(sqrt_done, turn + 1)
    chain(nc.vector.reciprocal(rstd[:, 2, :], rstd[:, 1, :]))
    chain.last_of([nc.vector.tensor_scalar(dst[:, t, :], src[:, t, :], mv[:, t, 0:1], rstd[:, 2, t:t + 1],
                                           ALU.subtract, ALU.mult) for t in range(T)])
    if relu:
        chain(nc.vector.tensor_scalar(dst[:, :, :], dst[:, :, :], 0.0, None, ALU.max))


def layer_norm_sqrt(nc, act, rstd, sqrt_asked, sqrt_done, turn):
    act.wait_ge(sqrt_asked, turn + 1)
    nc.scalar.activation(rstd[:, 1, :], rstd[:, 0, :], ACT.Sqrt).then_inc(sqrt_done, 1)


def build(nc, io, out):
    N, D = io["x"].shape
    A = io["l0_w1"].shape[1]
    NT, KT = N // P, D // P
    HEADS, HID = io["l3_a1"].shape

    scratch = lambda name, shape=(N, D): nc.dram_tensor(name, list(shape), F32).ap()
    y_dram = [scratch(f"y{s}_scratch") for s in range(2)]
    xf_dram, x1_dram, x2_dram, l2_dram, x3_dram = (scratch(n) for n in ("xf", "x1", "x2", "l2", "x3"))
    src_dram = scratch("src", (HEADS, N))
    tiled = lambda ap: ap.rearrange("(n p) d -> p n d", p=P)

    with ExitStack() as whole:
        hold = lambda n, s, d=F32: whole.enter_context(nc.sbuf_tensor(n, s, d))
        ident = hold("ident", [P, P])
        inv_degree, ones_seen = hold("inv_degree", [P, NT]), hold("ones_seen", [P, NT + 1])
        has_ones = hold("has_ones", [P, 1], I32)
        with ExitStack() as scope:
            sb = lambda n, s, d=F32: scope.enter_context(nc.sbuf_tensor(n, s, d))
            XA = [sb("feat0", [P, NT, D]), sb("feat1", [P, NT, D])]
            QK = [sb("qk0", [P, N]), sb("qk1", [P, N])]
            w1, w3 = sb("w1", [P, KT, A]), sb("w3", [P, KT, A])
            w2 = sb("w2", [A, A])
            first_sem = norm_phase(nc, io, XA[0], QK[0], (w1, w2, w3), ident, inv_degree, ones_seen, has_ones, tiled)
            for s in range(2):
                last_sem = graph_step(nc, io, s, XA, QK, (w1, w2, w3), ident, inv_degree, y_dram, xf_dram, tiled)
        edge = hold("edge", [P, NT, N], U8)
        with ExitStack() as scope:
            sb = lambda n, s, d=F32: scope.enter_context(nc.sbuf_tensor(n, s, d))
            qT, kT, V = sb("qT", [P, KT, N]), sb("kT", [P, KT, N]), sb("V", [P, NT, D])
            project_phase(nc, io, range(first_sem, last_sem), qT, kT, V, ident, y_dram[1], x1_dram, tiled)
            attention_phase(nc, io, qT, kT, V, edge, ident, x1_dram, x2_dram, l2_dram, tiled)
        joined = nc.values_load(has_ones[0:1, 0:1], min_val=0, max_val=N * N,
                                skip_runtime_bounds_check_because="a count of the entries of adj")
        with nc.If(joined != 0):
            relation_phase(nc, io, ident, l2_dram, tiled)
        enc = hold("enc", [P, NT, D])
        with ExitStack() as scope:
            sb = lambda n, s, d=F32: scope.enter_context(nc.sbuf_tensor(n, s, d))
            Wh = sb("Wh", [P, NT, HEADS, HID + 1])
            dst, dst_low, dst_neg = (sb(n, [P, NT, HEADS]) for n in ("dst", "dst_low", "dst_neg"))
            src_bias = sb("src_bias", [P, HEADS])
            heads_phase(nc, io, Wh, dst, dst_low, dst_neg, src_bias, ident, x2_dram, l2_dram, x3_dram, src_dram, tiled)
            gat_phase(nc, ident, Wh, edge, dst, dst_low, dst_neg, src_bias, enc, src_dram)
        mlp_phase(nc, io, enc, ident, x3_dram, out, tiled)


def project_qk_pe(nc, pe, XT, w, ps, q_row, filled, emptied, n):
    w1, w2, w3 = w
    KT = w1.shape[1]
    for which in (w3, w1):
        if n:
            pe.wait_ge(emptied, n)
        for k in range(KT):
            mm = nc.tensor.matmul(ps[0:64, :], which[:, k, :], XT[:, k, :], start=(k == 0), stop=(k == KT - 1))
        mm.then_inc(filled, 1)
        n += 1
    pe.wait_ge(emptied, n)
    nc.tensor.matmul(ps[0:64, :], w2[:, :], q_row[:, :], start=True, stop=True).then_inc(filled, 1)
    return n + 1


def project_qk_act(nc, act, ps, q_row, QK, g, filled, emptied, n):
    for dst in (QK[0:64, g * 512:(g + 1) * 512], q_row[:, :], QK[64:128, g * 512:(g + 1) * 512]):
        act.wait_ge(filled, n + 1)
        nc.scalar.copy(dst, ps[0:64, :]).then_inc(emptied, 1)
        n += 1
    return n


def norm_phase(nc, io, H, QK, w, ident, inv_degree, ones_seen, has_ones, tiled):
    N, D = io["x"].shape
    NT, KT, T = N // P, D // P, 4
    G = NT // T
    AHEAD = 7
    with ExitStack() as scope:
        sb = lambda n, s, d=F32: scope.enter_context(nc.sbuf_tensor("a_" + n, s, d))
        sem = lambda n: scope.enter_context(nc.semaphore("a_" + n))
        xin = sb("xin", [P, NT, D])
        adj_rows = sb("adj_rows", [P, AHEAD, N])
        XT = sb("XT", [P, KT, 512])
        q_row = sb("q_row", [64, 512])
        stats, mv, rstd = sb("stats", [P, T, 6]), sb("mv", [P, T, 2]), sb("rstd", [P, 3, T])
        junk, junk2 = sb("junk", [P, N], BF16), sb("junk2", [P, N], BF16)
        degree, ones_all = sb("degree", [P, NT]), sb("ones_all", [P, 1])
        psT = [scope.enter_context(nc.psum_tensor(f"a_psT{b}", [P, 512], F32)) for b in range(2)]
        psQ = scope.enter_context(nc.psum_tensor("a_psQ", [P, 512], F32))

        x_in = [sem(f"x_in{g}") for g in range(G)]
        first_sem = x_in[0].num
        w_in = sem("w_in")
        adj_in = [sem(f"adj_in{b}") for b in range(AHEAD)]
        adj_summed, adj_counted = sem("adj_summed"), sem("adj_counted")
        ones_added, ones_spread = sem("ones_added"), sem("ones_spread")
        id_made, chain_s = sem("id_made"), sem("chain")
        sqrt_asked, sqrt_done, h_ready = sem("sqrt_asked"), sem("sqrt_done"), sem("h_ready")
        t_filled, t_emptied, q_filled, q_emptied = sem("t_filled"), sem("t_emptied"), sem("q_filled"), sem("q_emptied")
        block = scope.enter_context(nc.Block())

        @block.sync
        def _(sp):
            for g in range(G):
                sp.dma_start(xin[:, g * T:(g + 1) * T, :], tiled(io["x"])[:, g * T:(g + 1) * T, :]).then_inc(x_in[g], 16)
            for t, name in zip(w, ("l0_w1", "l0_w2", "l0_w3")):
                src = io[name] if name == "l0_w2" else io[name].rearrange("(k p) a -> p k a", p=P)
                sp.dma_start(t[:], src).then_inc(w_in, 16)
            for i in range(NT):
                if i >= AHEAD:
                    sp.wait_ge(adj_summed, i - AHEAD + 1)
                    sp.wait_ge(adj_counted, i - AHEAD + 1)
                sp.dma_start(adj_rows[:, i % AHEAD, :], io["adj"][i * P:(i + 1) * P, :]).then_inc(adj_in[i % AHEAD], 16)

        @block.gpsimd
        def _(pool):
            make_identity(nc, pool, ident, id_made)
            pool.wait_ge(ones_added, 1)
            nc.gpsimd.partition_all_reduce(ones_all[:], ones_seen[:, NT:NT + 1], P,
                                           bass.bass_isa.ReduceOp.add).then_inc(ones_spread, 1)

        @block.vector
        def _(dve):
            chain = Chain(dve, chain_s)
            for g in range(G):
                dve.wait_ge(x_in[g], 16)
                layer_norm_batch(nc, chain, xin[:, g * T:(g + 1) * T, :], H[:, g * T:(g + 1) * T, :], stats, mv, rstd,
                                 sqrt_asked, sqrt_done, g, relu=True)
                dve.sem_inc(h_ready, 1)
            for i in range(NT):
                dve.wait_ge(adj_in[i % AHEAD], 16 * (i // AHEAD + 1))
                if i:
                    dve.wait_ge(adj_counted, i)
                ins = nc.vector.tensor_scalar(junk2[:, :], adj_rows[:, i % AHEAD, :], 1.0, 0.0, ALU.is_equal, ALU.add,
                                              accum_out=ones_seen[:, i:i + 1])
                ins.then_inc(adj_counted, 1)
            dve.wait_ge(adj_counted, NT)
            nc.vector.tensor_reduce(ones_seen[:, NT:NT + 1], ones_seen[:, 0:NT], AX.X, ALU.add).then_inc(ones_added, 1)
            dve.wait_ge(ones_spread, 1)
            chain(nc.vector.tensor_copy(has_ones[:], ones_all[:]))
            dve.wait_ge(adj_summed, NT)
            chain(nc.vector.tensor_scalar(degree[:, :], degree[:, :], 1.0, 1e-12, ALU.add, ALU.max))
            chain(nc.vector.reciprocal(inv_degree[:, :], degree[:, :]))

        @block.scalar
        def _(act):
            for g in range(G):
                layer_norm_sqrt(nc, act, rstd, sqrt_asked, sqrt_done, g)
            nT = nQ = 0
            for g in range(G):
                for k in range(KT):
                    act.wait_ge(t_filled, nT + 1)
                    if k == 0 and g:
                        act.wait_ge(q_filled, nQ)
                    nc.scalar.copy(XT[:, k, :], psT[nT % 2][:, :]).then_inc(t_emptied, 1)
                    nT += 1
                nQ = project_qk_act(nc, act, psQ, q_row, QK, g, q_filled, q_emptied, nQ)
            for i in range(NT):
                act.wait_ge(adj_in[i % AHEAD], 16 * (i // AHEAD + 1))
                if i:
                    act.wait_ge(adj_summed, i)
                nc.scalar.activation(junk[:, :], adj_rows[:, i % AHEAD, :], ACT.Copy,
                                     accum_out=degree[:, i:i + 1]).then_inc(adj_summed, 1)

        @block.tensor
        def _(pe):
            pe.wait_ge(id_made, 2)
            pe.wait_ge(w_in, 48)
            nT = nQ = 0
            for g in range(G):
                pe.wait_ge(h_ready, g + 1)
                for k in range(KT):
                    if nT >= 2:
                        pe.wait_ge(t_emptied, nT - 1)
                    for t in range(T):
                        tr = nc.tensor.transpose(psT[nT % 2][:, t * P:(t + 1) * P], H[:, g * T + t, k * P:(k + 1) * P], ident[:, :])
                    tr.then_inc(t_filled, 1)
                    nT += 1
                pe.wait_ge(t_emptied, nT)
                nQ = project_qk_pe(nc, pe, XT, w, psQ, q_row, q_filled, q_emptied, nQ)
    return first_sem


def graph_step(nc, io, s, XA, QK, w, ident, inv_degree, y_dram, xf_dram, tiled):
    N, D = io["x"].shape
    NT, KT, T = N // P, D // P, 4
    G, CH = NT // T, N // 512
    last_step = s == 1
    Xa, Xn = XA[s], XA[1 - s]
    Xf = XA[0]
    own = QK[s]
    with ExitStack() as scope:
        sb = lambda n, sh, d=F32: scope.enter_context(nc.sbuf_tensor(f"g{s}_{n}", sh, d))
        sem = lambda n: scope.enter_context(nc.semaphore(f"g{s}_{n}"))
        if last_step:
            xa_row = QK[0][:, 0:2 * D].rearrange("p (b d) -> p b d", b=2)
            y_before = QK[0][:, 2 * D:4 * D].rearrange("p (b d) -> p b d", b=2)
        prob = sb("prob", [P, 2 * T, N])
        PT = sb("PT", [P, 2, 512])
        PARTS, RING = 8, 3
        PART = NT // PARTS
        adj_T = sb("adj_T", [P, RING, PART, P])
        u1, u2 = sb("u1", [P, KT, D]), sb("u2", [P, KT, D])
        XfT, XaT = sb("XfT", [P, 2 * T, KT, P]), sb("XaT", [P, KT, T * P])
        q_tile = sb("q_tile", [64, P])
        y_row = sb("y_row", [P, D])
        xf_row = sb("xf_row", [P, 2, D])
        q_row = y_row[0:64, :]
        junk, junk_act = sb("junk", [P, 2, N], U8), sb("junk_act", [P, N], U8)
        (neg_trial, goal_2, excess, balance, above_2, lack, reached, factor, n_column) = (
            sb(n, [P, 1]) for n in ("neg_trial", "goal_2", "excess", "balance", "above_2", "lack", "reached", "factor", "n_column"))
        spread, middle = sb("spread", [P, BISECT_STEPS]), sb("middle", [P, BISECT_STEPS])
        neg_max, total, kept, inv_kept = (sb(n, [P, NT]) for n in ("neg_max", "total", "kept", "inv_kept"))
        factors = sb("factors", [P, BISECT_STEPS])
        floor = sb("floor", [P, T])
        trial, mass, goal, step_up = (sb(n, [P, T - 1]) for n in ("trial", "mass", "goal", "step_up"))
        psum = scope.enter_context(nc.psum_tensor(f"g{s}_psum", [P, 2 * N], F32))
        psL = [psum[:, 0:N], psum[:, N:2 * N]]
        psT = [psum[:, N + b * 512:N + (b + 1) * 512] for b in range(2)]
        psS = [psum[:, N + b * 512:N + (b + 1) * 512] for b in range(2, 4)]
        L = lambda i: psL[i % 2 if i < T else 0]

        adj_in, adj_used = [sem(f"adj_in{b}") for b in range(RING)], sem("adj_used")
        u_in, xf_in = sem("u_in"), sem("xf_in")
        yin = [sem(f"y_in{b}") for b in range(2)]
        q_staged = sem("q_staged")
        scores_done, max_done, exp_done, mask_done, inv_done = (sem(n) for n in ("scores_done", "max_done", "exp_done", "mask_done", "inv_done"))
        t_filled, t_emptied, pt_used = sem("t_filled"), sem("t_emptied"), sem("pt_used")
        s_filled, s_emptied = sem("s_filled"), sem("s_emptied")
        y_out, xf_out = sem("y_out"), [sem(f"xf_out{b}") for b in range(2)]
        act_floor, act_chain = sem("act_floor"), sem("act_chain")
        floor_read = sem("floor_read")
        columns_set = sem("columns_set")
        first_sem = adj_in[0].num
        chain_s = sem("chain")
        block = scope.enter_context(nc.Block())
        LEAST = (1 - TOP_P) / N * 0.99
        WIDTH = -math.log(LEAST) + 1e-3
        up = [math.exp(WIDTH / 2 ** (k + 1)) for k in range(BISECT_STEPS)]
        cuts = [3, 9, 15, BISECT_STEPS]
        ACT_TILE = T - 1
        LAST_QUARTERS = T + 2
        MORE = 3

        def order():
            for t in range(T):
                yield "scores", t, 0, 0
                yield "exp", t, 0, 0
            for g in range(G):
                for t in range(T):
                    if g:
                        yield "attend", (g - 1) * T + t, g, t
                    if g == 0:
                        yield "relate", 2 * t, g, t
                        yield "turn Xf", 2 * t, g, t
                    elif g + 1 < G:
                        yield "relate", (g + 1) * T + t, g, t
                    if g:
                        yield "turn Xa", (g - 1) * T + t, g, t
                    if g + 1 < G:
                        yield "scores", (g + 1) * T + t, g, t
                    if g == 0:
                        yield "relate", 2 * t + 1, g, t
                        yield "turn Xf", 2 * t + 1, g, t
                    if g:
                        yield "add", (g - 1) * T + t, g, t
                        if g + 1 < G:
                            yield "turn Xf", (g + 1) * T + t, g, t
                    if g + 1 < G:
                        yield "exp", (g + 1) * T + t, g, t
                if g and not last_step:
                    yield "project", g - 1, g, T - 1
            for t in range(T):
                for what in ("attend", "turn Xa", "add"):
                    yield what, (G - 1) * T + t, G - 1, T + t
            if not last_step:
                yield "project", G - 1, G - 1, 2 * T

        turn = {}
        uses = 0
        for what, i, _, _ in order():
            if what in ("attend", "relate", "add", "project"):
                turn[what, i] = uses
                uses += 3 if what == "project" else 1

        def store_y(sp, i):
            sp.wait_ge(s_emptied, turn["add", i] + 1)
            sp.dma_start(tiled(y_dram[s])[:, i, :], y_row[:, :]).then_inc(y_out, 16)

        def store_xf(sp, i):
            sp.wait_ge(s_emptied, turn["relate", i] + 1)
            sp.dma_start(tiled(xf_dram)[:, i, :], xf_row[:, i % 2, :]).then_inc(xf_out[i % 2], 16)

        @block.sync
        def _(sp):
            if last_step:
                sp.dma_start(Xf[:, :, :], tiled(xf_dram)).then_inc(xf_in, 16)
            for t, name in ((u1, f"l0_u1_{s}"), (u2, f"l0_u2_{s}")):
                sp.dma_start(t[:], io[name].rearrange("(k p) a -> p k a", p=P)).then_inc(u_in, 16)
            for what, i, _, _ in order():
                if what == "relate":
                    for part in range(PARTS):
                        n = PARTS * i + part
                        if n >= RING:
                            sp.wait_ge(adj_used, n - RING + 1)
                        sp.dma_start(adj_T[:, n % RING, :, :], io["adj_t"][i, :, part * PART:(part + 1) * PART, :])\
                            .then_inc(adj_in[n % RING], 16)
                    if not last_step and i >= 1:
                        store_xf(sp, i - 1)
                if what == "attend":
                    if last_step:
                        if i >= 2:
                            sp.wait_ge(s_filled, turn["add", i - 2] + 1)
                        sp.dma_start(y_before[:, i % 2, :], tiled(y_dram[0])[:, i, :]).then_inc(yin[i % 2], 16)
                    if i >= 1:
                        store_y(sp, i - 1)
            if not last_step:
                store_xf(sp, NT - 1)
            store_y(sp, NT - 1)
            sp.wait_ge(y_out, 16 * NT)
            if not last_step:
                for b in range(2):
                    sp.wait_ge(xf_out[b], 16 * NT // 2)

        @block.gpsimd
        def _(pool):
            for i in range(NT):
                if i:
                    pool.wait_ge(scores_done, i)
                nc.gpsimd.tensor_copy(q_tile[:, :], own[64:128, i * P:(i + 1) * P]).then_inc(q_staged, 1)

        @block.vector
        def _(dve):
            chain = Chain(dve, chain_s)
            chain.last_of([nc.vector.memset(factors[:, k:k + 1], up[k]) for k in range(BISECT_STEPS)])
            for k in range(BISECT_STEPS):
                reached_by = up[k + 1] if k + 1 < BISECT_STEPS else 1.0 - 2e-6
                missed_by = reached_by / up[k]
                nc.vector.memset(spread[:, k:k + 1], (reached_by - missed_by) / 2)
                nc.vector.memset(middle[:, k:k + 1], (reached_by + missed_by) / 2)
            nc.vector.memset(n_column[:, :], float(N)).then_inc(columns_set, 1)

            def row_max(i):
                dve.wait_ge(scores_done, i + 1)
                nc.vector.tensor_reduce(neg_max[:, i:i + 1], L(i), AX.X, ALU.max, negate=True).then_inc(max_done, 1)

            def bisect(g, k0, k1, a=0, b=ACT_TILE):
                base, per = chain.n, b - a + 4
                with dve.Fori(0, (k1 - k0) // MORE) as r:
                    n = [0]

                    def link(ins, wait=True):
                        n[0] += 1
                        ins.then_inc(chain_s, 1)
                        if wait:
                            dve.wait_ge(chain_s, r * (MORE * per) + (base + n[0]))

                    for m in range(MORE):
                        link(nc.vector.tensor_scalar(trial[:, a:b], floor[:, a:b], factors[:, bass.ds(r * MORE + (k0 + m), 1)],
                                                     None, ALU.mult))
                        for t in range(a, b):
                            slot = (g * T + t) % (2 * T)
                            link(nc.vector.scalar_tensor_tensor(
                                out=junk[:, t % 2, :], in0=prob[:, slot, :], scalar=trial[:, t:t + 1],
                                in1=prob[:, slot, :], op0=ALU.is_ge, op1=ALU.mult, accum_out=mass[:, t:t + 1]),
                                 wait=(t > a or t == b - 1))
                        link(nc.vector.tensor_tensor(step_up[:, a:b], mass[:, a:b], goal[:, a:b], ALU.is_ge))
                        link(nc.vector.tensor_tensor(step_up[:, a:b], step_up[:, a:b], trial[:, a:b], ALU.mult))
                        link(nc.vector.tensor_tensor(floor[:, a:b], floor[:, a:b], step_up[:, a:b], ALU.max))
                chain.n = base + per * (k1 - k0)

            def mask(i):
                row = prob[:, i % (2 * T), :]
                nc.vector.scalar_tensor_tensor(out=row, in0=row, scalar=floor[:, i % T:i % T + 1], in1=row, op0=ALU.is_ge,
                                               op1=ALU.mult, accum_out=kept[:, i:i + 1]).then_inc(mask_done, 1)
                dve.wait_ge(mask_done, i + 1)
                nc.vector.reciprocal(inv_kept[:, i:i + 1], kept[:, i:i + 1]).then_inc(inv_done, 1)

            for t in range(T):
                row_max(t)
            for g in range(G):
                dve.wait_ge(exp_done, (g + 1) * T)
                own_tiles = slice(g * T, g * T + ACT_TILE)
                chain(nc.vector.tensor_scalar(goal[:, :], total[:, own_tiles], TOP_P, None, ALU.mult))
                chain(nc.vector.tensor_scalar(floor[:, 0:ACT_TILE], total[:, own_tiles], LEAST, None, ALU.mult))
                if g + 1 < G:
                    for t in range(T):
                        bisect(g, cuts[t - 1] if t else 0, cuts[t])
                        if t == T - 1:
                            mask(g * T)
                        row_max((g + 1) * T + t)
                    for t in range(1, ACT_TILE):
                        mask(g * T + t)
                else:
                    for a, b in ((0, ACT_TILE - 1), (ACT_TILE - 1, ACT_TILE)):
                        bisect(g, 0, BISECT_STEPS, a, b)
                        for t in range(a, b):
                            mask(g * T + t)
                dve.wait_ge(act_floor, g + 1)
                chain(nc.vector.tensor_scalar(floor[:, ACT_TILE:T], neg_trial[:, :], -1.0, None, ALU.mult))
                dve.sem_inc(floor_read, 1)
                mask(g * T + ACT_TILE)

        @block.scalar
        def _(act):
            nT = nPT = 0
            chain = Chain(act, act_chain)

            def from_T(dst):
                nonlocal nT
                act.wait_ge(t_filled, nT + 1)
                nc.scalar.copy(dst, psT[nT % 2][:, :] if len(dst.shape) == 2 else
                               psT[nT % 2][:, :].rearrange("p (k i) -> p k i", k=KT)).then_inc(t_emptied, 1)
                nT += 1

            def bisect_until(n):
                nonlocal steps_done
                for n in range(steps_done, n):
                    g, k = divmod(n, BISECT_STEPS)
                    i = g * T + ACT_TILE
                    p = prob[:, i % (2 * T), :]
                    if k == 0:
                        if g:
                            act.wait_ge(floor_read, g)
                        else:
                            act.wait_ge(columns_set, 1)
                        act.wait_ge(exp_done, i + 1)
                        chain(nc.scalar.mul(neg_trial[:, :], total[:, i:i + 1], -LEAST * up[0]))
                        chain(nc.scalar.mul(goal_2[:, :], total[:, i:i + 1], 2 * TOP_P))
                    chain(nc.scalar.activation(junk_act[:, :], p, ACT.Relu, bias=neg_trial[:, :], accum_out=excess[:, :]))
                    chain(nc.scalar.activation(junk_act[:, :], p, ACT.Sign, bias=neg_trial[:, :], accum_out=balance[:, :]))
                    chain(nc.scalar.activation(above_2[:, :], balance[:, :], ACT.Identity, bias=n_column[:, :]))
                    chain(nc.scalar.activation(lack[:, :], above_2[:, :], ACT.Identity, scale=neg_trial[:, :], bias=goal_2[:, :]))
                    chain(nc.scalar.activation(reached[:, :], lack[:, :], ACT.Sign, scale=-0.5, bias=excess[:, :]))
                    chain(nc.scalar.activation(factor[:, :], reached[:, :], ACT.Identity, scale=spread[:, k:k + 1],
                                               bias=middle[:, k:k + 1]))
                    last = nc.scalar.activation(neg_trial[:, :], neg_trial[:, :], ACT.Copy, scale=factor[:, :])
                    if k + 1 < BISECT_STEPS:
                        chain(last)
                    else:
                        last.then_inc(act_floor, 1)
                    steps_done = n + 1

            def pace(g, quarter, part):
                share = (quarter + part) / (T if g + 1 < G else LAST_QUARTERS)
                bisect_until(g * BISECT_STEPS + round(BISECT_STEPS * min(share, 1)))

            def empty(what, i, dst, scale=None):
                act.wait_ge(s_filled, turn[what, i] + 1)
                nc.scalar.activation(dst, psS[turn[what, i] % 2][:, :], ACT.Copy,
                                     **({} if scale is None else {"scale": scale})).then_inc(s_emptied, 1)

            steps_done = 0
            for what, i, g, quarter in order():
                t = i % T
                if what == "scores":
                    if g:
                        pace(g, quarter, 1)
                elif what == "exp":
                    act.wait_ge(max_done, i + 1)
                    if i >= 2 * T:
                        act.wait_ge(pt_used, (i - 2 * T + 1) * CH)
                    nc.scalar.activation(prob[:, i % (2 * T), :], L(i), ACT.Exp, bias=neg_max[:, i:i + 1],
                                         accum_out=total[:, i:i + 1]).then_inc(exp_done, 1)
                elif what == "relate":
                    pace(g, quarter, 0.85 if g else 0.4 + 0.6 * (i % 2))
                    if not last_step and i >= 2:
                        act.wait_ge(xf_out[i % 2], 16 * (i // 2))
                    empty(what, i, xf_row[:, i % 2, :], inv_degree[:, i:i + 1])
                elif what == "turn Xf":
                    if i >= 2 * T:
                        act.wait_ge(s_filled, turn["add", i - 2 * T] + 1)
                    from_T(XfT[:, i % (2 * T), :, :])
                elif what == "attend":
                    for c in range(CH):
                        if nPT >= 2:
                            act.wait_ge(pt_used, nPT - 1)
                        from_T(PT[:, nPT % 2, :])
                        nPT += 1
                        if c % 2:
                            pace(g, quarter, 0.12 * c if g + 1 < G else 0.3 * c)
                    act.wait_ge(inv_done, i + 1)
                    empty(what, i, xa_row[:, i % 2, :] if last_step else Xn[:, i, :], inv_kept[:, i:i + 1])
                elif what == "turn Xa":
                    if t == 0 and i and not last_step:
                        act.wait_ge(s_filled, turn["project", i // T - 1] + 3)
                    elif last_step and i >= T:
                        act.wait_ge(s_filled, turn["add", i - T] + 1)
                    from_T(XaT[:, :, t * P:(t + 1) * P])
                elif what == "add":
                    pace(g, quarter, 1)
                    if i:
                        act.wait_ge(y_out, 16 * i)
                    empty(what, i, y_row[:, :])
                elif what == "project":
                    act.wait_ge(y_out, 16 * T * (i + 1))
                    n = turn[what, i]
                    for m, dst in enumerate((QK[1][0:64, i * 512:(i + 1) * 512], q_row, QK[1][64:128, i * 512:(i + 1) * 512])):
                        act.wait_ge(s_filled, n + m + 1)
                        nc.scalar.copy(dst, psS[(n + m) % 2][0:64, :]).then_inc(s_emptied, 1)

        @block.tensor
        def _(pe):
            nT = nPT = 0

            def to_T(srcs):
                nonlocal nT
                if nT >= 2:
                    pe.wait_ge(t_emptied, nT - 1)
                for n, src in enumerate(srcs):
                    tr = nc.tensor.transpose(psT[nT % 2][:, n * P:(n + 1) * P], src, ident[:, :])
                tr.then_inc(t_filled, 1)
                nT += 1

            def bank(what, i, more=0):
                n = turn[what, i] + more
                if n >= 2:
                    pe.wait_ge(s_emptied, n - 1)
                return psS[n % 2]

            for what, i, _, _ in order():
                t = i % T
                if what == "relate" and i == 0:
                    pe.wait_ge(exp_done, T)
                if what == "scores":
                    pe.wait_ge(q_staged, i + 1)
                    if i >= 2:
                        pe.wait_ge(exp_done, i - 1 if i < T else i)
                    for c in range(CH):
                        mm = nc.tensor.matmul(L(i)[:, c * 512:(c + 1) * 512], q_tile[:, :],
                                              own[0:64, c * 512:(c + 1) * 512], start=True, stop=True)
                    mm.then_inc(scores_done, 1)
                elif what == "relate":
                    if i == 0:
                        if last_step:
                            pe.wait_ge(xf_in, 16)
                        pe.wait_ge(u_in, 32)
                    ps = bank(what, i)
                    nc.tensor.matmul(ps[:, :], ident[:, :], Xf[:, i, :], start=True, stop=False)
                    for part in range(PARTS):
                        n = PARTS * i + part
                        pe.wait_ge(adj_in[n % RING], 16 * (n // RING + 1))
                        for jj in range(PART):
                            j = part * PART + jj
                            mm = nc.tensor.matmul(ps[:, :], adj_T[:, n % RING, jj, :], Xf[:, j, :],
                                                  start=False, stop=(j == NT - 1))
                        if part < PARTS - 1:
                            mm.then_inc(adj_used, 1)
                    mm.then_inc(s_filled, 1)
                elif what == "turn Xf":
                    pe.wait_ge(s_emptied, turn["relate", i] + 1)
                    pe.sem_inc(adj_used, 1)
                    to_T([xf_row[:, i % 2, k * P:(k + 1) * P] for k in range(KT)])
                elif what == "attend":
                    pe.wait_ge(mask_done, i + 1)

                    def transpose_part(c):
                        to_T([prob[:, i % (2 * T), (4 * c + n) * P:(4 * c + n + 1) * P] for n in range(4)])

                    transpose_part(0)
                    for c in range(CH):
                        if c + 1 < CH:
                            transpose_part(c + 1)
                        pe.wait_ge(t_emptied, nT - (1 if c + 1 < CH else 0))
                        if c == 0:
                            ps = bank(what, i)
                        for n in range(4):
                            j = 4 * c + n
                            mm = nc.tensor.matmul(ps[:, :], PT[:, nPT % 2, n * P:(n + 1) * P], Xa[:, j, :],
                                                  start=(j == 0), stop=(j == NT - 1))
                        if c + 1 < CH:
                            mm.then_inc(pt_used, 1)
                        nPT += 1
                    mm.then_inc(s_filled, 1)
                    pe.wait_ge(s_filled, turn[what, i] + 1)
                    pe.sem_inc(pt_used, 1)
                elif what == "turn Xa":
                    pe.wait_ge(s_emptied, turn["attend", i] + 1)
                    row = xa_row[:, i % 2, :] if last_step else Xn[:, i, :]
                    to_T([row[:, k * P:(k + 1) * P] for k in range(KT)])
                    xa_turned = nT
                elif what == "add":
                    if last_step:
                        pe.wait_ge(yin[i % 2], 16 * (i // 2 + 1))
                    before = y_before[:, i % 2, :] if last_step else Xf[:, i, :]
                    ps = bank(what, i)
                    nc.tensor.matmul(ps[:, :], ident[:, :], before, start=True, stop=False)
                    for k in range(KT):
                        nc.tensor.matmul(ps[:, :], XfT[:, i % (2 * T), k, :], u1[:, k, :], start=False, stop=False)
                    pe.wait_ge(t_emptied, xa_turned)
                    for k in range(KT):
                        mm = nc.tensor.matmul(ps[:, :], XaT[:, k, t * P:(t + 1) * P], u2[:, k, :],
                                              start=False, stop=(k == KT - 1))
                    mm.then_inc(s_filled, 1)
                elif what == "project":
                    for m, which in enumerate((w[2], w[0])):
                        ps = bank(what, i, m)
                        for k in range(KT):
                            mm = nc.tensor.matmul(ps[0:64, :], which[:, k, :], XaT[:, k, :], start=(k == 0), stop=(k == KT - 1))
                        mm.then_inc(s_filled, 1)
                    ps = bank(what, i, 2)
                    pe.wait_ge(s_emptied, turn[what, i] + 2)
                    nc.tensor.matmul(ps[0:64, :], w[1][:, :], q_row, start=True, stop=True).then_inc(s_filled, 1)
    return first_sem


def project_phase(nc, io, used_sems, qT, kT, V, ident, y_dram, x1_dram, tiled):
    N, D = io["x"].shape
    NT, KT, T = N // P, D // P, 4
    G = NT // T
    with ExitStack() as scope:
        sb = lambda n, s, d=F32: scope.enter_context(nc.sbuf_tensor("p_" + n, s, d))
        sem = lambda n: scope.enter_context(nc.semaphore("p_" + n))
        wq, wk, wv = (sb(n, [P, KT, D]) for n in ("wq", "wk", "wv"))
        bq, bk, bv = sb("bq", [P, KT]), sb("bk", [P, KT]), sb("bv", [P, D])
        gamma, beta = sb("gamma", [P, D]), sb("beta", [P, D])
        rows, x_rows, h = sb("rows", [P, T, D]), sb("x_rows", [P, T, D]), sb("h", [P, 2, T, D])
        HT = sb("HT", [P, KT, T * P])
        stats, mv, rstd = sb("stats", [P, T, 6]), sb("mv", [P, T, 2]), sb("rstd", [P, 3, T])
        psT = [scope.enter_context(nc.psum_tensor(f"p_psT{b}", [P, 512], F32)) for b in range(2)]
        psM = [scope.enter_context(nc.psum_tensor(f"p_psM{b}", [P, 512], F32)) for b in range(4)]
        psV = [scope.enter_context(nc.psum_tensor(f"p_psV{b}", [P, 512], F32)) for b in range(2)]
        v_filled, v_emptied = sem("v_filled"), sem("v_emptied")
        w_in, bias_in, y_in, x_in, x1_out = (sem(n) for n in ("w_in", "bias_in", "y_in", "x_in", "x1_out"))
        y_free, x1_ready, h_ready = sem("y_free"), sem("x1_ready"), sem("h_ready")
        sqrt_asked, sqrt_done, chain_s = sem("sqrt_asked"), sem("sqrt_done"), sem("chain")
        t_filled, t_emptied, m_filled, m_emptied = (sem(n) for n in ("t_filled", "t_emptied", "m_filled", "m_emptied"))
        products = 2 * KT
        block = scope.enter_context(nc.Block())

        @block.sync
        def _(sp):
            for g in range(G):
                both = slice(g * T, (g + 1) * T)
                if g:
                    sp.wait_ge(y_free, g)
                sp.dma_start(rows[:], tiled(y_dram)[:, both, :]).then_inc(y_in, 16)
                if g:
                    sp.wait_ge(x1_ready, g)
                    sp.dma_start(tiled(x1_dram)[:, (g - 1) * T:g * T, :], x_rows[:]).then_inc(x1_out, 16)
                    sp.wait_ge(x1_out, 16 * g)
                    sp.wait_ge(h_ready, g)
                sp.dma_start(x_rows[:], tiled(io["x"])[:, both, :]).then_inc(x_in, 16)
                if g == 0:
                    sp.dma_start(gamma[:], io["l0_gamma"].partition_broadcast(P)).then_inc(bias_in, 16)
                    sp.dma_start(beta[:], io["l0_beta"].partition_broadcast(P)).then_inc(bias_in, 16)
                    sp.dma_start(bq[:], io["l1_bq"]).then_inc(bias_in, 16)
                    sp.dma_start(bk[:], io["l1_bk"]).then_inc(bias_in, 16)
                    sp.dma_start(bv[:], io["l1_bv"].partition_broadcast(P)).then_inc(bias_in, 16)
                    for t, name in ((wq, "l1_wq"), (wk, "l1_wk"), (wv, "l1_wv")):
                        sp.dma_start(t[:], io[name].rearrange("(k p) n -> p k n", p=P)).then_inc(w_in, 16)
            sp.wait_ge(x1_ready, G)
            sp.dma_start(tiled(x1_dram)[:, (G - 1) * T:, :], x_rows[:]).then_inc(x1_out, 16)
            sp.wait_ge(x1_out, 16 * G)

        @block.gpsimd
        def _(pool):
            pool.sem_clear(used_sems)

        @block.vector
        def _(dve):
            chain = Chain(dve, chain_s)
            turn = 0

            def values(g):
                for t in range(T):
                    i = g * T + t
                    dve.wait_ge(v_filled, i + 1)
                    nc.vector.tensor_tensor(V[:, i, :], psV[i % 2][:, :], bv[:, :], ALU.add).then_inc(v_emptied, 1)

            for g in range(G):
                dve.wait_ge(y_in, 16 * (g + 1))
                layer_norm_batch(nc, chain, rows, rows, stats, mv, rstd, sqrt_asked, sqrt_done, turn, relu=False)
                turn += 1
                if g == 0:
                    dve.wait_ge(bias_in, 80)
                chain.last_of([nc.vector.tensor_tensor(rows[:, t, :], rows[:, t, :], gamma[:], ALU.mult) for t in range(T)])
                chain.last_of([nc.vector.tensor_tensor(rows[:, t, :], rows[:, t, :], beta[:], ALU.add) for t in range(T)])
                dve.wait_ge(x_in, 16 * (g + 1))
                nc.vector.tensor_tensor(x_rows[:], x_rows[:], rows[:], ALU.add).then_inc(x1_ready, 1)
                dve.wait_ge(x1_ready, g + 1)
                dve.sem_inc(y_free, 1)
                if g >= 2:
                    dve.wait_ge(t_filled, (g - 1) * KT)
                layer_norm_batch(nc, chain, x_rows, h[:, g % 2, :, :], stats, mv, rstd, sqrt_asked, sqrt_done, turn, relu=True)
                turn += 1
                dve.sem_inc(h_ready, 1)
                if g:
                    values(g - 1)
            values(G - 1)

        @block.scalar
        def _(act):
            n = 0

            def move(g):
                nonlocal n
                for k in range(KT):
                    act.wait_ge(t_filled, g * KT + k + 1)
                    if g and k == 0:
                        act.wait_ge(v_filled, g * T)
                    nc.scalar.copy(HT[:, k, :], psT[k % 2][:, :]).then_inc(t_emptied, 1)
                if g == 0:
                    act.wait_ge(bias_in, 80)
                for dst, bias in ((qT, bq), (kT, bk)):
                    if g + 1 < G and dst is kT:
                        layer_norm_sqrt(nc, act, rstd, sqrt_asked, sqrt_done, 2 * g + 2)
                    for m in range(KT):
                        act.wait_ge(m_filled, n + 1)
                        nc.scalar.activation(dst[:, m, g * 512:(g + 1) * 512], psM[n % 4][:, :], ACT.Identity,
                                             bias=bias[:, m:m + 1]).then_inc(m_emptied, 1)
                        n += 1
                if g + 1 < G:
                    layer_norm_sqrt(nc, act, rstd, sqrt_asked, sqrt_done, 2 * g + 3)

            layer_norm_sqrt(nc, act, rstd, sqrt_asked, sqrt_done, 0)
            layer_norm_sqrt(nc, act, rstd, sqrt_asked, sqrt_done, 1)
            for g in range(G):
                move(g)

        @block.tensor
        def _(pe):
            n = 0

            def bank():
                if n >= 4:
                    pe.wait_ge(m_emptied, n - 3)
                return psM[n % 4]

            for g in range(G):
                pe.wait_ge(h_ready, g + 1)
                for k in range(KT):
                    if g * KT + k >= 2:
                        pe.wait_ge(t_emptied, g * KT + k - 1)
                    for t in range(T):
                        tr = nc.tensor.transpose(psT[k % 2][:, t * P:(t + 1) * P], h[:, g % 2, t, k * P:(k + 1) * P], ident[:])
                    tr.then_inc(t_filled, 1)
                pe.wait_ge(t_emptied, (g + 1) * KT)
                if g == 0:
                    pe.wait_ge(w_in, 48)
                    pe.wait_ge(bias_in, 80)
                for weight in (wq, wk):
                    for m in range(KT):
                        ps = bank()
                        for k in range(KT):
                            mm = nc.tensor.matmul(ps[:, :], weight[:, k, m * P:(m + 1) * P], HT[:, k, :], start=(k == 0), stop=(k == KT - 1))
                        mm.then_inc(m_filled, 1)
                        n += 1
                for t in range(T):
                    i = g * T + t
                    if i >= 2:
                        pe.wait_ge(v_emptied, i - 1)
                    for k in range(KT):
                        mm = nc.tensor.matmul(psV[i % 2][:, :], HT[:, k, t * P:(t + 1) * P], wv[:, k, :], start=(k == 0), stop=(k == KT - 1))
                    mm.then_inc(v_filled, 1)


def attention_phase(nc, io, qT, kT, V, edge, ident, x1_dram, x2_dram, l2_dram, tiled):
    N, D = io["x"].shape
    NT, KT, T = N // P, D // P, 4
    CH = N // 512
    scale = 1.0 / math.sqrt(D)
    with ExitStack() as scope:
        sb = lambda n, s, d=F32: scope.enter_context(nc.sbuf_tensor("t_" + n, s, d))
        sem = lambda n: scope.enter_context(nc.semaphore("t_" + n))
        adj_rows, score, void = sb("adj_rows", [P, 2, N]), sb("score", [P, 2, N]), sb("void", [P, N])
        adj_T = sb("adj_T", [P, NT, P])
        PT = sb("PT", [P, 4, 512])
        x_rows, h = sb("x_rows", [P, T, D]), sb("h", [P, T, D])
        o_row = sb("o_row", [P, 2, D])
        stats, mv, rstd = sb("stats", [P, T, 6]), sb("mv", [P, T, 2]), sb("rstd", [P, 3, T])
        row_max, neg_max, total, inv_total = (sb(n, [P, NT]) for n in ("row_max", "neg_max", "total", "inv_total"))
        psL = scope.enter_context(nc.psum_tensor("t_psL", [P, N], F32))
        psT = [scope.enter_context(nc.psum_tensor(f"t_psT{b}", [P, 512], F32)) for b in range(2)]
        psO = scope.enter_context(nc.psum_tensor("t_psO", [P, 512], F32))
        adj_in, x1_in, x2_out = [sem(f"adj_in{b}") for b in range(2)], sem("x1_in"), sem("x2_out")
        scores_done, scaled, max_done, exp_done, inv_done = (sem(n) for n in ("scores_done", "scaled", "max_done", "exp_done", "inv_done"))
        t_filled, t_emptied, pt_used, o_emptied, x2_ready, h_ready = (sem(n) for n in ("t_filled", "t_emptied", "pt_used", "o_emptied", "x2_ready", "h_ready"))
        sqrt_asked, sqrt_done, chain_s = sem("sqrt_asked"), sem("sqrt_done"), sem("chain")
        adj_T_in, edge_done = sem("adj_T_in"), sem("edge_done")
        block = scope.enter_context(nc.Block())

        @block.sync
        def _(sp):
            def store(g):
                sp.wait_ge(h_ready, g + 1)
                sp.dma_start(tiled(x2_dram)[:, g * T:(g + 1) * T, :], x_rows[:]).then_inc(x2_out, 16)
                sp.dma_start(tiled(l2_dram)[:, g * T:(g + 1) * T, :], h[:]).then_inc(x2_out, 16)

            for i in range(NT):
                if i >= 2:
                    sp.wait_ge(scaled, i - 1)
                sp.dma_start(adj_rows[:, i % 2, :], io["adj"][i * P:(i + 1) * P, :]).then_inc(adj_in[i % 2], 16)
                if i:
                    sp.wait_ge(edge_done, i)
                sp.dma_start(adj_T[:], io["adj_t"][:, :, i, :].rearrange("n p c -> p n c")).then_inc(adj_T_in, 16)
                if i % T == 2:
                    g = i // T
                    if g:
                        store(g - 1)
                        sp.wait_ge(x2_out, 32 * g)
                    sp.dma_start(x_rows[:], tiled(x1_dram)[:, g * T:(g + 1) * T, :]).then_inc(x1_in, 16)
            store(NT // T - 1)
            sp.wait_ge(x2_out, 32 * NT // T)

        @block.vector
        def _(dve):
            chain = Chain(dve, chain_s)
            for i in range(NT + 1):
                if i < NT:
                    s_i = score[:, i % 2, :]
                    dve.wait_ge(scores_done, i + 1)
                    dve.wait_ge(adj_in[i % 2], 16 * (i // 2 + 1))
                    if i >= 2:
                        dve.wait_ge(t_filled, (i - 1) * CH)
                    nc.vector.scalar_tensor_tensor(out=s_i, in0=psL[:, :], scalar=scale, in1=adj_rows[:, i % 2, :],
                                                   op0=ALU.mult, op1=ALU.mult).then_inc(scaled, 1)
                    dve.wait_ge(scaled, i + 1)
                    chain(nc.vector.tensor_scalar(void[:, :], s_i, 0.0, -10000.0, ALU.is_equal, ALU.mult))
                    chain(nc.vector.tensor_tensor_reduce(out=s_i, in0=s_i, in1=void[:, :], scale=1.0, scalar=-3.0e38,
                                                         op0=ALU.add, op1=ALU.max, accum_out=row_max[:, i:i + 1]))
                    nc.vector.tensor_scalar(neg_max[:, i:i + 1], row_max[:, i:i + 1], -1.0, None, ALU.mult).then_inc(max_done, 1)
                if i:
                    j = i - 1
                    dve.wait_ge(adj_T_in, 16 * i)
                    nc.vector.tensor_scalar(edge[:, j, :], adj_T[:].rearrange("p n c -> p (n c)"), 0.0, None,
                                            ALU.is_gt).then_inc(edge_done, 1)
                    dve.wait_ge(exp_done, j + 1)
                    nc.vector.reciprocal(inv_total[:, j:j + 1], total[:, j:j + 1]).then_inc(inv_done, 1)
                if i >= 2 or i == NT:
                    for j in ([i - 2] if i < NT else [i - 2, i - 1]):
                        g, t = j // T, j % T
                        if t == 0:
                            dve.wait_ge(x1_in, 16 * (g + 1))
                        dve.wait_ge(o_emptied, j + 1)
                        nc.vector.tensor_tensor(x_rows[:, t, :], x_rows[:, t, :], o_row[:, j % 2, :], ALU.add).then_inc(x2_ready, 1)
                        if t == T - 1:
                            dve.wait_ge(x2_ready, j + 1)
                            if g:
                                dve.wait_ge(x2_out, 32 * g)
                            layer_norm_batch(nc, chain, x_rows, h, stats, mv, rstd, sqrt_asked, sqrt_done, g, relu=True)
                            dve.sem_inc(h_ready, 1)

        @block.scalar
        def _(act):
            nT = 0
            for i in range(NT + 1):
                if i:
                    j = i - 1
                    for c in range(CH):
                        if nT >= 4:
                            act.wait_ge(pt_used, nT - 3)
                        act.wait_ge(t_filled, nT + 1)
                        nc.scalar.copy(PT[:, nT % 4, :], psT[nT % 2][:, :]).then_inc(t_emptied, 1)
                        nT += 1
                if i < NT:
                    act.wait_ge(max_done, i + 1)
                    s_i = score[:, i % 2, :]
                    nc.scalar.activation(s_i, s_i, ACT.Exp, bias=neg_max[:, i:i + 1], accum_out=total[:, i:i + 1]).then_inc(exp_done, 1)
                if i:
                    act.wait_ge(pt_used, nT)
                    act.wait_ge(inv_done, j + 1)
                    if j >= 2:
                        act.wait_ge(x2_ready, j - 1)
                    nc.scalar.activation(o_row[:, j % 2, :], psO[:, :], ACT.Relu, scale=inv_total[:, j:j + 1]).then_inc(o_emptied, 1)
                if i >= 2 and (i - 2) % T == T - 1:
                    layer_norm_sqrt(nc, act, rstd, sqrt_asked, sqrt_done, (i - 2) // T)
            layer_norm_sqrt(nc, act, rstd, sqrt_asked, sqrt_done, NT // T - 1)

        @block.tensor
        def _(pe):
            nT = nPT = 0

            def transpose_part(i, c):
                nonlocal nT
                if nT >= 2:
                    pe.wait_ge(t_emptied, nT - 1)
                for n in range(4):
                    tr = nc.tensor.transpose(psT[nT % 2][:, n * P:(n + 1) * P],
                                             score[:, i % 2, (4 * c + n) * P:(4 * c + n + 1) * P], ident[:])
                tr.then_inc(t_filled, 1)
                nT += 1

            for i in range(NT + 1):
                if i < NT:
                    if i:
                        pe.wait_ge(scaled, i)
                    for c in range(CH):
                        for k in range(KT):
                            mm = nc.tensor.matmul(psL[:, c * 512:(c + 1) * 512], qT[:, k, i * P:(i + 1) * P],
                                                  kT[:, k, c * 512:(c + 1) * 512], start=(k == 0), stop=(k == KT - 1))
                    mm.then_inc(scores_done, 1)
                if i:
                    j = i - 1
                    pe.wait_ge(exp_done, j + 1)
                    transpose_part(j, 0)
                    for c in range(CH):
                        if c + 1 < CH:
                            transpose_part(j, c + 1)
                        pe.wait_ge(t_emptied, nT - (1 if c + 1 < CH else 0))
                        if c == 0 and j:
                            pe.wait_ge(o_emptied, j)
                        for n in range(4):
                            m = 4 * c + n
                            mm = nc.tensor.matmul(psO[:, :], PT[:, nPT % 4, n * P:(n + 1) * P], V[:, m, :],
                                                  start=(m == 0), stop=(m == NT - 1))
                        mm.then_inc(pt_used, 1)
                        nPT += 1


VOID = -1.0e30


def relation_phase(nc, io, ident, l2_dram, tiled):
    N, D = io["x"].shape
    NT, KT, T = N // P, D // P, 4
    G, CH = NT // T, N // 512
    E_ROWS, E_COLS = io["l2_pairs"].shape[0:2]
    HEADS, HID = io["l3_a1"].shape
    with ExitStack() as scope:
        sb = lambda n, s, d=F32: scope.enter_context(nc.sbuf_tensor("r_" + n, s, d))
        sem = lambda n: scope.enter_context(nc.semaphore("r_" + n))
        h_rows = sb("h_rows", [P, NT, D])
        qT, kT = sb("qT", [P, KT, N]), sb("kT", [P, KT, N])
        pairs_in = sb("pairs_in", [E_ROWS, E_COLS, 2], I32)
        pairs = sb("pairs", [E_ROWS, 2, E_COLS])
        tile_ids, row_id = sb("tile_ids", [P, P]), sb("row_id", [P, 1])
        column_id, none = sb("column_id", [P, N]), sb("none", [E_ROWS, 512], BF16)
        q_head = sb("q_head", [P, HEADS, P])
        with ExitStack() as inner:
            sbi = lambda n, s, d=F32: inner.enter_context(nc.sbuf_tensor("r_" + n, s, d))
            wq, wk, bq, bk = sbi("wq", [P, KT, D]), sbi("wk", [P, KT, D]), sbi("bq", [P, KT]), sbi("bk", [P, KT])
            HT = sbi("HT", [P, KT, T * P])
            psT = [inner.enter_context(nc.psum_tensor(f"r_psT{b}", [P, 512], F32)) for b in range(2)]
            psM = [inner.enter_context(nc.psum_tensor(f"r_psM{b}", [P, 512], F32)) for b in range(2)]
            loaded, t_filled, t_emptied = (inner.enter_context(nc.semaphore("r_" + n)) for n in ("loaded", "t_filled", "t_emptied"))
            m_filled, m_emptied = (inner.enter_context(nc.semaphore("r_" + n)) for n in ("m_filled", "m_emptied"))
            block = inner.enter_context(nc.Block())

            @block.sync
            def _(sp):
                sp.dma_start(h_rows[:], tiled(l2_dram)).then_inc(loaded, 16)
                for t, name in ((wq, "l2_wq"), (wk, "l2_wk")):
                    sp.dma_start(t[:], io[name].rearrange("(k p) n -> p k n", p=P)).then_inc(loaded, 16)
                for t, name in ((bq, "l2_bq"), (bk, "l2_bk"), (pairs_in, "l2_pairs")):
                    sp.dma_start(t[:], io[name]).then_inc(loaded, 16)

            @block.gpsimd
            def _(pool):
                for ids, step, rows in ((column_id, [1, N], 0), (tile_ids, [1, P], 0), (row_id, [1, 1], 1)):
                    nc.gpsimd.iota(ids[:], [step], base=0 if ids is column_id else -P, channel_multiplier=rows,
                                   allow_small_or_imprecise_dtypes=True)
                nc.gpsimd.memset(none[:], 0.0)
                nc.gpsimd.memset(q_head[:], 0.0)

            @block.vector
            def _(dve):
                dve.wait_ge(loaded, 96)
                nc.vector.tensor_copy(pairs[:].rearrange("p s e -> p e s"), pairs_in[:])

            @block.tensor
            def _(pe):
                pe.wait_ge(loaded, 96)
                nT = nM = 0
                for g in range(G):
                    if g:
                        pe.wait_ge(t_emptied, nT)
                    for k in range(KT):
                        if nT >= 2:
                            pe.wait_ge(t_emptied, nT - 1)
                        for t in range(T):
                            tr = nc.tensor.transpose(psT[nT % 2][:, t * P:(t + 1) * P], h_rows[:, g * T + t, k * P:(k + 1) * P], ident[:])
                        tr.then_inc(t_filled, 1)
                        nT += 1
                    pe.wait_ge(t_emptied, nT)
                    for weight in (wq, wk):
                        for m in range(KT):
                            if nM >= 2:
                                pe.wait_ge(m_emptied, nM - 1)
                            for k in range(KT):
                                mm = nc.tensor.matmul(psM[nM % 2][:, :], weight[:, k, m * P:(m + 1) * P], HT[:, k, :],
                                                      start=(k == 0), stop=(k == KT - 1))
                            mm.then_inc(m_filled, 1)
                            nM += 1

            @block.scalar
            def _(act):
                nT = nM = 0
                act.wait_ge(loaded, 96)
                for g in range(G):
                    for k in range(KT):
                        act.wait_ge(t_filled, nT + 1)
                        if g and k == 0:
                            act.wait_ge(m_filled, nM)
                        nc.scalar.copy(HT[:, k, :], psT[nT % 2][:, :]).then_inc(t_emptied, 1)
                        nT += 1
                    for dst, bias in ((qT, bq), (kT, bk)):
                        for m in range(KT):
                            act.wait_ge(m_filled, nM + 1)
                            nc.scalar.activation(dst[:, m, g * 512:(g + 1) * 512], psM[nM % 2][:, :], ACT.Identity,
                                                 bias=bias[:, m:m + 1]).then_inc(m_emptied, 1)
                            nM += 1

        adj_row, score = (sb(n, [P, N]) for n in ("adj_row", "score"))
        listed, base = sb("listed", [P, N]), sb("base", [P, N])
        own, agg = score, adj_row
        hot_sub, hot_obj = sb("hot_sub", [E_ROWS, P], BF16), sb("hot_obj", [E_ROWS, N], BF16)
        agg_T, out_row = sb("agg_T", [P, NT, P]), sb("out_row", [P, D])
        neg_max, total, weight = sb("neg_max", [P, 1]), sb("total", [P, 1]), sb("weight", [P, 1])
        psL = scope.enter_context(nc.psum_tensor("r_psL", [P, N], F32))
        psT = [scope.enter_context(nc.psum_tensor(f"r_psA{b}", [P, 512], F32)) for b in range(2)]
        psO = scope.enter_context(nc.psum_tensor("r_psO", [P, 512], F32))
        chain_s = sem("chain")
        turn_open, adj_loaded, stored = sem("turn_open"), sem("adj_loaded"), sem("stored")
        hot_ready, hot_used, counted = sem("hot_ready"), sem("hot_used"), sem("counted")
        q_staged, base_ready, scores_done, max_done, exp_done, head_added = (
            sem(n) for n in ("q_staged", "base_ready", "scores_done", "max_done", "exp_done", "head_added"))
        t_filled, t_emptied, o_filled, o_emptied = (sem(n) for n in ("u_filled", "u_emptied", "o_filled", "o_emptied"))
        block = scope.enter_context(nc.Block())

        @block.sync
        def _(sp):
            sp.sem_inc(turn_open, 1)
            with sp.Fori(0, NT) as i:
                sp.dma_start(adj_row[:], io["adj"][bass.ds(i * P, P), :]).then_inc(adj_loaded, 16)
                sp.wait_ge(o_emptied, i + 1)
                sp.dma_start(l2_dram[bass.ds(i * P, P), :], out_row[:]).then_inc(stored, 16)
                sp.wait_ge(stored, i * 16 + 16)
                sp.sem_inc(turn_open, 1)

        @block.gpsimd
        def _(pool):
            with pool.Fori(0, NT) as i:
                pool.wait_ge(turn_open, i + 1)
                for odd in range(2):
                    rows = slice(odd * HID, (odd + 1) * HID)
                    nc.gpsimd.tensor_copy(q_head[rows, odd::2, :], qT[rows, :, bass.ds(i * P, P)]).then_inc(q_staged, 1)

        @block.vector
        def _(dve):
            steps = 2 + 1 + 7 + 1 + 4 * HEADS
            with dve.Fori(0, NT) as i:
                n = [0]

                def link(ins):
                    n[0] += 1
                    ins.then_inc(chain_s, 1)
                    dve.wait_ge(chain_s, i * steps + n[0])

                dve.wait_ge(turn_open, i + 1)
                link(nc.vector.tensor_scalar(tile_ids[:], tile_ids[:], float(P), None, ALU.add))
                link(nc.vector.tensor_scalar(row_id[:], row_id[:], float(P), None, ALU.add))
                n[0] += 1
                nc.vector.memset(weight[:], 0.0).then_inc(chain_s, 1)
                with dve.Fori(0, E_COLS) as e:
                    dve.wait_ge(hot_used, i * E_COLS + e + 1)
                    nc.vector.tensor_scalar(hot_sub[:], tile_ids[0:E_ROWS, :], pairs[:, 0, bass.ds(e, 1)], None,
                                            ALU.is_equal).then_inc(hot_ready, 1)
                    nc.vector.tensor_scalar(hot_obj[:], column_id[0:E_ROWS, :], pairs[:, 1, bass.ds(e, 1)], None,
                                            ALU.is_equal).then_inc(hot_ready, 1)
                dve.wait_ge(counted, i + 1)
                link(nc.vector.tensor_scalar(own[:], column_id[:], row_id[:], None, ALU.is_equal))
                dve.wait_ge(adj_loaded, i * 16 + 16)
                link(nc.vector.tensor_scalar(adj_row[:], adj_row[:], 1.0, None, ALU.is_equal))
                link(nc.vector.scalar_tensor_tensor(out=listed[:], in0=psL[:], scalar=0.0, in1=adj_row[:],
                                                    op0=ALU.is_gt, op1=ALU.mult))
                link(nc.vector.scalar_tensor_tensor(out=listed[:], in0=own[:], scalar=0.0, in1=listed[:],
                                                    op0=ALU.is_equal, op1=ALU.mult))
                link(nc.vector.tensor_tensor(base[:], adj_row[:], own[:], ALU.max))
                link(nc.vector.tensor_scalar(base[:], base[:], 1.0, -VOID, ALU.subtract, ALU.mult))
                link(nc.vector.scalar_tensor_tensor(out=base[:], in0=own[:], scalar=1e-7, in1=base[:],
                                                    op0=ALU.mult, op1=ALU.add))
                dve.sem_inc(base_ready, 1)
                link(nc.vector.memset(agg[:], 0.0))
                for h in range(HEADS):
                    dve.wait_ge(scores_done, i * HEADS + (h + 1))
                    link(nc.vector.scalar_tensor_tensor(out=score[:], in0=psL[:], scalar=1.0 / math.sqrt(HID), in1=listed[:],
                                                        op0=ALU.mult, op1=ALU.mult))
                    link(nc.vector.tensor_tensor(score[:], score[:], base[:], ALU.add))
                    nc.vector.tensor_reduce(neg_max[:], score[:], AX.X, ALU.max, negate=True).then_inc(max_done, 1)
                    dve.wait_ge(exp_done, i * HEADS + (h + 1))
                    link(nc.vector.tensor_scalar(total[:], total[:], float(HEADS), None, ALU.mult))
                    link(nc.vector.reciprocal(weight[:], total[:]))
                    nc.vector.scalar_tensor_tensor(out=agg[:], in0=score[:], scalar=weight[:], in1=agg[:],
                                                   op0=ALU.mult, op1=ALU.add).then_inc(head_added, 1)
                    dve.wait_ge(head_added, i * HEADS + (h + 1))

        @block.scalar
        def _(act):
            with act.Fori(0, NT) as i:
                for h in range(HEADS):
                    act.wait_ge(max_done, i * HEADS + (h + 1))
                    nc.scalar.activation(score[:], score[:], ACT.Exp, bias=neg_max[:], accum_out=total[:]).then_inc(exp_done, 1)
                for c in range(CH):
                    act.wait_ge(t_filled, i * CH + (c + 1))
                    nc.scalar.copy(agg_T[:, 4 * c:4 * c + 4, :], psT[c % 2][:, :].rearrange("p (n r) -> p n r", n=4)).then_inc(t_emptied, 1)
                act.wait_ge(o_filled, i + 1)
                nc.scalar.copy(out_row[:], psO[:]).then_inc(o_emptied, 1)

        @block.tensor
        def _(pe):
            pe.sem_inc(hot_used, 1)

            def add_nothing(start, stop):
                for c in range(CH):
                    mm = nc.tensor.matmul(psL[:, c * 512:(c + 1) * 512], none[:, 0:P], none[:], start=start, stop=stop)
                return mm

            with pe.Fori(0, NT) as i:
                pe.wait_ge(turn_open, i + 1)
                add_nothing(True, False)
                with pe.Fori(0, E_COLS) as e:
                    pe.wait_ge(hot_ready, i * (2 * E_COLS) + e * 2 + 2)
                    for c in range(CH):
                        mm = nc.tensor.matmul(psL[:, c * 512:(c + 1) * 512], hot_sub[:], hot_obj[:, c * 512:(c + 1) * 512],
                                              start=False, stop=False)
                    mm.then_inc(hot_used, 1)
                add_nothing(False, True).then_inc(counted, 1)
                pe.wait_ge(q_staged, i * 2 + 2)
                pe.wait_ge(base_ready, i + 1)
                for h in range(HEADS):
                    if h:
                        pe.wait_ge(max_done, i * HEADS + h)
                    for c in range(CH):
                        mm = nc.tensor.matmul(psL[:, c * 512:(c + 1) * 512], q_head[:, h, :], kT[:, h * HID // P, c * 512:(c + 1) * 512],
                                              start=True, stop=True)
                    mm.then_inc(scores_done, 1)
                pe.wait_ge(head_added, i * HEADS + HEADS)
                for c in range(CH):
                    if c >= 2:
                        pe.wait_ge(t_emptied, i * CH + (c - 1))
                    for n in range(4):
                        tr = nc.tensor.transpose(psT[c % 2][:, n * P:(n + 1) * P], agg[:, (4 * c + n) * P:(4 * c + n + 1) * P], ident[:])
                    tr.then_inc(t_filled, 1)
                pe.wait_ge(t_emptied, i * CH + CH)
                for j in range(NT):
                    mm = nc.tensor.matmul(psO[:], agg_T[:, j, :], h_rows[:, j, :], start=(j == 0), stop=(j == NT - 1))
                mm.then_inc(o_filled, 1)


def heads_phase(nc, io, Wh, dst, dst_low, dst_neg, src_bias, ident, x2_dram, l2_dram, x3_dram, src_dram, tiled):
    N, D = io["x"].shape
    NT, KT, T = N // P, D // P, 4
    G = NT // T
    HEADS, HID = io["l3_a1"].shape
    with ExitStack() as scope:
        sb = lambda n, s, d=F32: scope.enter_context(nc.sbuf_tensor("h_" + n, s, d))
        sem = lambda n: scope.enter_context(nc.semaphore("h_" + n))
        w = sb("w", [P, KT, D])
        a1, a2 = sb("a1", [P, D]), sb("a2", [P, D])
        x_rows, l_rows = sb("x_rows", [P, G, T, D]), sb("l_rows", [P, G, T, D])
        HT = sb("HT", [P, KT, T * P])
        prod = sb("prod", [P, HEADS, HID])
        src, src_T = sb("src", [P, NT, HEADS]), sb("src_T", [HEADS, N])
        top, top_all = sb("top", [P, HEADS]), sb("top_all", [P, HEADS])
        stats, mv, rstd = sb("stats", [P, T, 6]), sb("mv", [P, T, 2]), sb("rstd", [P, 3, T])
        psT = [scope.enter_context(nc.psum_tensor(f"h_psT{b}", [P, 512], F32)) for b in range(2)]
        psM = [scope.enter_context(nc.psum_tensor(f"h_psM{b}", [P, 512], F32)) for b in range(2)]
        psS = [scope.enter_context(nc.psum_tensor(f"h_psS{b}", [HEADS, 512], F32)) for b in range(2)]
        w_in, x_in, x3_out = sem("w_in"), [sem(f"x_in{g}") for g in range(G)], sem("x3_out")
        x3_ready, h_ready, src_out = sem("x3_ready"), sem("h_ready"), sem("src_out")
        sqrt_asked, sqrt_done, chain_s = sem("sqrt_asked"), sem("sqrt_done"), sem("chain")
        t_filled, t_emptied, m_filled, m_emptied = (sem(n) for n in ("t_filled", "t_emptied", "m_filled", "m_emptied"))
        one_set, src_done, s_filled, s_emptied = sem("one_set"), sem("src_done"), sem("s_filled"), sem("s_emptied")
        top_done, top_spread, bias_done = sem("top_done"), sem("top_spread"), sem("bias_done")
        block = scope.enter_context(nc.Block())

        @block.sync
        def _(sp):
            for g in range(G):
                both = slice(g * T, (g + 1) * T)
                sp.dma_start(x_rows[:, g], tiled(x2_dram)[:, both, :]).then_inc(x_in[g], 16)
                sp.dma_start(l_rows[:, g], tiled(l2_dram)[:, both, :]).then_inc(x_in[g], 16)
                if g == 0:
                    sp.dma_start(w[:], io["l3_w"].rearrange("(k p) n -> p k n", p=P)).then_inc(w_in, 16)
                    sp.dma_start(a1[:], io["l3_a1"].rearrange("h d -> (h d)").partition_broadcast(P)).then_inc(w_in, 16)
                    sp.dma_start(a2[:], io["l3_a2"].rearrange("h d -> (h d)").partition_broadcast(P)).then_inc(w_in, 16)
            for g in range(G):
                sp.wait_ge(x3_ready, g + 1)
                sp.dma_start(tiled(x3_dram)[:, g * T:(g + 1) * T, :], x_rows[:, g]).then_inc(x3_out, 16)
            sp.wait_ge(s_emptied, N // 512)
            sp.dma_start(src_dram, src_T[:]).then_inc(src_out, 16)
            sp.wait_ge(src_out, 16)
            sp.wait_ge(x3_out, 16 * G)

        @block.gpsimd
        def _(pool):
            nc.gpsimd.memset(Wh[:, :, :, HID:HID + 1], 1.0).then_inc(one_set, 1)
            pool.wait_ge(top_done, 1)
            nc.gpsimd.partition_all_reduce(top_all[:], top[:], P, bass.bass_isa.ReduceOp.max).then_inc(top_spread, 1)

        @block.vector
        def _(dve):
            chain = Chain(dve, chain_s)

            def parts(i):
                dve.wait_ge(m_emptied, i + 1)
                for a, dest in ((a1, src), (a2, dst)):
                    chain(nc.vector.tensor_tensor(prod[:], Wh[:, i, :, 0:HID], a[:].rearrange("p (h d) -> p h d", h=HEADS), ALU.mult))
                    chain(nc.vector.tensor_reduce(dest[:, i, :], prod[:], AX.X, ALU.add))

            for g in range(G):
                dve.wait_ge(x_in[g], 32)
                nc.vector.tensor_tensor(x_rows[:, g], x_rows[:, g], l_rows[:, g], ALU.add).then_inc(x3_ready, 1)
                dve.wait_ge(x3_ready, g + 1)
                layer_norm_batch(nc, chain, x_rows[:, g], l_rows[:, g], stats, mv, rstd, sqrt_asked, sqrt_done, g, relu=True)
                dve.sem_inc(h_ready, 1)
                if g == 0:
                    continue
                if g == 1:
                    dve.wait_ge(w_in, 48)
                for i in range((g - 1) * T, g * T):
                    parts(i)
            for i in range((G - 1) * T, NT):
                parts(i)
            dve.sem_inc(src_done, 1)
            nc.vector.tensor_reduce(top[:], dst[:].rearrange("p n h -> p h n"), AX.X, ALU.max).then_inc(top_done, 1)
            dve.wait_ge(top_spread, 1)
            chain.last_of([nc.vector.tensor_tensor(dst[:, i, :], dst[:, i, :], top_all[:], ALU.subtract) for i in range(NT)])
            chain(nc.vector.tensor_scalar(dst_low[:], dst[:], SLOPE, -SHIFT, ALU.mult, ALU.add))
            chain(nc.vector.tensor_scalar(dst[:], dst[:], SHIFT, None, ALU.add))
            chain(nc.vector.tensor_scalar(src_bias[:], top_all[:], 1 - SLOPE, -2 * SHIFT, ALU.mult, ALU.add))
            dve.sem_inc(bias_done, 1)
            dve.wait_ge(s_emptied, N // 512 + 2)
            chain(nc.vector.tensor_scalar(dst_neg[:], dst_low[:], -1.0, None, ALU.mult))

        @block.scalar
        def _(act):
            act.wait_ge(one_set, 1)
            layer_norm_sqrt(nc, act, rstd, sqrt_asked, sqrt_done, 0)
            for g in range(G):
                for k in range(KT):
                    act.wait_ge(t_filled, g * KT + k + 1)
                    if g and k == 0:
                        act.wait_ge(m_filled, g * T)
                    nc.scalar.copy(HT[:, k, :], psT[k % 2][:, :]).then_inc(t_emptied, 1)
                if g + 1 < G:
                    layer_norm_sqrt(nc, act, rstd, sqrt_asked, sqrt_done, g + 1)
                for i in range(g * T, (g + 1) * T):
                    act.wait_ge(m_filled, i + 1)
                    nc.scalar.copy(Wh[:, i, :, 0:HID], psM[i % 2][:, :].rearrange("p (h d) -> p h d", h=HEADS)).then_inc(m_emptied, 1)
            for c in range(N // 512):
                act.wait_ge(s_filled, c + 1)
                nc.scalar.copy(src_T[:, c * 512:(c + 1) * 512], psS[c % 2][:, :]).then_inc(s_emptied, 1)
            act.wait_ge(bias_done, 1)
            for t in (dst, dst_low):
                nc.scalar.activation(t[:], t[:], ACT.Exp).then_inc(s_emptied, 1)

        @block.tensor
        def _(pe):
            for g in range(G):
                pe.wait_ge(h_ready, g + 1)
                for k in range(KT):
                    if g * KT + k >= 2:
                        pe.wait_ge(t_emptied, g * KT + k - 1)
                    for t in range(T):
                        tr = nc.tensor.transpose(psT[k % 2][:, t * P:(t + 1) * P], l_rows[:, g, t, k * P:(k + 1) * P], ident[:])
                    tr.then_inc(t_filled, 1)
                pe.wait_ge(t_emptied, (g + 1) * KT)
                if g == 0:
                    pe.wait_ge(w_in, 48)
                for t in range(T):
                    i = g * T + t
                    if i >= 2:
                        pe.wait_ge(m_emptied, i - 1)
                    for k in range(KT):
                        mm = nc.tensor.matmul(psM[i % 2][:, :], HT[:, k, t * P:(t + 1) * P], w[:, k, :], start=(k == 0), stop=(k == KT - 1))
                    mm.then_inc(m_filled, 1)
            pe.wait_ge(src_done, 1)
            for c in range(N // 512):
                if c >= 2:
                    pe.wait_ge(s_emptied, c - 1)
                for n in range(4):
                    tr = nc.tensor.transpose(psS[c % 2][:, n * P:(n + 1) * P], src[:, 4 * c + n, :], ident[:])
                tr.then_inc(s_filled, 1)


SLOPE = 0.2
SHIFT = 40.0


def gat_phase(nc, ident, Wh, edge, dst, dst_low, dst_neg, src_bias, enc, src_dram):
    _, NT, HEADS, W1 = Wh.shape
    HID, N = W1 - 1, edge.shape[2]
    CH = N // 512
    PER = 512 // W1
    BANKS = -(-NT // PER)
    with ExitStack() as scope:
        sb = lambda n, s, d=F32: scope.enter_context(nc.sbuf_tensor("e_" + n, s, d))
        sem = lambda n: scope.enter_context(nc.semaphore("e_" + n))
        source = sb("source", [P, 2, N])
        above, prob = sb("above", [P, 2, N]), sb("prob", [P, 2, N])
        inv = sb("inv", [P, NT])
        sums_T = sb("sums_T", [W1, N])
        acc = scope.enter_context(nc.psum_tensor("e_acc", [W1, N], F32))
        turned = [scope.enter_context(nc.psum_tensor(f"e_turned{k}", [P, 512], F32)) for k in range(BANKS)]
        src_in, src_ready = [sem(f"src_in{b}") for b in range(2)], sem("src_ready")
        above_done, prob_done, prob_used, inv_done = (sem(n) for n in ("above_done", "prob_done", "prob_used", "inv_done"))
        acc_copied, sums_turned, head_taken = sem("acc_copied"), sem("sums_turned"), sem("head_taken")
        block = scope.enter_context(nc.Block())

        def sums(k):
            n = min(PER, NT - k * PER)
            return turned[k][:, 0:n * W1].rearrange("p (n w) -> p n w", w=W1), slice(k * PER, k * PER + n)

        @block.sync
        def _(sp):
            for h in range(HEADS):
                if h >= 2:
                    sp.wait_ge(above_done, (h - 1) * NT)
                sp.dma_start(source[:, h % 2, :], src_dram[h].partition_broadcast(P)).then_inc(src_in[h % 2], 16)

        @block.scalar
        def _(act):
            def copy_sums(h):
                act.wait_ge(prob_used, (h + 1) * NT)
                if h:
                    act.wait_ge(sums_turned, h)
                for c in range(CH):
                    nc.scalar.copy(sums_T[:, c * 512:(c + 1) * 512], acc[:, c * 512:(c + 1) * 512]).then_inc(acc_copied, 1)

            for h in range(HEADS):
                act.wait_ge(src_in[h % 2], 16 * (h // 2 + 1))
                row = source[:, h % 2, :]
                nc.scalar.activation(row, row, ACT.Exp, scale=1 - SLOPE, bias=src_bias[:, h:h + 1]).then_inc(src_ready, 1)
                act.wait_ge(src_ready, h + 1)
                for j in range(NT):
                    n = h * NT + j
                    if n >= 2:
                        act.wait_ge(prob_done, n - 1)
                    nc.scalar.activation(above[:, n % 2, :], row, ACT.Relu, scale=dst[:, j, h:h + 1],
                                         bias=dst_neg[:, j, h:h + 1]).then_inc(above_done, 1)
                    if h and j == 1:
                        copy_sums(h - 1)
            copy_sums(HEADS - 1)

        @block.vector
        def _(dve):
            def take(h):
                dve.wait_ge(sums_turned, h + 1)
                for k in range(BANKS):
                    part, tiles = sums(k)
                    nc.vector.reciprocal(inv[:, tiles], part[:, :, HID]).then_inc(inv_done, 1)
                dve.wait_ge(inv_done, (h + 1) * BANKS)
                for k in range(BANKS):
                    part, tiles = sums(k)
                    n = part.shape[1]
                    nc.vector.tensor_tensor(enc[:, tiles, h * HID:(h + 1) * HID], part[:, :, 0:HID],
                                            inv[:, tiles].unsqueeze(2).broadcast_to([P, n, HID]), ALU.mult).then_inc(head_taken, 1)

            for h in range(HEADS):
                for j in range(NT):
                    n = h * NT + j
                    dve.wait_ge(above_done, n + 1)
                    if n >= 2:
                        dve.wait_ge(prob_used, n - 1)
                    nc.vector.scalar_tensor_tensor(out=prob[:, n % 2, :], in0=above[:, n % 2, :], scalar=dst_low[:, j, h:h + 1],
                                                   in1=edge[:, j, :], op0=ALU.add, op1=ALU.mult).then_inc(prob_done, 1)
                    if h and j == 4:
                        take(h - 1)
            take(HEADS - 1)

        @block.tensor
        def _(pe):
            def turn_sums(h):
                pe.wait_ge(acc_copied, (h + 1) * CH)
                if h:
                    pe.wait_ge(head_taken, h * BANKS)
                for i in range(NT):
                    k, m = i // PER, i % PER
                    tr = nc.tensor.transpose(turned[k][:, m * W1:(m + 1) * W1], sums_T[:, i * P:(i + 1) * P], ident[0:W1, 0:W1])
                tr.then_inc(sums_turned, 1)

            for h in range(HEADS):
                for j in range(NT):
                    n = h * NT + j
                    pe.wait_ge(prob_done, n + 1)
                    for c in range(CH):
                        if h and j == 0:
                            pe.wait_ge(acc_copied, (h - 1) * CH + c + 1)
                        mm = nc.tensor.matmul(acc[:, c * 512:(c + 1) * 512], Wh[:, j, h, :], prob[:, n % 2, c * 512:(c + 1) * 512],
                                              start=(j == 0), stop=(j == NT - 1))
                    mm.then_inc(prob_used, 1)
                    if h and j == 1:
                        turn_sums(h - 1)
            turn_sums(HEADS - 1)


def mlp_phase(nc, io, enc, ident, x3_dram, out, tiled):
    _, NT, D = enc.shape
    KT, T = D // P, 4
    G = NT // T
    widths = [io[f"l3_w{n}"].shape[1] for n in range(1, 5)]
    with ExitStack() as scope:
        sb = lambda n, s, d=F32: scope.enter_context(nc.sbuf_tensor("f_" + n, s, d))
        sem = lambda n: scope.enter_context(nc.semaphore("f_" + n))
        w, b = [], []
        for n in range(1, 5):
            rows, cols = io[f"l3_w{n}"].shape
            w.append(sb(f"w{n}", [P, rows // P, cols]))
            b.append(sb(f"b{n}", [P, cols // P] if n < 4 else [P, cols]))
        low, lifted, act_in = sb("low", [P, T, D]), sb("lifted", [P, T, D]), sb("act_in", [P, 2, T, D])
        x_rows = sb("x_rows", [P, 2, T, D])
        o_rows = sb("o_rows", [P, 2, D])
        layers = [sb("layer0", [P, KT, 512])] + [sb(f"layer{n}", [P, widths[n - 1] // P, 512]) for n in range(1, 4)]
        psT = [scope.enter_context(nc.psum_tensor(f"f_psT{k}", [P, 512], F32)) for k in range(2)]
        psO = [scope.enter_context(nc.psum_tensor(f"f_psO{k}", [P, 512], F32)) for k in range(2)]
        o_filled, o_emptied, x_lifted = sem("o_filled"), sem("o_emptied"), sem("x_lifted")
        psM = [scope.enter_context(nc.psum_tensor(f"f_psM{k}", [P, 512], F32)) for k in range(4)]
        w_in, x_in, o_out = sem("w_in"), [sem(f"x_in{k}") for k in range(2)], [sem(f"o_out{k}") for k in range(2)]
        low_done, exp_done, elu_done, chain_s = sem("low_done"), sem("exp_done"), sem("elu_done"), sem("chain")
        t_filled, t_emptied, m_filled, m_emptied = (sem(n) for n in ("t_filled", "t_emptied", "m_filled", "m_emptied"))
        sizes = [widths[n] // P for n in range(3)]
        block = scope.enter_context(nc.Block())

        def store(sp, g):
            for t in range(T):
                i = g * T + t
                sp.wait_ge(o_emptied, i + 1)
                sp.dma_start(tiled(out)[:, i, :], o_rows[:, i % 2, :]).then_inc(o_out[i % 2], 16)

        @block.sync
        def _(sp):
            for n in range(4):
                sp.dma_start(w[n][:], io[f"l3_w{n + 1}"].rearrange("(k p) n -> p k n", p=P)).then_inc(w_in, 16)
                bias = io[f"l3_b{n + 1}"]
                sp.dma_start(b[n][:], bias if n < 3 else bias.partition_broadcast(P)).then_inc(w_in, 16)
            for g in range(G):
                if g >= 2:
                    sp.wait_ge(o_emptied, (g - 1) * T)
                sp.dma_start(x_rows[:, g % 2, :, :], tiled(x3_dram)[:, g * T:(g + 1) * T, :]).then_inc(x_in[g % 2], 16)
                if g:
                    store(sp, g - 1)
            store(sp, G - 1)
            for k in range(2):
                sp.wait_ge(o_out[k], 16 * NT // 2)

        @block.vector
        def _(dve):
            chain = Chain(dve, chain_s)

            def finish(g):
                dve.wait_ge(x_in[g % 2], 16 * (g // 2 + 1))
                for t in range(T):
                    nc.vector.tensor_tensor(x_rows[:, g % 2, t, :], x_rows[:, g % 2, t, :], b[3][:, :], ALU.add).then_inc(x_lifted, 1)
                dve.wait_ge(x_lifted, (g + 1) * T)
                for t in range(T):
                    i = g * T + t
                    dve.wait_ge(o_filled, i + 1)
                    if i >= 2:
                        dve.wait_ge(o_out[i % 2], 16 * (i // 2))
                    nc.vector.tensor_tensor(o_rows[:, i % 2, :], psO[i % 2][:, :], x_rows[:, g % 2, t, :], ALU.add).then_inc(o_emptied, 1)

            for g in range(G):
                part = enc[:, g * T:(g + 1) * T, :]
                if g:
                    dve.wait_ge(elu_done, g)
                nc.vector.tensor_scalar(low[:], part, 0.0, None, ALU.min).then_inc(low_done, 1)
                chain(nc.vector.tensor_scalar(lifted[:], part, 0.0, -1.0, ALU.max, ALU.add))
                dve.wait_ge(exp_done, g + 1)
                if g >= 2:
                    dve.wait_ge(t_filled, (g - 1) * KT)
                nc.vector.tensor_tensor(act_in[:, g % 2, :, :], low[:], lifted[:], ALU.add).then_inc(elu_done, 1)
                if g == 0:
                    dve.wait_ge(w_in, 128)
                else:
                    finish(g - 1)
            finish(G - 1)

        @block.scalar
        def _(act):
            n = 0
            act.wait_ge(w_in, 128)

            def elu_exp(g):
                act.wait_ge(low_done, g + 1)
                nc.scalar.activation(low[:], low[:], ACT.Exp).then_inc(exp_done, 1)

            elu_exp(0)
            for g in range(G):
                if g + 1 < G:
                    elu_exp(g + 1)
                for k in range(KT):
                    act.wait_ge(t_filled, g * KT + k + 1)
                    nc.scalar.copy(layers[0][:, k, :], psT[k % 2][:, :]).then_inc(t_emptied, 1)
                for layer in range(3):
                    for m in range(sizes[layer]):
                        act.wait_ge(m_filled, n + 1)
                        nc.scalar.activation(layers[layer + 1][:, m, :], psM[n % 4][:, :], ACT.Relu,
                                             bias=b[layer][:, m:m + 1]).then_inc(m_emptied, 1)
                        n += 1

        @block.tensor
        def _(pe):
            n = 0

            def bank():
                if n >= 4:
                    pe.wait_ge(m_emptied, n - 3)
                return psM[n % 4]

            pe.wait_ge(w_in, 128)
            for g in range(G):
                pe.wait_ge(elu_done, g + 1)
                for k in range(KT):
                    if g * KT + k >= 2:
                        pe.wait_ge(t_emptied, g * KT + k - 1)
                    for t in range(T):
                        tr = nc.tensor.transpose(psT[k % 2][:, t * P:(t + 1) * P], act_in[:, g % 2, t, k * P:(k + 1) * P], ident[:])
                    tr.then_inc(t_filled, 1)
                pe.wait_ge(t_emptied, (g + 1) * KT)
                for layer in range(3):
                    for m in range(sizes[layer]):
                        ps = bank()
                        K = layers[layer].shape[1]
                        for k in range(K):
                            mm = nc.tensor.matmul(ps[:, :], w[layer][:, k, m * P:(m + 1) * P], layers[layer][:, k, :],
                                                  start=(k == 0), stop=(k == K - 1))
                        mm.then_inc(m_filled, 1)
                        n += 1
                    pe.wait_ge(m_emptied, n)
                for t in range(T):
                    i = g * T + t
                    if i >= 2:
                        pe.wait_ge(o_emptied, i - 1)
                    for k in range(2):
                        mm = nc.tensor.matmul(psO[i % 2][:, :], layers[3][:, k, t * P:(t + 1) * P], w[3][:, k, :],
                                              start=(k == 0), stop=(k == 1))
                    mm.then_inc(o_filled, 1)


def laid_out(np, v):
    adj = v["adj"]
    n = adj.shape[0] // P
    heads, d, hid = v["L3_gnn_W"].shape
    columns = lambda b: b.reshape(-1, P).T
    out = {
        "x": v["x"], "adj": adj, "adj_t": adj.reshape(n, P, n, P).transpose(0, 3, 2, 1),
        "l0_w1": v["L0_gnn_W1"], "l0_w2": v["L0_gnn_W2"], "l0_w3": v["L0_gnn_W3"],
        "l0_u1_0": v["L0_gnn_U1_0"], "l0_u1_1": v["L0_gnn_U1_1"], "l0_u2_0": v["L0_gnn_U2_0"], "l0_u2_1": v["L0_gnn_U2_1"],
        "l0_gamma": v["L0_gnn_gamma"], "l0_beta": v["L0_gnn_beta"],
        "l1_wq": v["L1_gnn_W_q"].T, "l1_wk": v["L1_gnn_W_k"].T, "l1_wv": v["L1_gnn_W_v"].T,
        "l1_bq": columns(v["L1_gnn_b_q"]), "l1_bk": columns(v["L1_gnn_b_k"]), "l1_bv": v["L1_gnn_b_v"],
        "l2_wq": v["L2_gnn_Wq"].T, "l2_wk": v["L2_gnn_Wk"].T, "l2_bq": columns(v["L2_gnn_bq"]), "l2_bk": columns(v["L2_gnn_bk"]),
        "l2_pairs": v["L2_gnn_rel_pair_index"].reshape(125, -1, 2),
        "l3_w": v["L3_gnn_W"].transpose(1, 0, 2).reshape(d, heads * hid), "l3_a1": v["L3_gnn_a1"], "l3_a2": v["L3_gnn_a2"],
    }
    for k in range(1, 5):
        out[f"l3_w{k}"] = v[f"L3_gnn_W{k}"].T
        out[f"l3_b{k}"] = columns(v[f"L3_gnn_b{k}"]) if k < 4 else v["L3_gnn_b4"]
    return {name: np.ascontiguousarray(a) for name, a in out.items()}


def kernel(**inputs):
    import numpy as _np
    import concourse.bacc as _bacc
    from concourse import mybir as _mybir
    from concourse.bass_utils import run_bass_kernel_spmd as _run

    nc = _bacc.Bacc("TRN2", target_bir_lowering=False, num_devices=1)
    arrays = laid_out(_np, {k: _np.asarray(v) for k, v in inputs.items()})
    io = {k: nc.dram_tensor(f"in_{k}_dram", a.shape, _mybir.dt.from_np(a.dtype), kind="ExternalInput").ap()
          for k, a in arrays.items()}
    out = nc.dram_tensor("out_dram", inputs["x"].shape, F32, kind="ExternalOutput").ap()
    build(nc, io, out)
    r = _run(nc, [{f"in_{k}_dram": a for k, a in arrays.items()}], core_ids=[0])
    return r.results[0]["out_dram"]
```
